# Optimizing a Trainium2 kernel written in Bass

```python
import numpy as np
import jax
import jax.numpy as jnp

def _softmax(x, axis=-1):
    return jax.nn.softmax(x, axis=axis)

def _gelu(x):
    return jax.nn.gelu(x, approximate=True)

def _silu(x):
    return jax.nn.silu(x)

def _sigmoid(x):
    return jax.nn.sigmoid(x)

def _layernorm(x, axis=-1, eps=1e-05):
    m = jnp.mean(x, axis=axis, keepdims=True)
    v = jnp.var(x, axis=axis, keepdims=True)
    return (x - m) / jnp.sqrt(v + eps)

def _scatter_add(tgt, idx, src, axis=0):
    return tgt.at[idx].add(src)

def _segment_sum(src, seg, n):
    return jax.ops.segment_sum(src, seg, n)
kernel_name = 'mk_vit_tower_cls_d2_tok_img256_r4_6039fd'

def setup_inputs(seed: int=0):
    np.random.seed(seed)
    _w = jnp.asarray

    def _rec_inputs():
        import jax
        import jax.numpy as jnp
        _rk = jax.random.key(seed)
        x = -4.65018e-05 + 0.999886 * jax.random.normal(jax.random.fold_in(_rk, 1), (32, 3, 128, 128), jnp.float32)
        cls_tok = 0.02 * jax.random.normal(jax.random.fold_in(_rk, 5), (1, 1, 64), jnp.float32)
        return (x, cls_tok)
    x, cls_tok = _rec_inputs()

    def _L0_tok_setup():
        import jax, jax.numpy as jnp
        import numpy as np
        B, C, H, P, D = (64, 3, 128, 16, 64)
        NP = H // P
        key = jax.random.key(seed)
        ks = jax.random.split(key, 7)
        s = lambda fan_in: 1.0 / np.sqrt(fan_in)
        return {'x': jax.random.normal(ks[0], (B, C, H, H), dtype=jnp.float32), 'Wp': jax.random.normal(ks[1], (P * P * C, D), dtype=jnp.float32) * s(P * P * C), 'bp': jax.random.normal(ks[2], (D,), dtype=jnp.float32) * 0.01, 'W1': jax.random.normal(ks[3], (2, D), dtype=jnp.float32) * s(2), 'b1': jax.random.normal(ks[4], (D,), dtype=jnp.float32) * 0.01, 'W2': jax.random.normal(ks[5], (D, D), dtype=jnp.float32) * s(D), 'b2': jax.random.normal(ks[6], (D,), dtype=jnp.float32) * 0.01}
    _L0_tok_all = _L0_tok_setup()
    _L0_tok_in = {k: v for k, v in _L0_tok_all.items() if k in ('Wp', 'bp', 'W1', 'b1', 'W2', 'b2')}
    del _L0_tok_all

    def _L0_attn_setup():
        import jax, jax.numpy as jnp
        import numpy as np
        key = jax.random.key(seed)
        ks = jax.random.split(key, 5)
        b, t, e, h = (8, 256, 64, 8)
        w = lambda k, shape: jax.random.normal(k, shape, dtype=jnp.float32) * 0.02
        return {'x': jax.random.normal(ks[0], (b, t, e), dtype=jnp.float32), 'Wq': w(ks[1], (e, e * h)), 'bq': jnp.zeros((e * h,), jnp.float32), 'Wk': w(ks[2], (e, e * h)), 'bk': jnp.zeros((e * h,), jnp.float32), 'Wv': w(ks[3], (e, e * h)), 'bv': jnp.zeros((e * h,), jnp.float32), 'Wu': w(ks[4], (e * h, e)), 'bu': jnp.zeros((e,), jnp.float32)}
    _L0_attn_all = _L0_attn_setup()
    _L0_attn_in = {k: v for k, v in _L0_attn_all.items() if k in ('Wq', 'bq', 'Wk', 'bk', 'Wv', 'bv', 'Wu', 'bu')}
    del _L0_attn_all

    def _L0_ffn_setup():
        import jax, jax.numpy as jnp
        import numpy as np
        BN_EPS = 0.001

        def _bn(h, g, b, m, v):
            return g * (h - m) * jax.lax.rsqrt(v + BN_EPS) + b
        key = jax.random.key(seed)
        ks = jax.random.split(key, 8)
        B, F, Df = (64, 64, 64)
        E, H, D = (8, 64, 64)
        s1 = 1.0 / np.sqrt(Df)
        s2 = 1.0 / np.sqrt(H)
        return {'x': jax.random.normal(ks[0], (B, F, Df), jnp.float32), 'Wr': jax.random.normal(ks[1], (Df, E), jnp.float32) * s1, 'br': jnp.zeros((E,), jnp.float32), 'W1': jax.random.normal(ks[2], (E, Df, H), jnp.float32) * s1, 'b1': jnp.zeros((E, H), jnp.float32), 'g1': jnp.ones((E, H), jnp.float32), 'be1': jnp.zeros((E, H), jnp.float32), 'm1': jnp.zeros((E, H), jnp.float32), 'v1': jnp.ones((E, H), jnp.float32), 'W2': jax.random.normal(ks[3], (E, H, H), jnp.float32) * s2, 'b2': jnp.zeros((E, H), jnp.float32), 'g2': jnp.ones((E, H), jnp.float32), 'be2': jnp.zeros((E, H), jnp.float32), 'm2': jnp.zeros((E, H), jnp.float32), 'v2': jnp.ones((E, H), jnp.float32), 'Wo': jax.random.normal(ks[4], (E, H, D), jnp.float32) * s2, 'bo': jnp.zeros((E, D), jnp.float32)}
    _L0_ffn_all = _L0_ffn_setup()
    _L0_ffn_in = {k: v for k, v in _L0_ffn_all.items() if k in ('Wr', 'br', 'W1', 'b1', 'g1', 'be1', 'm1', 'v1', 'W2', 'b2', 'g2', 'be2', 'm2', 'v2', 'Wo', 'bo')}
    del _L0_ffn_all

    def _L1_attn_setup():
        import jax, jax.numpy as jnp
        import numpy as np
        H, N, L, BATCH = (64, 64, 512, 4)
        DT_MIN, DT_MAX = (0.001, 0.1)

        def _hippo_pql(n_state):
            n = np.arange(1, n_state + 1)
            hippo = np.where(n[:, None] > n[None, :], np.sqrt(2 * n[:, None] + 1.0) * np.sqrt(2 * n[None, :] + 1.0), np.where(n[:, None] == n[None, :], n[:, None] + 1.0, 0.0))
            p = 0.5 * np.sqrt(2 * n + 1.0)
            q = 2.0 * p
            S = -hippo + p[:, None] * q[None, :]
            lam, V = np.linalg.eig(S)
            Vc = V.conj().T
            p_c = (Vc @ p).astype(np.complex64)
            q_c = (Vc @ q.conj()).astype(np.complex64)
            return (p_c, q_c, lam.astype(np.complex64))

        def _stack_ri(z):
            return jnp.stack([jnp.asarray(z.real, jnp.float32), jnp.asarray(z.imag, jnp.float32)], axis=-1)

        def _forward(u, p_ri, q_ri, lambda_ri, B_ri, Ct_ri, D, log_step):
            l_max = u.shape[1]
            cplx = lambda x: jax.lax.complex(x[..., 0], x[..., 1])
            p, q, lam = (cplx(p_ri), cplx(q_ri), cplx(lambda_ri))
            Bm, Ct = (cplx(B_ri), cplx(Ct_ri))
            omega = jnp.exp(2j * jnp.pi / l_max * jnp.arange(l_max, dtype=jnp.float32)).astype(jnp.complex64)
            step = jnp.exp(log_step)
            g = (2.0 / step).astype(jnp.complex64)[:, None] * ((1.0 - omega) / (1.0 + omega))[None, :]
            c = 2.0 / (1.0 + omega)
            r = 1.0 / (g[:, :, None] - lam[None, None, :])
            a0, a1 = (jnp.conj(Ct), jnp.conj(q))
            b0, b1 = (Bm, p)
            k00 = jnp.einsum('hn,hln->hl', a0 * b0, r)
            k01 = jnp.einsum('hn,hln->hl', a0 * b1[None, :], r)
            k10 = jnp.einsum('hn,hln->hl', a1[None, :] * b0, r)
            k11 = jnp.einsum('n,hln->hl', a1 * b1, r)
            at_roots = c[None, :] * (k00 - k01 * k10 / (1.0 + k11))
            K = jnp.roll(jnp.flip(jnp.fft.ifft(at_roots, axis=-1), axis=-1), 1, axis=-1).real[None]
            ut = jnp.transpose(u, (0, 2, 1))
            ud = jnp.fft.rfft(ut, n=2 * l_max, axis=-1)
            Kd = jnp.fft.rfft(K, n=2 * l_max, axis=-1)
            y = jnp.fft.irfft(ud * Kd, n=2 * l_max, axis=-1)[..., :l_max]
            y = jnp.transpose(y, (0, 2, 1)).astype(u.dtype)
            return y + D * u
        key = jax.random.key(seed)
        k_b, k_ct, k_step, k_u = jax.random.split(key, 4)
        p_c, q_c, lam_c = _hippo_pql(N)
        std = np.sqrt(2.0 / (H + N)).astype(np.float32)
        B_ri = jax.random.normal(k_b, (H, N, 2), jnp.float32) * std
        Ct_ri = jax.random.normal(k_ct, (H, N, 2), jnp.float32) * std
        D = jnp.ones((1, 1, H), jnp.float32)
        scale = np.float32(np.log(DT_MAX) - np.log(DT_MIN))
        log_step = jax.random.uniform(k_step, (H,), jnp.float32) * scale + np.float32(np.log(DT_MIN))
        u = jax.random.normal(k_u, (BATCH, L, H), jnp.float32)
        return {'u': u, 'p_ri': _stack_ri(p_c), 'q_ri': _stack_ri(q_c), 'lambda_ri': _stack_ri(lam_c), 'B_ri': B_ri, 'Ct_ri': Ct_ri, 'D': D, 'log_step': log_step}
    _L1_attn_all = _L1_attn_setup()
    _L1_attn_in = {k: v for k, v in _L1_attn_all.items() if k in ('p_ri', 'q_ri', 'lambda_ri', 'B_ri', 'Ct_ri', 'D', 'log_step')}
    del _L1_attn_all

    def _L1_ffn_setup():
        import math
        import jax, jax.numpy as jnp
        import numpy as np
        CAPACITY_FACTOR = 1.25
        key = jax.random.key(seed)
        ks = jax.random.split(key, 5)
        B, L, D, F, E = (8, 2048, 64, 256, 8)
        h = jax.random.normal(ks[0], (B, L, D), dtype=jnp.float32)
        gate_w = jax.random.normal(ks[1], (D, E), dtype=jnp.float32) * 0.02
        gate_b = jnp.zeros((E,), dtype=jnp.float32)
        w1 = jax.random.normal(ks[2], (E, D, F), dtype=jnp.float32) * (1.0 / math.sqrt(D))
        b1 = jnp.zeros((E, F), dtype=jnp.float32)
        w2 = jax.random.normal(ks[3], (E, F, D), dtype=jnp.float32) * (1.0 / math.sqrt(F))
        b2 = jnp.zeros((E, D), dtype=jnp.float32)
        return {'h': h, 'gate_w': gate_w, 'gate_b': gate_b, 'w1': w1, 'b1': b1, 'w2': w2, 'b2': b2}
    _L1_ffn_all = _L1_ffn_setup()
    _L1_ffn_in = {k: v for k, v in _L1_ffn_all.items() if k in ('gate_w', 'gate_b', 'w1', 'b1', 'w2', 'b2')}
    del _L1_ffn_all
    return {'x': x, 'cls_tok': cls_tok, 'L0_tok_Wp': _L0_tok_in['Wp'], 'L0_tok_bp': _L0_tok_in['bp'], 'L0_tok_W1': _L0_tok_in['W1'], 'L0_tok_b1': _L0_tok_in['b1'], 'L0_tok_W2': _L0_tok_in['W2'], 'L0_tok_b2': _L0_tok_in['b2'], 'L0_attn_Wq': _L0_attn_in['Wq'], 'L0_attn_bq': _L0_attn_in['bq'], 'L0_attn_Wk': _L0_attn_in['Wk'], 'L0_attn_bk': _L0_attn_in['bk'], 'L0_attn_Wv': _L0_attn_in['Wv'], 'L0_attn_bv': _L0_attn_in['bv'], 'L0_attn_Wu': _L0_attn_in['Wu'], 'L0_attn_bu': _L0_attn_in['bu'], 'L0_ffn_Wr': _L0_ffn_in['Wr'], 'L0_ffn_br': _L0_ffn_in['br'], 'L0_ffn_W1': _L0_ffn_in['W1'], 'L0_ffn_b1': _L0_ffn_in['b1'], 'L0_ffn_g1': _L0_ffn_in['g1'], 'L0_ffn_be1': _L0_ffn_in['be1'], 'L0_ffn_m1': _L0_ffn_in['m1'], 'L0_ffn_v1': _L0_ffn_in['v1'], 'L0_ffn_W2': _L0_ffn_in['W2'], 'L0_ffn_b2': _L0_ffn_in['b2'], 'L0_ffn_g2': _L0_ffn_in['g2'], 'L0_ffn_be2': _L0_ffn_in['be2'], 'L0_ffn_m2': _L0_ffn_in['m2'], 'L0_ffn_v2': _L0_ffn_in['v2'], 'L0_ffn_Wo': _L0_ffn_in['Wo'], 'L0_ffn_bo': _L0_ffn_in['bo'], 'L1_attn_p_ri': _L1_attn_in['p_ri'], 'L1_attn_q_ri': _L1_attn_in['q_ri'], 'L1_attn_lambda_ri': _L1_attn_in['lambda_ri'], 'L1_attn_B_ri': _L1_attn_in['B_ri'], 'L1_attn_Ct_ri': _L1_attn_in['Ct_ri'], 'L1_attn_D': _L1_attn_in['D'], 'L1_attn_log_step': _L1_attn_in['log_step'], 'L1_ffn_gate_w': _L1_ffn_in['gate_w'], 'L1_ffn_gate_b': _L1_ffn_in['gate_b'], 'L1_ffn_w1': _L1_ffn_in['w1'], 'L1_ffn_b1': _L1_ffn_in['b1'], 'L1_ffn_w2': _L1_ffn_in['w2'], 'L1_ffn_b2': _L1_ffn_in['b2']}

def reference(x, cls_tok, L0_tok_Wp, L0_tok_bp, L0_tok_W1, L0_tok_b1, L0_tok_W2, L0_tok_b2, L0_attn_Wq, L0_attn_bq, L0_attn_Wk, L0_attn_bk, L0_attn_Wv, L0_attn_bv, L0_attn_Wu, L0_attn_bu, L0_ffn_Wr, L0_ffn_br, L0_ffn_W1, L0_ffn_b1, L0_ffn_g1, L0_ffn_be1, L0_ffn_m1, L0_ffn_v1, L0_ffn_W2, L0_ffn_b2, L0_ffn_g2, L0_ffn_be2, L0_ffn_m2, L0_ffn_v2, L0_ffn_Wo, L0_ffn_bo, L1_attn_p_ri, L1_attn_q_ri, L1_attn_lambda_ri, L1_attn_B_ri, L1_attn_Ct_ri, L1_attn_D, L1_attn_log_step, L1_ffn_gate_w, L1_ffn_gate_b, L1_ffn_w1, L1_ffn_b1, L1_ffn_w2, L1_ffn_b2):
    import jax
    import jax.numpy as jnp

    def _L0_tok_ref(x, Wp, bp, W1, b1, W2, b2):
        import jax, jax.numpy as jnp
        import numpy as np
        B, C, H, P, D = (64, 3, 128, 16, 64)
        NP = H // P
        b = x.shape[0]
        patches = x.reshape(b, C, NP, P, NP, P)
        patches = patches.transpose(0, 2, 4, 1, 3, 5).reshape(b, NP * NP, C * P * P)
        embedded = jnp.einsum('bnk,kd->bnd', patches, Wp) + bp
        gx, gy = jnp.meshgrid(jnp.arange(NP, dtype=jnp.float32), jnp.arange(NP, dtype=jnp.float32), indexing='ij')
        xy = jnp.stack([gx, gy], axis=-1).reshape(1, -1, 2) / (NP - 1)
        pos = jax.nn.relu(xy @ W1 + b1) @ W2 + b2
        return embedded + pos

    def _L0_attn_ref(x, Wq, bq, Wk, bk, Wv, bv, Wu, bu):
        import jax, jax.numpy as jnp
        import numpy as np
        b, t, e = x.shape
        h = Wq.shape[1] // e
        q = (x @ Wq + bq).reshape(b, t, h, e)
        k = (x @ Wk + bk).reshape(b, t, h, e)
        v = (x @ Wv + bv).reshape(b, t, h, e)
        scores = jnp.einsum('bihe,bjhe->bhij', q, k) / jnp.sqrt(jnp.asarray(e, jnp.float32))
        i = jnp.arange(t)[:, None]
        j = jnp.arange(t)[None, :]
        scores = jnp.where(j >= i, -jnp.inf, scores)
        scores = jnp.where(i == 0, 0.0, scores)
        att = jax.nn.softmax(scores, axis=-1)
        att = jnp.where(i == 0, 0.0, att)
        out = jnp.einsum('bhij,bjhe->bihe', att, v).reshape(b, t, h * e)
        return out @ Wu + bu

    def _L0_ffn_ref(x, Wr, br, W1, b1, g1, be1, m1, v1, W2, b2, g2, be2, m2, v2, Wo, bo):
        import jax, jax.numpy as jnp
        import numpy as np
        BN_EPS = 0.001

        def _bn(h, g, b, m, v):
            return g * (h - m) * jax.lax.rsqrt(v + BN_EPS) + b
        feat = jnp.mean(x, axis=0)
        w = jax.nn.softmax(feat @ Wr + br, axis=-1)
        h = jnp.einsum('bfd,edh->bfeh', x, W1) + b1
        h = jax.nn.relu(_bn(h, g1, be1, m1, v1))
        h = jnp.einsum('bfeh,ehk->bfek', h, W2) + b2
        h = jax.nn.relu(_bn(h, g2, be2, m2, v2))
        y = jnp.einsum('bfeh,ehd->bfed', h, Wo) + bo
        return jnp.einsum('bfed,fe->bfd', y, w)

    def _L1_attn_ref(u, p_ri, q_ri, lambda_ri, B_ri, Ct_ri, D, log_step):
        import jax, jax.numpy as jnp
        import numpy as np
        H, N, L, BATCH = (64, 64, 512, 4)
        DT_MIN, DT_MAX = (0.001, 0.1)

        def _hippo_pql(n_state):
            n = np.arange(1, n_state + 1)
            hippo = np.where(n[:, None] > n[None, :], np.sqrt(2 * n[:, None] + 1.0) * np.sqrt(2 * n[None, :] + 1.0), np.where(n[:, None] == n[None, :], n[:, None] + 1.0, 0.0))
            p = 0.5 * np.sqrt(2 * n + 1.0)
            q = 2.0 * p
            S = -hippo + p[:, None] * q[None, :]
            lam, V = np.linalg.eig(S)
            Vc = V.conj().T
            p_c = (Vc @ p).astype(np.complex64)
            q_c = (Vc @ q.conj()).astype(np.complex64)
            return (p_c, q_c, lam.astype(np.complex64))

        def _stack_ri(z):
            return jnp.stack([jnp.asarray(z.real, jnp.float32), jnp.asarray(z.imag, jnp.float32)], axis=-1)

        def _forward(u, p_ri, q_ri, lambda_ri, B_ri, Ct_ri, D, log_step):
            l_max = u.shape[1]
            cplx = lambda x: jax.lax.complex(x[..., 0], x[..., 1])
            p, q, lam = (cplx(p_ri), cplx(q_ri), cplx(lambda_ri))
            Bm, Ct = (cplx(B_ri), cplx(Ct_ri))
            omega = jnp.exp(2j * jnp.pi / l_max * jnp.arange(l_max, dtype=jnp.float32)).astype(jnp.complex64)
            step = jnp.exp(log_step)
            g = (2.0 / step).astype(jnp.complex64)[:, None] * ((1.0 - omega) / (1.0 + omega))[None, :]
            c = 2.0 / (1.0 + omega)
            r = 1.0 / (g[:, :, None] - lam[None, None, :])
            a0, a1 = (jnp.conj(Ct), jnp.conj(q))
            b0, b1 = (Bm, p)
            k00 = jnp.einsum('hn,hln->hl', a0 * b0, r)
            k01 = jnp.einsum('hn,hln->hl', a0 * b1[None, :], r)
            k10 = jnp.einsum('hn,hln->hl', a1[None, :] * b0, r)
            k11 = jnp.einsum('n,hln->hl', a1 * b1, r)
            at_roots = c[None, :] * (k00 - k01 * k10 / (1.0 + k11))
            K = jnp.roll(jnp.flip(jnp.fft.ifft(at_roots, axis=-1), axis=-1), 1, axis=-1).real[None]
            ut = jnp.transpose(u, (0, 2, 1))
            ud = jnp.fft.rfft(ut, n=2 * l_max, axis=-1)
            Kd = jnp.fft.rfft(K, n=2 * l_max, axis=-1)
            y = jnp.fft.irfft(ud * Kd, n=2 * l_max, axis=-1)[..., :l_max]
            y = jnp.transpose(y, (0, 2, 1)).astype(u.dtype)
            return y + D * u
        return _forward(u, p_ri, q_ri, lambda_ri, B_ri, Ct_ri, D, log_step)

    def _L1_ffn_ref(h, gate_w, gate_b, w1, b1, w2, b2):
        import math
        import jax, jax.numpy as jnp
        import numpy as np
        CAPACITY_FACTOR = 1.25
        B, L, D = h.shape
        E = gate_w.shape[1]
        T = B * L
        C = max(1, math.ceil(CAPACITY_FACTOR * T / E))
        x = h.reshape(T, D)
        logits = x @ gate_w + gate_b
        probs = jax.nn.softmax(logits, axis=-1)
        idx = jnp.argmax(probs, axis=-1)
        prb = jnp.take_along_axis(probs, idx[:, None], axis=1)[:, 0]
        one_hot = jax.nn.one_hot(idx, E, dtype=jnp.float32)
        pos = (jnp.cumsum(one_hot, axis=0) * one_hot).sum(-1).astype(jnp.int32) - 1
        kept = pos < C
        pos_safe = jnp.where(kept, pos, C)
        buf = jnp.zeros((E, C, D), dtype=h.dtype).at[idx, pos_safe].set(x, mode='drop')
        hmid = jax.nn.relu(jnp.einsum('ecd,edf->ecf', buf, w1) + b1[:, None, :])
        ybuf = jnp.einsum('ecf,efd->ecd', hmid, w2) + b2[:, None, :]
        pos_g = jnp.minimum(pos, C - 1)
        y_tok = ybuf[idx, pos_g] * (prb * kept)[:, None]
        y = y_tok.reshape(B, L, D)
        y = jnp.nan_to_num(y, nan=0.0, posinf=10000.0, neginf=-10000.0)
        return y
    h = _L0_tok_ref(x, L0_tok_Wp, L0_tok_bp, L0_tok_W1, L0_tok_b1, L0_tok_W2, L0_tok_b2)
    h = jnp.concatenate([jnp.broadcast_to(cls_tok, (h.shape[0], 1, h.shape[2])), h], axis=1)
    h = h + _L0_attn_ref(_layernorm(h, axis=-1), L0_attn_Wq, L0_attn_bq, L0_attn_Wk, L0_attn_bk, L0_attn_Wv, L0_attn_bv, L0_attn_Wu, L0_attn_bu)
    h = h + _L0_ffn_ref(_layernorm(h, axis=-1), L0_ffn_Wr, L0_ffn_br, L0_ffn_W1, L0_ffn_b1, L0_ffn_g1, L0_ffn_be1, L0_ffn_m1, L0_ffn_v1, L0_ffn_W2, L0_ffn_b2, L0_ffn_g2, L0_ffn_be2, L0_ffn_m2, L0_ffn_v2, L0_ffn_Wo, L0_ffn_bo)
    h = h + _L1_attn_ref(_layernorm(h, axis=-1), L1_attn_p_ri, L1_attn_q_ri, L1_attn_lambda_ri, L1_attn_B_ri, L1_attn_Ct_ri, L1_attn_D, L1_attn_log_step)
    h = h + _L1_ffn_ref(_layernorm(h, axis=-1), L1_ffn_gate_w, L1_ffn_gate_b, L1_ffn_w1, L1_ffn_b1, L1_ffn_w2, L1_ffn_b2)
    return h

_drawn_inputs = setup_inputs


def setup_inputs(seed=0):
    import zlib

    import numpy as np

    out = dict(_drawn_inputs(seed))
    spreads = {'L0_attn_bq': (0.0, 0.8),
     'L0_attn_bk': (0.0, 0.8),
     'L0_attn_bv': (0.0, 0.1),
     'L0_attn_bu': (0.0, 0.1),
     'L0_ffn_br': (0.0, 0.1),
     'L0_ffn_b1': (0.0, 0.399),
     'L0_ffn_g1': (1.0, 0.2),
     'L0_ffn_be1': (0.0, 0.388),
     'L0_ffn_m1': (0.0, 0.408),
     'L0_ffn_v1': (1.0, 0.6),
     'L0_ffn_b2': (0.0, 0.302),
     'L0_ffn_g2': (1.0, 0.2),
     'L0_ffn_be2': (0.0, 0.327),
     'L0_ffn_m2': (0.0, 0.289),
     'L0_ffn_v2': (1.0, 0.6),
     'L0_ffn_bo': (0.0, 0.1),
     'L1_attn_D': (1.0, 0.2),
     'L1_ffn_gate_b': (0.0, 0.1),
     'L1_ffn_b1': (0.0, 0.8),
     'L1_ffn_b2': (0.0, 0.8)}
    factors = {'L0_tok_bp': 5.042,
     'L0_tok_b1': 7.292,
     'L0_tok_b2': 4.737,
     'L0_attn_Wq': 8.0,
     'L0_attn_Wk': 8.0,
     'L1_attn_p_ri': 4.956,
     'L1_attn_q_ri': 6.621,
     'L1_attn_lambda_ri': 5.951,
     'L1_attn_B_ri': 5.522,
     'L1_attn_Ct_ri': 5.355,
     'L1_attn_log_step': 6.447}
    for name, (base, spread) in spreads.items():
        noise = np.random.default_rng([zlib.crc32(name.encode()), seed]).standard_normal(out[name].shape)
        drawn = base * np.exp(spread * noise) if base else spread * noise
        out[name] = jnp.asarray(drawn.astype(out[name].dtype))
    for name, factor in factors.items():
        out[name] = (out[name] * factor).astype(out[name].dtype)
    return out
```

```python
from contextlib import ExitStack

import numpy as np

import concourse.bass as bass
from concourse import mybir

B, CH, IMG, P = 32, 3, 128, 16
D = 64
NG = IMG // P
NPOS = NG * NG
L = NPOS + 1
KT = CH * P * P // 128
NH = 8
G = 4
GB = B // G
PAIRS = B // 2
NE = 8
EP = NE // 2
F = 256
CAP = -(-5 * B * L // (4 * NE))
SL = 384
SC = SL // 128
DROP = 1.0e6
LN_EPS, BN_EPS = 1e-5, 1e-3
RSC = 2.0 ** -24
KW = D + L + 1
BCH = [(0, 7), (7, 7), (14, 6), (20, 6), (26, 6)]

F32 = mybir.dt.float32
BF16 = mybir.dt.bfloat16
U32 = mybir.dt.uint32
ALU = mybir.AluOpType
ACT = mybir.ActivationFunctionType
X = mybir.AxisListType.X


def shape_constants():
    l = np.arange(L)
    tau = np.tan(np.pi * l / L)
    c128 = np.zeros((128, 128 + L + 64), np.float32)
    c128[:, :128] = np.eye(128)
    c128[:, 128:128 + L] = 2.0 * RSC * tau[None]
    i, j = np.arange(128)[:, None] % 64, np.arange(64)[None]
    c128[:, 128 + L:] = np.where(j <= i, 0.0, -1.0e30)
    k = np.concatenate([np.full(D, -1), np.arange(L), [0]])
    ang = 2 * np.pi * ((l[:, None] * np.maximum(k, 0)[None]) % L) / L
    used = (k >= 0)[None] / L
    pos = np.concatenate([np.arange(1, L), [0]])
    tri = (pos[:, None] <= pos[None]).astype(np.float64)
    base = np.repeat(np.arange(NE) * SL, B)
    chained = np.tile((np.arange(B) > 0) * 1.0, NE)
    first = np.tile(NE - np.arange(NE), B)
    cl = np.concatenate([np.cos(ang) * used, np.sin(ang) * used, tau[:, None], tri], axis=1)
    cr = np.tile(np.concatenate([base, chained, first]), (L, 1))
    n = np.arange(NPOS)
    xy = np.stack([n // NG / (NG - 1), n % NG / (NG - 1), np.ones(NPOS)])
    sel = np.zeros((NE, EP, 128))
    for e in range(NE):
        sel[e, e // 2, 64 * (e % 2):64 * (e % 2) + 64] = 1.0
    return {"c128": c128, "cl": cl.astype(np.float32), "cr": cr.astype(np.float32), "cxy": xy.astype(np.float32),
            "csel": sel.reshape(NE, EP * 128).astype(np.float32)}


def build(nc, t, out):
    kd = nc.dram_tensor("kernel_rows", (D, KW), F32, kind="Internal").ap()
    slots = nc.dram_tensor("expert_slots", (NE * SL, D), F32, kind="Internal").ap()
    yslots = nc.dram_tensor("expert_out", (NE * SL, D), F32, kind="Internal").ap()

    ctx = ExitStack()
    with ctx:
        def sb(name, shape, dt=F32):
            return ctx.enter_context(nc.sbuf_tensor(name, shape, dt))

        def sem(name):
            return ctx.enter_context(nc.semaphore(name))

        ps = ctx.enter_context(nc.psum_tensor("ps", [128, 8, 512], F32))

        rx = sb("rx", [128, NX * 2048])
        rxt = sb("rxt", [128, KT * 1024])
        rz = sb("rz", [128, 8192])
        rv = sb("rv", [128, 8192])
        rs = sb("rs", [128, 3 * 32 * L])

        ximg = rx[:, :].rearrange("p (c y x) -> p c y x", c=NX, y=P)
        xt = rxt[:, :].rearrange("p (k b y x) -> p k b y x", k=KT, y=NG, x=NG)
        et = rx[0:D, 2048:3072].rearrange("p (a n) -> p a n", a=2)
        zz = [r.rearrange("p (b h j) -> p b h j", b=GB, h=NH) for r in
              (rz[0:L, 0:4096], rz[0:L, 4096:8192], rx[0:L, 0:4096], rx[0:L, 4096:8192])]
        vv = rv[:, :].rearrange("p (b h d) -> p b h d", b=B, h=NH // 2)
        xr = [rv[:, 4096 + 2048 * i:6144 + 2048 * i].rearrange("p (k g n) -> p k g n", k=2, g=NG) for i in range(2)]
        g_w = rs[:, 0:32 * L].rearrange("p (h l) -> p h l", h=32)
        g_inv = rs[:, 32 * L:64 * L].rearrange("p (h l) -> p h l", h=32)
        g_winv = rs[:, 64 * L:96 * L].rearrange("p (h l) -> p h l", h=32)
        sx = [rs[:, 512 * i:512 * i + 512] for i in range(2)]
        pp = [rs[:, 1024 + 512 * i:1536 + 512 * i] for i in range(2)]
        pt = [rs[:, 2048 + 512 * i:2560 + 512 * i] for i in range(2)]
        toep = rxt[0:L, 0:D * L].rearrange("p (h l) -> p h l", h=D)
        h1 = [rv[:, 512 * i:512 * i + 512] for i in range(2)]
        h2 = [rv[:, 1024 + 512 * i:1536 + 512 * i] for i in range(2)]
        h2w = [rv[:, 2048 + 512 * i:2560 + 512 * i] for i in range(2)]
        y3 = [rv[0:D, 3072 + 512 * i:3584 + 512 * i] for i in range(2)]
        xb = rv[:, 4096:4096 + NE * SC * D].rearrange("p (c d) -> p c d", d=D)
        yb = rv[:, 6144:6144 + NE * SC * D].rearrange("p (c d) -> p c d", d=D)
        xe = rz[0:L, 0:NE * SL].rearrange("p (e s) -> p e s", e=NE)
        hm = [rz[:, 4096 + 768 * i:4864 + 768 * i].rearrange("p (f s) -> p f s", f=2) for i in range(2)]
        yg = rx[0:L, 0:B * D].rearrange("p (b d) -> p b d", d=D)
        scr = rx[0:L, 2048:2048 + 3 * 512].rearrange("p (a n) -> p a n", a=3)
        w1e = rx[0:L, 8192:8192 + NE * F].rearrange("p (e f) -> p e f", e=NE)
        w2e = rxt[:, 4160:4160 + NE * 2 * D].rearrange("p (e f d) -> p e f d", e=NE, f=2)
        b2e = rxt[:, 5184:5184 + NE * D].rearrange("p (e d) -> p e d", e=NE)

        c128 = sb("c128_sb", [128, 128 + L + 64])
        ident, ttab, cmask = c128[:, 0:128], c128[:, 128:128 + L], c128[:, 128 + L:]
        cl = sb("cl_sb", [L, 2 * KW + 1 + L])
        cr = rs[0:L, 2048:2048 + 3 * NE * B]
        o = 2 * KW + 1
        cosx, sinx, tau, tri = cl[:, 0:KW], cl[:, KW:2 * KW], cl[:, o - 1:o], cl[:, o:o + L]
        ebase, chained, first = (cr[:, NE * B * i:NE * B * (i + 1)] for i in range(3))
        cxy = sb("cxy_sb", [3, NPOS])
        ibf = sb("ibf", [128, 128], BF16)
        mbf = sb("mbf", [128, 512], BF16)
        tribf = sb("tribf", [L, L], BF16)
        onebf = sb("onebf", [L, L], BF16)
        ones = sb("ones", [1, 64])
        expo = sb("expo", [128, 8])
        hh = sb("hh", [L, B, D])
        uu = sb("uu", [L, B, D])
        sq = sb("sq", [L, 2, GB * D])
        ut = sb("ut", [L, B, L])
        st = sb("st", [L, 4, 4 * G, GB])
        wp = sb("wp", [128, KT, D])
        w1t, w2t, bpt = sb("w1t", [3, D]), sb("w2t", [L, D]), sb("bpt", [1, D])
        rr, posb = sb("rr", [L, NPOS]), sb("posb", [NPOS, D])
        wqkv = [rz[0:L, 512 * i:512 * i + 512] for i in range(3)]
        wu = rz[0:D, 1536:2048].rearrange("p (h d) -> p h d", h=NH)
        wt = [rz[0:D, 2048 + NH * L * i:2048 + NH * L * (i + 1)].rearrange("p (h l) -> p h l", h=NH) for i in range(3)]
        mm_ = sb("mm_", [L, NH, L])
        nn_ = sb("nn_", [L, 2, NH // 2, D])
        bub = sb("bub", [L, D])
        mx, rc = sb("mx", [128, 2, NH]), sb("rc", [128, 2, NH])
        lam, pri, qri = sb("lam", [128, 2]), sb("pri", [128, 2]), sb("qri", [128, 2])
        bct = rz[0:32, 3616:4128].rearrange("p (q a n r) -> p q a n r", q=2, a=2, r=2)
        bc = sb("bc", [128, 4, 32])
        lsb, gg = sb("lsb", [128, 32]), sb("gg", [128, 32])
        dcol = sb("dcol", [D, 1])
        ws = sb("ws", [128, 8])
        wc = sb("wc", [128, 4, 2, 32])
        wtmp = sb("wtmp", [128, 2, 32])
        zeros = sb("zeros", [128, 256])
        va, vb = sb("va", [128, 32, 2, 8]), sb("vb", [128, 32, 2, 8])
        ks = rs[0:L, 4864:4864 + 8 * D].rearrange("p (c h) -> p c h", c=8)
        kt_ = rs[0:L, 5376:5376 + 10 * D].rearrange("p (c h) -> p c h", c=10)
        kx = sb("kx", [D, KW])
        bnr = sb("bnr", [40, 128])
        bn = sb("bn", [128, 10, EP])
        bna = sb("bna", [128, 4, EP])
        wra = sb("wra", [L, NE])
        w1r = rs[0:D, 3072:3584].rearrange("p (e h) -> p e h", e=NE)
        w2f = rs[:, 3584:4096].rearrange("p (a k) -> p a k", a=EP)
        wof = rs[:, 4096:4352].rearrange("p (a d) -> p a d", a=EP)
        csel = rs[0:NE, 4352:4864]
        bof = sb("bof", [NE, D])
        feat = sb("feat", [L, L])
        rt = sb("rt", [L, 40])
        wtt = sb("wtt", [NE, L])
        wb = sb("wb", [128, EP, L])
        bow = sb("bow", [L, D])
        gwa = sb("gwa", [L, NE])
        ra = rs[0:L, 0:1536].rearrange("p (a n) -> p a n", a=6)
        ohb = sb("ohb", [L, 256], BF16)
        rb = sb("rb", [L, 12, B])
        idxs, idxg = sb("idxs", [L, B], U32), sb("idxg", [L, B], U32)
        fin = rs[0:L, 1536:2048].bitcast(U32)

        cst_in, tok_in, qkv_in, s4_in, cls_in = (sem(n) for n in ("cst_in", "tok_in", "qkv_in", "s4_in", "cls_in"))
        bn_in, ffn_in, moe_in = sem("bn_in"), sem("ffn_in"), sem("moe_in")
        x_in = [sem(f"x_in{i}") for i in range(2 * CH)]
        wp_in = sem("wp_in")
        w2_zero = sem("w2_zero")
        set_v, set_p = sem("set_v"), sem("set_p")
        wt_done, wt_cp, mn_done, mn_cp = sem("wt_done"), sem("wt_cp"), sem("mn_done"), sem("mn_cp")
        r_done, r_cp, pos_done, pos_cp = sem("r_done"), sem("r_cp"), sem("pos_done"), sem("pos_cp")
        bt_done, bt_cp = sem("bt_done"), sem("bt_cp")
        bn_done, bn_cp, bn_pow, bn_ok = sem("bn_done"), sem("bn_cp"), sem("bn_pow"), sem("bn_ok")
        vstep = sem("vstep")
        g_exp, g_outer, g_shift, g_sq, g_recip, g_prod = (sem(n) for n in (
            "g_exp", "g_outer", "g_shift", "g_sq", "g_recip", "g_prod"))
        g_den, vab_ok, kk_done, kk_cp, at_ok, kx_done, kx_ok = (sem(n) for n in (
            "g_den", "vab_ok", "kk_done", "kk_cp", "at_ok", "kx_done", "kx_ok"))
        kd_out, t_in, t_zero = sem("kd_out"), sem("t_in"), sem("t_zero")
        xr_ok, xt_done, xt_cv, xt_ca = sem("xr_ok"), sem("xt_done"), sem("xt_cv"), sem("xt_ca")
        emb_done, et_cp, lt_done, h0_ok = sem("emb_done"), sem("et_cp"), sem("lt_done"), sem("h0_ok")
        ln_sum, ln_mean, ln_cen, ln_sq, ln_var, ln_vs, ln_pow, ln_u = (sem(n) for n in (
            "ln_sum", "ln_mean", "ln_cen", "ln_sq", "ln_var", "ln_vs", "ln_pow", "ln_u"))
        ut_done, ut_cp = sem("ut_done"), sem("ut_cp")
        z_done, z_cp, v_done, v_cp = sem("z_done"), sem("z_cp"), sem("v_done"), sem("v_cp")
        s_done, mx_ok, sub_ok, exp_ok, sum_ok, rc_ok, p_ok = (sem(n) for n in (
            "s_done", "mx_ok", "sub_ok", "exp_ok", "sum_ok", "rc_ok", "p_ok"))
        pt_done, pt_cp, pv_done, bu_add, o_add = (sem(n) for n in ("pt_done", "pt_cp", "pv_done", "bu_add", "o_add"))
        ft_ok, lg_done, rt_exp, w_ok, wtt_done, wtt_cp, wb_done, wb_cp, bow_add = (sem(n) for n in (
            "ft_ok", "lg_done", "rt_exp", "w_ok", "wtt_done", "wtt_cp", "wb_done", "wb_cp", "bow_add"))
        l1_done, r1_ok, l2_done, r2_ok, wm_ok, l3_step, y3_cp, yt_done, y_add = (sem(n) for n in (
            "l1_done", "r1_ok", "l2_done", "r2_ok", "wm_ok", "l3_step", "y3_cp", "yt_done", "y_add"))
        cv_done, cv_add = sem("cv_done"), sem("cv_add")
        gt_done, gt_sub, gt_exp, oh_ok, pre_done, idx_ok, co_ok = (sem(n) for n in (
            "gt_done", "gt_sub", "gt_exp", "oh_ok", "pre_done", "idx_ok", "co_ok"))
        z_out, sc_out, xe_one = sem("z_out"), sem("sc_out"), sem("xe_one")
        xb_in = [sem(f"xb_in{i}") for i in range(2)]
        xe_done, xe_cp, f1_done, f1_ca, f1_cv, f2_done, yb_ok, y_out = (sem(n) for n in (
            "xe_done", "xe_cp", "f1_done", "f1_ca", "f1_cv", "f2_done", "yb_ok", "y_out"))
        yg_in = [sem(f"yg_in{g}") for g in range(G)]
        fin_ok, o_out = sem("fin_ok"), sem("o_out")

        def bank(i, n=512, rows=128, at=0):
            return ps[0:rows, i, at:at + n]

        def grp(x, g):
            return x[:, GB * g:GB * g + GB]

        def move_patches(eng, r):
            c, k, g = r // 4, (r % 4) // 2, r % 2
            out_ = xt[:, 2 * (c % CH) + k, :, :, 4 * g:4 * g + 4].rearrange("p b y x -> p x (b y)")
            in_ = bank(r % 4).rearrange("p (x n) -> p x n", x=4)
            return eng.copy(out_, in_) if r % 2 else eng.tensor_copy(out_, in_)

        block = ctx.enter_context(nc.Block())

        @block.sync
        def _(sp):
            sp.dma_start(c128[:, :], t["c128"]).then_inc(cst_in, 16)
            sp.dma_start(cl[:, :], t["cl"]).then_inc(cst_in, 16)
            for c in range(2 * CH):
                src = t["x"][16 * (c // CH):16 * (c // CH) + 16, c % CH].rearrange("b (g y) x -> b g (y x)", g=NG)
                if c >= NX:
                    sp.wait_ge(xr_ok, 2 * (c - NX + 1))
                q = 2048 * (c % NX)
                sp.dma_start(rx[:, q:q + 2048], src).then_inc(x_in[c], 16)
            for j, name in enumerate(("v1", "g1", "b1", "m1", "be1", "v2", "g2", "b2", "m2", "be2")):
                sp.dma_start(bnr[EP * j:EP * j + EP, :],
                             t["L0_ffn_" + name].rearrange("(p e) h -> p (e h)", e=2)).then_inc(bn_in, 16)
            sp.dma_start(wra[0:D, :], t["L0_ffn_Wr"]).then_inc(ffn_in, 16)
            sp.dma_start(wra[D:L, :], t["L0_ffn_br"].unsqueeze(0)).then_inc(ffn_in, 16)
            sp.wait_ge(kk_done, 1)
            sp.dma_start(w1r[:, :, :], t["L0_ffn_W1"].rearrange("e d h -> d e h")).then_inc(ffn_in, 16)
            sp.wait_ge(w2_zero, 1)
            for q in range(2):
                sp.dma_start(w2f[D * q:D * q + D, :, D * q:D * q + D],
                             t["L0_ffn_W2"].rearrange("(p e) h k -> e h p k", e=2)[q]).then_inc(ffn_in, 16)
            sp.dma_start(wof[:, :, :], t["L0_ffn_Wo"].rearrange("(p e) h d -> (e h) p d", e=2)).then_inc(ffn_in, 16)
            sp.dma_start(bof[:, :], t["L0_ffn_bo"]).then_inc(ffn_in, 16)
            sp.dma_start(csel[:, :], t["csel"]).then_inc(ffn_in, 16)
            for q in range(NE * SC // 4):
                sp.dma_start(slots[512 * q:512 * q + 512, :].rearrange("(p c) d -> p (c d)", p=128),
                             zeros[:, :]).then_inc(z_out, 16)
            sp.wait_ge(kx_ok, 1)
            sp.dma_start(kd, kx[:, :]).then_inc(kd_out, 16)
            sp.wait_ge(kd_out, 16)
            sp.wait_ge(emb_done, G)
            for m in range(D):
                sp.dma_start(toep[m:m + 1, :, 0:D], kd[:, D - m:2 * D - m].unsqueeze(0)).then_inc(t_in, 16)
            sp.dma_start(toep[D:L, :, :], kd[:, D + 1:KW].unsqueeze(0)).then_inc(t_in, 16)
            sp.wait_ge(s_done, PAIRS)
            sp.dma_start(w1e[0:D, :, :], t["L1_ffn_w1"].rearrange("e d f -> d e f")).then_inc(moe_in, 16)
            sp.dma_start(w1e[D:L, :, :], t["L1_ffn_b1"].unsqueeze(0)).then_inc(moe_in, 16)
            sp.dma_start(w2e[:, :, :, :], t["L1_ffn_w2"].rearrange("e (f p) d -> p e f d", p=128)).then_inc(moe_in, 16)
            sp.dma_start(b2e[:, :, :], t["L1_ffn_b2"].partition_broadcast(128)).then_inc(moe_in, 16)
            sp.wait_ge(pv_done, 2 * PAIRS)
            sp.dma_start(cr, t["cr"]).then_inc(moe_in, 16)
            sp.dma_start(gwa[0:D, :], t["L1_ffn_gate_w"]).then_inc(moe_in, 16)
            sp.dma_start(gwa[D:L, :], t["L1_ffn_gate_b"].unsqueeze(0)).then_inc(moe_in, 16)
            sp.wait_ge(sc_out, 16 * B)
            for q in range(2):
                n = NE * SC // 2
                sp.dma_start(xb[:, n * q:n * q + n, :],
                             slots[128 * n * q:128 * n * (q + 1), :].rearrange("(c p) d -> p c d", p=128)
                             ).then_inc(xb_in[q], 16)
            for e in range(NE):
                sp.wait_ge(yb_ok, e + 1)
                sp.dma_start(yslots[SL * e:SL * e + SL, :].rearrange("(c p) d -> p c d", p=128),
                             yb[:, SC * e:SC * e + SC, :]).then_inc(y_out, 16)
            for g in range(G):
                sp.wait_ge(fin_ok, g + 1)
                o_g = out[GB * g:GB * g + GB]
                sp.dma_start(o_g[:, 1:L, :].rearrange("b l d -> l b d"), grp(hh[0:D], g)).then_inc(o_out, 16)
                sp.dma_start(o_g[:, 0:1, :].rearrange("b l d -> l b d"), grp(hh[D:L], g)).then_inc(o_out, 16)
            sp.wait_ge(o_out, 32 * G)

        @block.gpsimd
        def _(po):
            for r, name in ((lam, "lambda"), (pri, "p"), (qri, "q")):
                for q in range(2):
                    po.dma_start(r[D * q:D * q + D, :], t[f"L1_attn_{name}_ri"]).then_inc(s4_in, 16)
            for q in range(2):
                po.dma_start(lsb[D * q:D * q + D, :],
                             t["L1_attn_log_step"][32 * q:32 * q + 32].partition_broadcast(D)).then_inc(s4_in, 16)
            for q, name in enumerate(("B", "Ct")):
                po.dma_start(bct[:, q], t[f"L1_attn_{name}_ri"].rearrange("(a h) n r -> h a n r", a=2)).then_inc(s4_in, 16)
            po.dma_start(dcol[:, :], t["L1_attn_D"].rearrange("a b h -> (a b h)").unsqueeze(1)).then_inc(s4_in, 16)
            po.dma_start(cxy[:, :], t["cxy"]).then_inc(tok_in, 16)
            po.dma_start(w1t[0:2, :], t["L0_tok_W1"]).then_inc(tok_in, 16)
            po.dma_start(w1t[2:3, :], t["L0_tok_b1"].unsqueeze(0)).then_inc(tok_in, 16)
            po.dma_start(w2t[0:D, :], t["L0_tok_W2"]).then_inc(tok_in, 16)
            po.dma_start(w2t[D:L, :], t["L0_tok_b2"].unsqueeze(0)).then_inc(tok_in, 16)
            po.dma_start(bpt[:, :], t["L0_tok_bp"].unsqueeze(0)).then_inc(tok_in, 16)
            po.dma_start(hh[D:L, :, :], t["cls_tok"].rearrange("a b d -> (a b) d").broadcast_to([B, D]).unsqueeze(0)
                         ).then_inc(cls_in, 16)
            po.dma_start(bub[:, :], t["L0_attn_bu"].partition_broadcast(L)).then_inc(cls_in, 16)
            for n, (tile, value) in enumerate(((ones[:, :], 1.0), (rr[D:L, :], 1.0),
                                (ut[D:L, :, :], 1.0), (expo[:, :], -0.5), (zeros[:, :], 0.0),
                                (va[:, :, :, :], 0.0), (vb[:, :, :, :], 0.0))):
                po.memset(tile, value).then_inc(set_p, 1)
                po.wait_ge(set_p, n + 1)
            po.wait_ge(g_exp, 1)
            po.wait_ge(cst_in, 32)
            po.tensor_tensor(g_w, gg[:, :].unsqueeze(2).broadcast_to([128, 32, L]),
                             ttab.unsqueeze(1).broadcast_to([128, 32, L]), ALU.mult).then_inc(g_outer, 1)
            po.wait_ge(set_p, N_SET_P)
            po.wait_ge(g_recip, 1)
            po.tensor_tensor(g_winv, g_w, g_inv, ALU.mult).then_inc(g_prod, 1)

            def root(i):
                po.wait_ge(ln_vs, i + 1)
                po.tensor_tensor(st[:, 3, i, :], st[:, 2, i, :], expo[0:L, 0:GB], ALU.pow).then_inc(ln_pow, 1)

            def norm(p):
                po.wait_ge(rc_ok, p + 1)
                if p >= 2:
                    po.wait_ge(pt_done, p - 1)
                po.tensor_tensor(pp[p % 2].rearrange("p (h j) -> p h j", h=NH),
                                 sx[p % 2].rearrange("p (h j) -> p h j", h=NH),
                                 rc[:, p % 2].unsqueeze(2).broadcast_to([128, NH, 64]), ALU.mult).then_inc(p_ok, 1)

            def bias_u(g):
                po.wait_ge(ln_cen, g + 1)
                po.wait_ge(cls_in, 32)
                po.tensor_tensor(grp(hh, g), grp(hh, g), bub[:, :].unsqueeze(1).broadcast_to([L, GB, D]),
                                 ALU.add).then_inc(bu_add, 1)

            for g in range(G):
                root(g)
                bias_u(g)
                if g == 1:
                    po.wait_ge(kk_done, 1)
                    po.memset(w2f[:, :, :], 0.0).then_inc(w2_zero, 1)
            po.wait_ge(bn_cp, 3)
            po.wait_ge(set_p, N_SET_P)
            for i in range(2):
                po.tensor_tensor(bna[:, 2 * i, :], bn[:, 5 * i, :], expo[:, 0:EP], ALU.pow).then_inc(bn_pow, 1)
            for p in range(PAIRS + 1):
                if p < PAIRS:
                    norm(p)
                if p >= 4 and p % 4 == 0:
                    root(G + p // 4 - 1)
            po.wait_ge(wb_cp, 2)
            for g in range(G):
                po.wait_ge(ln_cen, G + g + 1)
                po.tensor_tensor(grp(hh, g), grp(hh, g), bow[:, :].unsqueeze(1).broadcast_to([L, GB, D]),
                                 ALU.add).then_inc(bow_add, 1)
            for g in range(2 * G):
                root(2 * G + g)
            po.wait_ge(idx_ok, 2)
            po.wait_ge(z_out, 16 * NE * SC // 4)
            po.wait_ge(ln_u, 4 * G)
            for b in range(B):
                po.indirect_dma_start(out=slots, out_offset=bass.IndirectOffsetOnAxis(ap=idxs[:, b:b + 1], axis=0),
                                      in_=uu[:, b, :], in_offset=None, bounds_check=NE * SL - 1,
                                      oob_is_err=False).then_inc(sc_out, 16)
            po.wait_ge(y_out, 16 * NE)
            for b in range(B):
                po.indirect_dma_start(out=yg[:, b, :], out_offset=None, in_=yslots,
                                      in_offset=bass.IndirectOffsetOnAxis(ap=idxg[:, b:b + 1], axis=0),
                                      bounds_check=NE * SL - 1, oob_is_err=False).then_inc(yg_in[b // GB], 16)

        @block.scalar
        def _(sc):
            for w, n in zip(wqkv, "qkv"):
                sc.dma_start(w[0:D, :], t[f"L0_attn_W{n}"]).then_inc(qkv_in, 16)
                sc.dma_start(w[D:L, :], t[f"L0_attn_b{n}"].unsqueeze(0)).then_inc(qkv_in, 16)
            sc.dma_start(wu[:, :, :], t["L0_attn_Wu"].rearrange("(h e) d -> e h d", h=NH)).then_inc(qkv_in, 16)
            sc.dma_start(wp[:, :, :], t["L0_tok_Wp"].rearrange("(k p) d -> p k d", p=128)).then_inc(wp_in, 16)
            sc.wait_ge(s4_in, 16 * N_S4)
            sc.activation(gg[:, :], lsb[:, :], ACT.Exp, scale=-1.0).then_inc(g_exp, 1)
            sc.wait_ge(r_done, 1)
            sc.activation(rr[0:D, :], bank(1, NPOS, D), ACT.Relu).then_inc(r_cp, 1)
            sc.wait_ge(g_shift, 1)
            sc.activation(g_inv, g_w, ACT.Square).then_inc(g_sq, 1)

            def patches(r):
                sc.wait_ge(xt_done, r + 1)
                move_patches(sc, r).then_inc(xt_ca, 1)

            def embedded(g):
                sc.wait_ge(emb_done, g + 1)
                if g >= 2:
                    sc.wait_ge(lt_done, g - 1)
                sc.copy(et[:, g % 2, :], bank(4, 512, D)).then_inc(et_cp, 1)

            def square(i):
                sc.wait_ge(ln_cen, i + 1)
                if i >= 2:
                    sc.wait_ge(ln_var, i - 1)
                sc.activation(sq[:, i % 2, :].rearrange("p (b d) -> p b d", b=GB), grp(uu, i % G),
                              ACT.Square).then_inc(ln_sq, 1)

            def turned(i, attention):
                for q in range(2):
                    sc.wait_ge(ut_done, 2 * i + q + 1)
                    if i == 0 and q == 0:
                        sc.wait_ge(set_p, N_SET_P)
                    b0 = GB * (i % G) + 4 * q
                    src = bank(q, 4 * L, D).rearrange("p (b l) -> p b l", b=4)
                    if attention:
                        sc.copy(ut[0:D, b0:b0 + 4, 1:L], src[:, :, 0:D])
                        sc.copy(ut[0:D, b0:b0 + 4, 0:1], src[:, :, D:L]).then_inc(ut_cp, 1)
                    else:
                        sc.copy(ut[0:D, b0:b0 + 4, :], src).then_inc(ut_cp, 1)

            def keys(g, h):
                sc.wait_ge(z_done, NH * g + h + 1)
                sc.copy(zz[g][:, :, h, :], bank(h % 2, 512, L).rearrange("p (b j) -> p b j", b=GB)).then_inc(z_cp, 1)

            def values(g, q):
                sc.wait_ge(v_done, 4 * g + q + 1)
                b0 = GB * g + 2 * q
                sc.copy(vv[:, b0:b0 + 2].rearrange("p b h d -> p (b h d)"), bank(2)).then_inc(v_cp, 1)

            def prep(g):
                turned(g, True)
                for q in range(4):
                    keys(g, 2 * q)
                    keys(g, 2 * q + 1)
                    values(g, q)

            def expo_(p):
                sc.wait_ge(sub_ok, p + 1)
                sc.activation(sx[p % 2], sx[p % 2], ACT.Exp, scale=float(D) ** -0.5).then_inc(exp_ok, 1)

            def ptcopy(p):
                sc.wait_ge(pt_done, p + 1)
                if p >= 2:
                    sc.wait_ge(pv_done, 2 * (p - 1))
                sc.copy(pt[p % 2], bank(5 + p % 2)).then_inc(pt_cp, 1)

            for r in range(1, 12, 2):
                patches(r)
            embedded(0)
            embedded(1)
            square(0)
            square(1)
            prep(0)
            prep(1)
            for r in range(13, 24, 2):
                patches(r)
            embedded(2)
            embedded(3)
            square(2)
            square(3)
            prep(2)
            prep(3)
            for p in range(PAIRS + 2):
                if p < PAIRS:
                    expo_(p)
                if 1 <= p <= PAIRS:
                    ptcopy(p - 1)
                if p >= 5 and (p - 5) % 4 == 0:
                    square(G + (p - 5) // 4)
                if p == PAIRS + 1:
                    pass
            for g in range(G):
                turned(G + g, False)
            sc.wait_ge(rt_exp, 1)
            sc.activation(rt[:, 8:16], bank(6, NE, L), ACT.Exp, bias=rt[:, 0:1], accum_out=rt[:, 1:2]).then_inc(rt_exp, 1)

            def relu1(k):
                sc.wait_ge(l1_done, k + 1)
                if k >= 2:
                    sc.wait_ge(l2_done, k - 1)
                if k == 0:
                    sc.wait_ge(bn_ok, 2)
                n = BCH[k // EP][1] * L
                sc.activation(h1[k % 2][:, 0:n], bank(k % 2, n), ACT.Relu, bias=bna[:, 1, k % EP:k % EP + 1],
                              scale=bna[:, 0, k % EP:k % EP + 1]).then_inc(r1_ok, 1)

            def relu2(k):
                sc.wait_ge(l2_done, k + 1)
                if k >= 2:
                    sc.wait_ge(wm_ok, k - 1)
                n = BCH[k // EP][1] * L
                sc.activation(h2[k % 2][:, 0:n], bank(2 + k % 2, n), ACT.Relu, bias=bna[:, 3, k % EP:k % EP + 1],
                              scale=bna[:, 2, k % EP:k % EP + 1]).then_inc(r2_ok, 1)

            def mixed(c):
                sc.wait_ge(l3_step, EP * (c + 1))
                if c >= 2:
                    sc.wait_ge(yt_done, c - 1)
                n = BCH[c][1] * L
                sc.copy(y3[c % 2][:, 0:n], bank(4 + c % 2, n, D)).then_inc(y3_cp, 1)

            steps = EP * len(BCH)
            for k in range(steps + 3):
                if k < steps:
                    relu1(k)
                if 1 <= k <= steps:
                    relu2(k - 1)
                if k >= 2 and (k - 2) % EP == EP - 1:
                    mixed((k - 2) // EP)
            for g in range(G):
                square(2 * G + g)
            for g in range(G):
                square(3 * G + g)
            for g in range(G):
                turned(2 * G + g, False)
            sc.wait_ge(gt_sub, 1)
            sc.activation(ra[:, 0, :], ra[:, 0, :], ACT.Exp).then_inc(gt_exp, 1)
            sc.wait_ge(xe_one, 1)
            for e in range(NE + 1):
                if e < NE:
                    sc.wait_ge(xe_done, e + 1)
                    sc.copy(xe[0:D, e, :], bank(e % 2, SL, D)).then_inc(xe_cp, 1)
                if e >= 1:
                    sc.wait_ge(f1_done, 2 * e - 1)
                    if e >= 3:
                        sc.wait_ge(f2_done, e - 2)
                    sc.activation(hm[(e - 1) % 2][:, 0, :], bank(2, SL), ACT.Relu).then_inc(f1_ca, 1)

        @block.vector
        def _(ve):
            steps = [0]

            def chain(ins):
                ins.then_inc(vstep, 1)
                steps[0] += 1
                ve.wait_ge(vstep, steps[0])

            ve.memset(onebf[:, :], 1.0).then_inc(set_v, 1)
            ve.wait_ge(cst_in, 32)
            ve.tensor_copy(ibf[:, :], ident).then_inc(set_v, 1)
            ve.tensor_copy(tribf[:, :], tri).then_inc(set_v, 1)
            ve.tensor_copy(mbf[:, :].rearrange("p (h j) -> p h j", h=NH),
                           cmask.unsqueeze(1).broadcast_to([128, NH, 64])).then_inc(set_v, 1)
            for i in range(6):
                ve.wait_ge(wt_done, i + 1)
                ve.tensor_copy(wt[i // 2][:, 4 * (i % 2):4 * (i % 2) + 4, :],
                               bank(i, 4 * L, D).rearrange("p (h l) -> p h l", h=4)).then_inc(wt_cp, 1)
            for i in range(2):
                ve.wait_ge(mn_done, i + 1)
                ve.tensor_copy(mm_[:, 4 * i:4 * i + 4, :],
                               bank(6 + i, 4 * L, L).rearrange("p (h l) -> p h l", h=4)).then_inc(mn_cp, 1)
            ve.wait_ge(mn_done, 3)
            ve.tensor_copy(nn_[:, :, :, :].rearrange("p a h d -> p h a d"),
                           bank(0, 512, L).rearrange("p (h a d) -> p h a d", a=2, d=D)).then_inc(mn_cp, 1)
            ve.wait_ge(pos_done, 1)
            ve.tensor_copy(posb[:, :], bank(2, D, NPOS)).then_inc(pos_cp, 1)
            ve.wait_ge(bt_done, 1)
            ve.tensor_copy(bc[:, :, :], bank(3, 128).rearrange("p (a h) -> p a h", a=4)).then_inc(bt_cp, 1)
            ve.wait_ge(bt_cp, 1)

            ve.wait_ge(s4_in, 16 * N_S4)
            u_re, u_im = bc[:, 0, :], bc[:, 1, :]
            x_re, x_im = bc[:, 2, :], bc[:, 3, :]
            pc, qc = (pri[:, 0:1], pri[:, 1:2]), (qri[:, 0:1], qri[:, 1:2])
            t0, t1 = wtmp[:, 0, :], wtmp[:, 1, :]
            chain(ve.tensor_tensor(t0, x_im, u_im, ALU.mult))
            chain(ve.tensor_tensor(t1, x_re, u_re, ALU.mult))
            chain(ve.tensor_tensor(wc[:, 0, 0], t0, t1, ALU.add))
            chain(ve.tensor_tensor(t0, x_im, u_re, ALU.mult))
            chain(ve.tensor_tensor(t1, x_re, u_im, ALU.mult))
            chain(ve.tensor_tensor(wc[:, 0, 1], t1, t0, ALU.subtract))
            chain(ve.tensor_scalar(t0, x_im, pc[1], None, ALU.mult))
            chain(ve.scalar_tensor_tensor(wc[:, 1, 0], x_re, pc[0], t0, ALU.mult, ALU.add))
            chain(ve.tensor_scalar(t0, x_im, pc[0], None, ALU.mult))
            chain(ve.scalar_tensor_tensor(wc[:, 1, 1], x_re, pc[1], t0, ALU.mult, ALU.subtract))
            chain(ve.tensor_scalar(t0, u_im, qc[1], None, ALU.mult))
            chain(ve.scalar_tensor_tensor(wc[:, 2, 0], u_re, qc[0], t0, ALU.mult, ALU.add))
            chain(ve.tensor_scalar(t0, u_re, qc[1], None, ALU.mult))
            chain(ve.scalar_tensor_tensor(wc[:, 2, 1], u_im, qc[0], t0, ALU.mult, ALU.subtract))
            chain(ve.tensor_scalar(ws[:, 0:2], qri[:, :], pc[1], None, ALU.mult))
            chain(ve.tensor_scalar(ws[:, 2:4], qri[:, :], pc[0], None, ALU.mult))
            chain(ve.tensor_tensor(ws[:, 4:5], ws[:, 2:3], ws[:, 1:2], ALU.add))
            chain(ve.tensor_tensor(ws[:, 5:6], ws[:, 0:1], ws[:, 3:4], ALU.subtract))
            chain(ve.tensor_copy(wc[:, 3], ws[:, 4:6].unsqueeze(2).broadcast_to([128, 2, 32])))
            chain(ve.tensor_scalar(ws[:, 0:2], lam[:, :], RSC, None, ALU.mult))
            chain(ve.tensor_tensor(ws[:, 2:3], ws[:, 0:1], ws[:, 0:1], ALU.mult))
            chain(ve.tensor_scalar(ws[:, 3:4], ws[:, 0:1], -RSC, None, ALU.mult))
            ve.wait_ge(set_p, N_SET_P)
            for q in range(2):
                r = slice(D * q, D * q + D)
                dst_a = va[r, :, q, :].rearrange("p h c -> p c h")
                dst_b = vb[r, :, q, :].rearrange("p h (x c) -> p c x h", c=2)
                w_all = wc[r].rearrange("p x c h -> p (x c) h")
                ve.tensor_scalar(dst_a, w_all, ws[r, 3:4], None, ALU.mult).then_inc(vab_ok, 1)
                ve.tensor_scalar(dst_b[:, 0], wc[r, :, 1], -RSC, None, ALU.mult).then_inc(vab_ok, 1)
                ve.tensor_scalar(dst_b[:, 1], wc[r, :, 0], RSC, None, ALU.mult).then_inc(vab_ok, 1)
            ve.wait_ge(g_outer, 1)
            ve.tensor_scalar(g_w, g_w, ws[:, 1:2], None, ALU.add).then_inc(g_shift, 1)
            ve.wait_ge(g_sq, 1)
            ve.tensor_scalar(g_inv, g_inv, ws[:, 2:3], None, ALU.add).then_inc(g_den, 1)
            ve.wait_ge(g_den, 1)
            ve.reciprocal(g_inv, g_inv).then_inc(g_recip, 1)

            def mean(i):
                ve.tensor_reduce(st[:, 0, i, :], grp(hh, i % G), X, ALU.add).then_inc(ln_sum, 1)
                ve.wait_ge(ln_sum, i + 1)
                ve.tensor_scalar(st[:, 1, i, :], st[:, 0, i, :], 1.0 / D, None, ALU.mult).then_inc(ln_mean, 1)
                ve.wait_ge(ln_mean, i + 1)
                ve.tensor_tensor(grp(uu, i % G), grp(hh, i % G),
                                 st[:, 1, i, :].unsqueeze(2).broadcast_to([L, GB, D]), ALU.subtract).then_inc(ln_cen, 1)

            def var(i):
                ve.wait_ge(ln_sq, i + 1)
                ve.tensor_reduce(st[:, 0, i, :], sq[:, i % 2, :].rearrange("p (b d) -> p b d", b=GB), X,
                                 ALU.add).then_inc(ln_var, 1)
                ve.wait_ge(ln_var, i + 1)
                ve.tensor_scalar(st[:, 2, i, :], st[:, 0, i, :], 1.0 / D, LN_EPS, ALU.mult, ALU.add).then_inc(ln_vs, 1)

            def scale(i):
                ve.wait_ge(ln_pow, i + 1)
                ve.tensor_tensor(grp(uu, i % G), grp(uu, i % G),
                                 st[:, 3, i, :].unsqueeze(2).broadcast_to([L, GB, D]), ALU.mult).then_inc(ln_u, 1)

            def rearranged(c):
                ve.wait_ge(x_in[c], 16)
                if c >= 2:
                    ve.wait_ge(xt_done, 4 * (c - 1))
                for k in range(2):
                    ve.tensor_copy(xr[c % 2][:, k].rearrange("p g (y x) -> p g y x", y=8),
                                   ximg[:, c % NX, 8 * k:8 * k + 8, :].rearrange("p y (g x) -> p g y x", g=NG)
                                   ).then_inc(xr_ok, 1)

            def patches(r):
                ve.wait_ge(xt_done, r + 1)
                move_patches(ve, r).then_inc(xt_cv, 1)

            def tokens(g):
                ve.wait_ge(lt_done, g + 1)
                if g == 0:
                    ve.wait_ge(pos_cp, 1)
                    ve.wait_ge(cls_in, 32)
                ve.tensor_tensor(grp(hh[0:NPOS], g), bank(5, 512, NPOS).rearrange("p (b d) -> p b d", b=GB),
                                 posb[:, :].unsqueeze(1).broadcast_to([NPOS, GB, D]), ALU.add).then_inc(h0_ok, 1)
                ve.wait_ge(h0_ok, g + 1)

            def half(i):
                rearranged(3 * i)
                for c in range(3 * i, 3 * i + 3):
                    if c + 1 < 3 * i + 3:
                        rearranged(c + 1)
                    patches(4 * c)
                    patches(4 * c + 2)
                g0 = 2 * i
                tokens(g0)
                mean(g0)
                tokens(g0 + 1)
                mean(g0 + 1)
                var(g0)
                var(g0 + 1)
                scale(g0)
                scale(g0 + 1)

            half(0)

            ve.wait_ge(kk_done, 1)
            chain(ve.tensor_copy(ks[:, :, :].rearrange("p c (a h) -> p c a h", a=2),
                                 bank(6, 512, L).rearrange("p (h a c) -> p c a h", a=2, c=8)))
            k_ = [ks[:, i, :] for i in range(8)]
            a_ = [kt_[:, i, :] for i in range(10)]

            def tt(dst, x, y, op):
                chain(ve.tensor_tensor(dst, x, y, op))

            tt(a_[0], k_[2], k_[4], ALU.mult)
            tt(a_[1], k_[3], k_[5], ALU.mult)
            tt(a_[0], a_[0], a_[1], ALU.subtract)
            tt(a_[1], k_[2], k_[5], ALU.mult)
            tt(a_[2], k_[3], k_[4], ALU.mult)
            tt(a_[1], a_[1], a_[2], ALU.add)
            chain(ve.tensor_scalar(a_[2], k_[6], 1.0, None, ALU.add))
            tt(a_[3], a_[2], a_[2], ALU.mult)
            tt(a_[4], k_[7], k_[7], ALU.mult)
            tt(a_[3], a_[3], a_[4], ALU.add)
            chain(ve.reciprocal(a_[4], a_[3]))
            tt(a_[5], a_[0], a_[2], ALU.mult)
            tt(a_[6], a_[1], k_[7], ALU.mult)
            tt(a_[5], a_[5], a_[6], ALU.add)
            tt(a_[5], a_[5], a_[4], ALU.mult)
            tt(a_[6], a_[1], a_[2], ALU.mult)
            tt(a_[7], a_[0], k_[7], ALU.mult)
            tt(a_[6], a_[6], a_[7], ALU.subtract)
            tt(a_[6], a_[6], a_[4], ALU.mult)
            tt(a_[5], k_[0], a_[5], ALU.subtract)
            tt(a_[6], k_[1], a_[6], ALU.subtract)
            chain(ve.scalar_tensor_tensor(a_[8], a_[6], tau, a_[5], ALU.mult, ALU.add))
            chain(ve.tensor_scalar(a_[7], a_[5], tau, None, ALU.mult))
            ve.tensor_tensor(a_[9], a_[6], a_[7], ALU.subtract).then_inc(at_ok, 1)

            half(1)

            ve.wait_ge(kx_done, 1)
            chain(ve.tensor_copy(kx[:, :], bank(7, KW, D)))
            chain(ve.tensor_scalar(kx[:, D:D + 1], kx[:, D:D + 1], dcol[:, 0:1], None, ALU.add))
            ve.tensor_scalar(kx[:, KW - 1:KW], kx[:, KW - 1:KW], dcol[:, 0:1], None, ALU.add).then_inc(kx_ok, 1)
            ve.wait_ge(emb_done, G)
            ve.memset(toep[0:D, :, D:L], 0.0).then_inc(t_zero, 1)

            ve.wait_ge(bn_done, 1)
            ve.tensor_copy(bn[:, :, :], bank(7, 40).rearrange("p (a e) -> p a e", a=10)).then_inc(bn_cp, 1)
            ve.wait_ge(bn_cp, 1)
            for i in range(2):
                ve.tensor_scalar(bn[:, 5 * i], bn[:, 5 * i], BN_EPS, None, ALU.add).then_inc(bn_cp, 1)
            ve.wait_ge(bn_pow, 2)
            for i in range(2):
                chain(ve.tensor_tensor(bna[:, 2 * i], bna[:, 2 * i], bn[:, 5 * i + 1], ALU.mult))
                chain(ve.tensor_tensor(bna[:, 2 * i + 1], bn[:, 5 * i + 2], bn[:, 5 * i + 3], ALU.subtract))
                chain(ve.tensor_tensor(bna[:, 2 * i + 1], bna[:, 2 * i + 1], bna[:, 2 * i], ALU.mult))
                ve.tensor_tensor(bna[:, 2 * i + 1], bna[:, 2 * i + 1], bn[:, 5 * i + 4], ALU.add).then_inc(bn_ok, 1)

            def rowmax(p):
                ve.wait_ge(s_done, p + 1)
                ve.tensor_reduce(mx[:, p % 2], bank(3 + p % 2).rearrange("p (h j) -> p h j", h=NH), X,
                                 ALU.max).then_inc(mx_ok, 1)
                if p >= 2:
                    ve.wait_ge(p_ok, p - 1)
                ve.wait_ge(mx_ok, p + 1)
                ve.tensor_tensor(sx[p % 2].rearrange("p (h j) -> p h j", h=NH),
                                 bank(3 + p % 2).rearrange("p (h j) -> p h j", h=NH),
                                 mx[:, p % 2].unsqueeze(2).broadcast_to([128, NH, 64]), ALU.subtract).then_inc(sub_ok, 1)

            def rowsum(p):
                ve.wait_ge(exp_ok, p + 1)
                ve.tensor_reduce(mx[:, p % 2], sx[p % 2].rearrange("p (h j) -> p h j", h=NH), X,
                                 ALU.add).then_inc(sum_ok, 1)
                ve.wait_ge(sum_ok, p + 1)
                ve.reciprocal(rc[:, p % 2], mx[:, p % 2]).then_inc(rc_ok, 1)

            def attended(g):
                ve.wait_ge(pv_done, GB * (g + 1))
                ve.wait_ge(bu_add, g + 1)
                ve.tensor_tensor(grp(hh[0:NPOS], g), grp(hh[0:NPOS], g),
                                 bank(7, 512, NPOS).rearrange("p (b d) -> p b d", b=GB), ALU.add).then_inc(o_add, 1)
                ve.wait_ge(o_add, g + 1)

            for p in range(PAIRS + 4):
                if p < PAIRS:
                    rowmax(p)
                if 1 <= p <= PAIRS:
                    rowsum(p - 1)
                if p >= 5 and (p - 5) % 4 == 0:
                    g = (p - 5) // 4
                    attended(g)
                    mean(G + g)
                if p >= 6 and (p - 6) % 4 == 0:
                    var(G + (p - 6) // 4)
                if p >= 7 and (p - 7) % 4 == 0:
                    scale(G + (p - 7) // 4)

            ve.wait_ge(ut_cp, 4 * G)
            chain(ve.tensor_reduce(feat[:, :], ut[:, :, :].rearrange("p b l -> p l b"), X, ALU.add))
            ve.tensor_scalar(feat[:, :], feat[:, :], 1.0 / B, None, ALU.mult).then_inc(ft_ok, 1)
            ve.wait_ge(lg_done, 1)
            ve.tensor_reduce(rt[:, 0:1], bank(6, NE, L), X, ALU.max, negate=True).then_inc(rt_exp, 1)
            ve.wait_ge(rt_exp, 2)
            chain(ve.reciprocal(rt[:, 2:3], rt[:, 1:2]))
            ve.tensor_scalar(rt[:, 16:24], rt[:, 8:16], rt[:, 2:3], None, ALU.mult).then_inc(w_ok, 1)
            ve.wait_ge(wtt_done, 1)
            ve.tensor_copy(wtt[:, :], bank(6, L, NE)).then_inc(wtt_cp, 1)
            ve.wait_ge(wb_done, 1)
            ve.tensor_copy(wb[:, :, :], bank(7, EP * L).rearrange("p (a l) -> p a l", a=EP)).then_inc(wb_cp, 1)
            ve.tensor_copy(bow[:, :], bank(7, D, L, EP * L)).then_inc(wb_cp, 1)

            def weigh(k):
                ve.wait_ge(r2_ok, k + 1)
                if k >= 2:
                    ve.wait_ge(l3_step, k - 1)
                if k == 0:
                    ve.wait_ge(wb_cp, 2)
                nb = BCH[k // EP][1]
                ve.tensor_tensor(h2w[k % 2][:, 0:nb * L].rearrange("p (b l) -> p b l", b=nb),
                                 h2[k % 2][:, 0:nb * L].rearrange("p (b l) -> p b l", b=nb),
                                 wb[:, k % EP].unsqueeze(1).broadcast_to([128, nb, L]), ALU.mult).then_inc(wm_ok, 1)

            def fed(c):
                b0, nb = BCH[c]
                ve.wait_ge(yt_done, c + 1)
                if c == 0:
                    ve.wait_ge(bow_add, G)
                ve.tensor_tensor(hh[:, b0:b0 + nb], hh[:, b0:b0 + nb],
                                 bank(6 + c % 2, nb * D, L).rearrange("p (b d) -> p b d", b=nb),
                                 ALU.add).then_inc(y_add, 1)

            for k in range(EP * len(BCH) + 4):
                if k < EP * len(BCH):
                    weigh(k)
                if k >= 3 and (k - 3) % EP == EP - 1:
                    fed((k - 3) // EP)
            ve.wait_ge(y_add, len(BCH))

            def layer_norm(n):
                mean(G * n)
                mean(G * n + 1)
                var(G * n)
                mean(G * n + 2)
                scale(G * n)
                var(G * n + 1)
                mean(G * n + 3)
                scale(G * n + 1)
                var(G * n + 2)
                var(G * n + 3)
                scale(G * n + 2)
                scale(G * n + 3)

            ve.memset(xe[D:L, :, :], 1.0).then_inc(xe_one, 1)
            layer_norm(2)
            for q in range(4):
                ve.wait_ge(cv_done, q + 1)
                ve.tensor_tensor(hh[:, :, 16 * q:16 * q + 16], hh[:, :, 16 * q:16 * q + 16],
                                 bank(q, 512, L).rearrange("p (h b) -> p b h", h=16), ALU.add).then_inc(cv_add, 1)
            ve.wait_ge(cv_add, 4)
            layer_norm(3)

            def be(x):
                return x.rearrange("p (b e) -> p b e", e=NE)

            def eb(x):
                return x.rearrange("p (e b) -> p b e", b=B)

            def over(x):
                return x.unsqueeze(2).broadcast_to([L, B, NE])

            gt = [ra[:, i, :] for i in range(6)]
            gb_ = [rb[:, i, :] for i in range(12)]
            ve.wait_ge(gt_done, 1)
            ve.wait_ge(moe_in, 16 * 7)
            chain(ve.tensor_reduce(gb_[0], be(bank(6, 256, L)), X, ALU.max))
            ve.tensor_tensor(be(gt[0]), be(bank(6, 256, L)), over(gb_[0]), ALU.subtract).then_inc(gt_sub, 1)
            ve.wait_ge(gt_exp, 1)
            chain(ve.tensor_reduce(gb_[1], be(gt[0]), X, ALU.add))
            chain(ve.reciprocal(gb_[2], gb_[1]))
            chain(ve.tensor_tensor(be(gt[1]), be(gt[0]), over(gb_[2]), ALU.mult))
            chain(ve.tensor_reduce(gb_[3], be(gt[1]), X, ALU.max))
            chain(ve.tensor_tensor(be(gt[2]), be(gt[1]), over(gb_[3]), ALU.is_equal))
            chain(ve.tensor_tensor(be(gt[2]), be(gt[2]), eb(first), ALU.mult))
            chain(ve.tensor_reduce(gb_[4], be(gt[2]), X, ALU.max))
            chain(ve.tensor_tensor(eb(gt[3]), be(gt[2]), over(gb_[4]), ALU.is_equal))
            ve.tensor_copy(ohb[:, :], gt[3]).then_inc(oh_ok, 1)
            chain(ve.tensor_tensor(gt[4], gt[3], ebase, ALU.mult))
            chain(ve.tensor_reduce(gb_[5], eb(gt[4]), X, ALU.add))
            ve.wait_ge(pre_done, 2)
            chain(ve.tensor_copy(gt[4], bank(1, 256, L)))
            chain(ve.tensor_tensor_scan(gt[5], chained, gt[4], 0.0, ALU.mult, ALU.add))
            chain(ve.tensor_tensor(gt[5], gt[5], gt[4], ALU.subtract))
            chain(ve.tensor_tensor(gt[5], gt[5], bank(0, 256, L), ALU.add))
            chain(ve.tensor_tensor(gt[5], gt[5], gt[3], ALU.mult))
            chain(ve.tensor_reduce(gb_[6], eb(gt[5]), X, ALU.add))
            chain(ve.tensor_scalar(gb_[7], gb_[6], float(CAP) + 0.5, DROP, ALU.is_gt, ALU.mult))
            chain(ve.tensor_tensor(gb_[8], gb_[6], gb_[7], ALU.add))
            chain(ve.tensor_tensor(gb_[8], gb_[8], gb_[5], ALU.add))
            ve.tensor_scalar(idxs[:, :], gb_[8], -1.0, None, ALU.add).then_inc(idx_ok, 1)
            chain(ve.tensor_scalar(gb_[9], gb_[6], float(CAP), -1.0, ALU.min, ALU.add))
            ve.tensor_tensor(idxg[:, :], gb_[9], gb_[5], ALU.add).then_inc(idx_ok, 1)
            chain(ve.tensor_scalar(gb_[10], gb_[6], float(CAP) + 0.5, None, ALU.is_lt))
            chain(ve.tensor_tensor(gb_[11], gb_[10], gb_[3], ALU.mult))

            for e in range(NE + 1):
                if e < NE:
                    ve.wait_ge(f1_done, 2 * e + 2)
                    if e >= 2:
                        ve.wait_ge(f2_done, e - 1)
                    ve.tensor_scalar(hm[e % 2][:, 1, :], bank(3, SL), 0.0, None, ALU.max).then_inc(f1_cv, 1)
                if e >= 1:
                    ve.wait_ge(f2_done, e)
                    q = e - 1
                    ve.tensor_tensor(yb[:, SC * q:SC * q + SC, :],
                                     bank(4 + q % 2, SC * D).rearrange("p (c d) -> p c d", d=D),
                                     b2e[:, q].unsqueeze(1).broadcast_to([128, SC, D]), ALU.add).then_inc(yb_ok, 1)
            for g in range(G):
                ve.wait_ge(yg_in[g], 16 * GB)
                y = grp(yg, g)
                r1, r2 = (scr[:, i, :].rearrange("p (b d) -> p b d", b=GB) for i in range(2))
                ok = fin[:, :].rearrange("p (b d) -> p b d", b=GB)
                chain(ve.tensor_tensor(y, y, gb_[11][:, GB * g:GB * g + GB].unsqueeze(2).broadcast_to([L, GB, D]),
                                       ALU.mult))
                chain(ve.tensor_scalar(ok, y, 0.0, 0.0, ALU.mult, ALU.is_equal))
                chain(ve.tensor_scalar(r1, y, 0.0, 1.0e4, ALU.is_gt, ALU.mult))
                chain(ve.tensor_scalar(r2, y, 0.0, -1.0e4, ALU.is_lt, ALU.mult))
                chain(ve.tensor_tensor(r1, r1, r2, ALU.add))
                chain(ve.copy_predicated(r1, ok, y))
                ve.tensor_tensor(grp(hh, g), grp(hh, g), r1, ALU.add).then_inc(fin_ok, 1)

        @block.tensor
        def _(pe):
            pe.wait_ge(cst_in, 32)
            pe.wait_ge(qkv_in, 16 * 7)
            for i in range(6):
                for j in range(4):
                    h = 4 * (i % 2) + j
                    m = pe.transpose(bank(i, L, D, L * j), wqkv[i // 2][:, D * h:D * h + D], ident[0:L, 0:L])
                m.then_inc(wt_done, 1)
            pe.wait_ge(wt_cp, 4)
            for h in range(NH):
                m = pe.matmul(bank(6 + h // 4, L, L, L * (h % 4)), wt[1][:, h, :], wt[0][:, h, :], start=True, stop=True)
                if h % 4 == 3:
                    m.then_inc(mn_done, 1)
            pe.wait_ge(wt_cp, 6)
            for h in range(NH):
                m = pe.matmul(bank(0, D, L, D * h), wt[2][:, h, :], wu[:, h, :], start=True, stop=True)
            m.then_inc(mn_done, 1)
            pe.wait_ge(tok_in, 16 * 6)
            pe.wait_ge(set_p, N_SET_P)
            pe.matmul(bank(1, NPOS, D), w1t[:, :], cxy[:, :], start=True, stop=True).then_inc(r_done, 1)
            pe.wait_ge(r_cp, 1)
            pe.matmul(bank(2, D, NPOS), rr[:, :], w2t[:, :], start=True, stop=False)
            pe.matmul(bank(2, D, NPOS), ones[:, :], bpt[:, :], start=False, stop=True).then_inc(pos_done, 1)
            pe.wait_ge(s4_in, 16 * N_S4)
            for i in range(4):
                m = pe.transpose(bank(3, 32, 128, 32 * i),
                                 bct[:, i // 2, :, :, i % 2].rearrange("p a n -> p (a n)"), ident[0:32, 0:32])
            m.then_inc(bt_done, 1)
            pe.wait_ge(bt_cp, 1)
            pe.wait_ge(pos_cp, 1)
            pe.wait_ge(mn_cp, 3)
            pe.wait_ge(wp_in, 16)

            def turn_patches(c):
                for k in range(2):
                    pe.wait_ge(xr_ok, 2 * c + k + 1)
                    for g in range(2):
                        r = 4 * c + 2 * k + g
                        if r >= 4:
                            pe.wait_ge(xt_ca if g else xt_cv, (r - 4) // 2 + 1)
                        for x in range(4):
                            m = pe.transpose(bank(r % 4, 128, 128, 128 * x), xr[c % 2][:, k, 4 * g + x, :], ident)
                        m.then_inc(xt_done, 1)

            def embed(g):
                pe.wait_ge(xt_cv, 6 * (g // 2) + 6)
                pe.wait_ge(xt_ca, 6 * (g // 2) + 6)
                if g >= 1:
                    pe.wait_ge(et_cp, g)
                b0 = GB * (g % 2)
                for k in range(KT):
                    m = pe.matmul(bank(4, 512, D), wp[:, k, :],
                                  xt[:, k, b0:b0 + GB].rearrange("p b y x -> p (b y x)"),
                                  start=(k == 0), stop=(k == KT - 1))
                m.then_inc(emb_done, 1)

            def turn_tokens(g):
                pe.wait_ge(et_cp, g + 1)
                if g >= 1:
                    pe.wait_ge(h0_ok, g)
                for b in range(GB):
                    m = pe.transpose(bank(5, D, NPOS, D * b), et[:, g % 2, NPOS * b:NPOS * b + NPOS], ident[0:D, 0:D])
                m.then_inc(lt_done, 1)

            def half(i):
                for c in range(3 * i, 3 * i + 3):
                    turn_patches(c)
                g = 2 * i
                embed(g)
                turn_tokens(g)
                embed(g + 1)
                turn_tokens(g + 1)

            def turn_norm(i):
                pe.wait_ge(ln_u, i + 1)
                for q in range(2):
                    for j in range(4):
                        m = pe.transpose(bank(q, L, D, L * j), uu[:, GB * (i % G) + 4 * q + j, :], ident[0:L, 0:L])
                    m.then_inc(ut_done, 1)

            def prep(g):
                if g == 0:
                    pe.wait_ge(xt_cv, 6)
                    pe.wait_ge(xt_ca, 6)
                if g == 2:
                    pe.wait_ge(xt_cv, 12)
                    pe.wait_ge(xt_ca, 12)
                if g >= 1:
                    pe.wait_ge(z_cp, NH * g)
                turn_norm(g)
                pe.wait_ge(ut_cp, 2 * g + 2)
                for h in range(NH):
                    if h >= 2:
                        pe.wait_ge(z_cp, NH * g + h - 1)
                    pe.matmul(bank(h % 2, 512, L), mm_[:, h, :], grp(ut, g)[:, :, 0:D],
                              start=True, stop=True).then_inc(z_done, 1)
                    if h % 2:
                        q = h // 2
                        if 4 * g + q >= 1:
                            pe.wait_ge(v_cp, 4 * g + q)
                        for b in range(2):
                            for a in range(2):
                                m = pe.matmul(ps[D * a:D * a + D, 2, 256 * b:256 * b + 256],
                                              ut[:, GB * g + 2 * q + b, 0:D],
                                              nn_[:, a].rearrange("p h d -> p (h d)"), start=True, stop=True)
                        m.then_inc(v_done, 1)

            half(0)
            prep(0)
            prep(1)
            pe.wait_ge(vab_ok, 6)
            pe.wait_ge(g_prod, 1)
            for h in range(32):
                pe.matmul(bank(6, 16, L, 16 * h), g_inv[:, h, :], va[:, h].rearrange("p a c -> p (a c)"),
                          start=True, stop=False)
                m = pe.matmul(bank(6, 16, L, 16 * h), g_winv[:, h, :], vb[:, h].rearrange("p a c -> p (a c)"),
                              start=False, stop=True)
            m.then_inc(kk_done, 1)
            pe.wait_ge(z_cp, 2 * NH)
            pe.wait_ge(v_cp, 8)
            half(1)
            pe.wait_ge(at_ok, 1)
            pe.matmul(bank(7, KW, D), kt_[:, 8, :], cosx, start=True, stop=False)
            pe.matmul(bank(7, KW, D), kt_[:, 9, :], sinx, start=False, stop=True).then_inc(kx_done, 1)
            pe.wait_ge(kx_ok, 1)
            pe.wait_ge(bn_in, 160)
            pe.transpose(bank(7, 40), bnr[:, :], ident[0:40, 0:40]).then_inc(bn_done, 1)
            prep(2)
            prep(3)
            pe.wait_ge(bn_cp, 1)

            pe.wait_ge(set_v, 4)

            def scores(p):
                if p >= 2:
                    pe.wait_ge(sub_ok, p - 1)
                pe.wait_ge(z_cp, NH * (p // 4) + NH)
                pe.matmul(bank(3 + p % 2), ibf[:, :], mbf[:, :], start=True, stop=False, skip_group_check=True)
                for a in range(2):
                    b = 2 * p + a
                    m = pe.matmul(ps[D * a:D * a + D, 3 + p % 2, :], ut[:, b, 1:L],
                                  zz[b // GB][:, b % GB].rearrange("p h j -> p (h j)"),
                                  start=False, stop=True, skip_group_check=True)
                m.then_inc(s_done, 1)

            def turn_probs(p):
                pe.wait_ge(p_ok, p + 1)
                if p >= 2:
                    pe.wait_ge(pt_cp, p - 1)
                for j in range(4):
                    m = pe.transpose(bank(5 + p % 2, 128, 128, 128 * j), pp[p % 2][:, 128 * j:128 * j + 128], ident)
                m.then_inc(pt_done, 1)

            def attend(p):
                pe.wait_ge(pt_cp, p + 1)
                pe.wait_ge(v_cp, p + 1)
                if p % 4 == 0 and p:
                    pe.wait_ge(o_add, p // 4)
                for a in range(2):
                    b = 2 * p + a
                    for j in range(4):
                        m = pe.matmul(bank(7, D, NPOS, D * (b % GB)), pt[p % 2][:, 128 * j + D * a:128 * j + D * a + D],
                                      vv[:, b, j, :], start=(j == 0), stop=(j == 3))
                    m.then_inc(pv_done, 1)

            for p in range(PAIRS + 2):
                if p < PAIRS:
                    scores(p)
                if 1 <= p <= PAIRS:
                    turn_probs(p - 1)
                    if p == 1:
                        pass
                if p >= 2:
                    attend(p - 2)
            for g in range(G):
                if g:
                    pe.wait_ge(ut_cp, 2 * (G + g))
                turn_norm(G + g)
            pe.wait_ge(ft_ok, 1)
            pe.wait_ge(ffn_in, 16 * N_FFN)
            pe.matmul(bank(6, NE, L), feat[:, :], wra[:, :], start=True, stop=True).then_inc(lg_done, 1)
            pe.wait_ge(w_ok, 1)
            pe.transpose(bank(6, L, NE), rt[:, 16:24], ident[0:L, 0:L]).then_inc(wtt_done, 1)
            pe.wait_ge(wtt_cp, 1)
            pe.wait_ge(o_add, G)
            for a in range(EP):
                pe.matmul(bank(7, L, 128, L * a), csel[:, 128 * a:128 * a + 128], wtt[:, :], start=True, stop=True)
            pe.matmul(bank(7, D, L, EP * L), wtt[:, :], bof[:, :], start=True, stop=True).then_inc(wb_done, 1)

            def layer1(k):
                if k >= 2:
                    pe.wait_ge(r1_ok, k - 1)
                b0, nb = BCH[k // EP]
                a = k % EP
                pe.matmul(bank(k % 2, nb * L), w1r[:, 2 * a:2 * a + 2, :].rearrange("p e h -> p (e h)"),
                          ut[0:D, b0:b0 + nb].rearrange("p b l -> p (b l)"), start=True, stop=True).then_inc(l1_done, 1)

            def layer2(k):
                pe.wait_ge(r1_ok, k + 1)
                if k >= 2:
                    pe.wait_ge(r2_ok, k - 1)
                n = BCH[k // EP][1] * L
                pe.matmul(bank(2 + k % 2, n), w2f[:, k % EP, :], h1[k % 2][:, 0:n],
                          start=True, stop=True).then_inc(l2_done, 1)

            def layer3(k):
                pe.wait_ge(wm_ok, k + 1)
                c, a = k // EP, k % EP
                if a == 0 and c >= 2:
                    pe.wait_ge(y3_cp, c - 1)
                n = BCH[c][1] * L
                m = pe.matmul(bank(4 + c % 2, n, D), wof[:, a, :], h2w[k % 2][:, 0:n],
                              start=(a == 0), stop=(a == EP - 1))
                m.then_inc(l3_step, 1)

            def turn_mixed(c):
                pe.wait_ge(y3_cp, c + 1)
                if c >= 2:
                    pe.wait_ge(y_add, c - 1)
                if c == 1:
                    pe.wait_ge(wb_cp, 2)
                for b in range(BCH[c][1]):
                    m = pe.transpose(bank(6 + c % 2, D, L, D * b), y3[c % 2][:, L * b:L * b + L], ident[0:D, 0:D])
                m.then_inc(yt_done, 1)

            pe.wait_ge(bn_ok, 2)
            pe.wait_ge(ut_cp, 4 * G)
            for k in range(EP * len(BCH) + 4):
                if k < EP * len(BCH):
                    layer1(k)
                if 1 <= k <= EP * len(BCH):
                    layer2(k - 1)
                if 2 <= k <= EP * len(BCH) + 1:
                    layer3(k - 2)
                if k >= 3 and (k - 3) % EP == EP - 1:
                    turn_mixed((k - 3) // EP)

            pe.wait_ge(ln_u, 3 * G)
            pe.wait_ge(t_in, 16 * L)
            pe.wait_ge(t_zero, 1)
            pe.wait_ge(y3_cp, len(BCH))
            for h in range(D):
                m = pe.matmul(bank(h // 16, B, L, B * (h % 16)), toep[:, h, :], uu[:, :, h], start=True, stop=True)
                if h % 16 == 15:
                    m.then_inc(cv_done, 1)
            pe.wait_ge(cv_add, 4)
            for g in range(G):
                if g:
                    pe.wait_ge(ut_cp, 2 * (2 * G + g))
                pe.wait_ge(ln_u, 3 * G + g + 1)
                for q in range(2):
                    for j in range(4):
                        m = pe.transpose(bank(q, L, D, L * j), uu[:, GB * g + 4 * q + j, :], ident[0:L, 0:L])
                    m.then_inc(ut_done, 1)
            pe.wait_ge(ut_cp, 6 * G)
            pe.wait_ge(moe_in, 16 * 7)
            for b in range(B):
                m = pe.matmul(bank(6, NE, L, NE * b), ut[:, b, :], gwa[:, :], start=True, stop=True)
            m.then_inc(gt_done, 1)
            pe.wait_ge(oh_ok, 1)
            pe.matmul(bank(0, 256, L), tribf[:, :], ohb[:, :], start=True, stop=True).then_inc(pre_done, 1)
            pe.matmul(bank(1, 256, L), onebf[:, :], ohb[:, :], start=True, stop=True).then_inc(pre_done, 1)
            pe.wait_ge(idx_ok, 2)

            def turn_slots(e):
                pe.wait_ge(xb_in[e // (NE // 2)], 16)
                if e >= 2:
                    pe.wait_ge(xe_cp, e - 1)
                for c in range(SC):
                    m = pe.transpose(bank(e % 2, 128, D, 128 * c), xb[:, SC * e + c, :], ident)
                m.then_inc(xe_done, 1)

            def up(e):
                pe.wait_ge(xe_cp, e + 1)
                for f in range(2):
                    if e:
                        pe.wait_ge(f1_cv if f else f1_ca, e)
                    pe.matmul(bank(2 + f, SL), w1e[:, e, 128 * f:128 * f + 128], xe[:, e, :],
                              start=True, stop=True).then_inc(f1_done, 1)

            def down(e):
                pe.wait_ge(f1_ca, e + 1)
                pe.wait_ge(f1_cv, e + 1)
                if e >= 2:
                    pe.wait_ge(yb_ok, e - 1)
                for c in range(SC):
                    for f in range(2):
                        m = pe.matmul(bank(4 + e % 2, D, 128, D * c), hm[e % 2][:, f, 128 * c:128 * c + 128],
                                      w2e[:, e, f, :], start=(f == 0), stop=(f == 1))
                m.then_inc(f2_done, 1)

            for e in range(NE + 2):
                if e < NE:
                    turn_slots(e)
                if 1 <= e <= NE:
                    up(e - 1)
                if e >= 2:
                    down(e - 2)


NX = 5
N_S4, N_FFN, N_SET_P = 11, 8, 7

_INS = ["x", "cls_tok", "L0_tok_Wp", "L0_tok_bp", "L0_tok_W1", "L0_tok_b1", "L0_tok_W2", "L0_tok_b2",
        "L0_attn_Wq", "L0_attn_bq", "L0_attn_Wk", "L0_attn_bk", "L0_attn_Wv", "L0_attn_bv", "L0_attn_Wu",
        "L0_attn_bu", "L0_ffn_Wr", "L0_ffn_br", "L0_ffn_W1", "L0_ffn_b1", "L0_ffn_g1", "L0_ffn_be1",
        "L0_ffn_m1", "L0_ffn_v1", "L0_ffn_W2", "L0_ffn_b2", "L0_ffn_g2", "L0_ffn_be2", "L0_ffn_m2",
        "L0_ffn_v2", "L0_ffn_Wo", "L0_ffn_bo", "L1_attn_p_ri", "L1_attn_q_ri", "L1_attn_lambda_ri",
        "L1_attn_B_ri", "L1_attn_Ct_ri", "L1_attn_D", "L1_attn_log_step", "L1_ffn_gate_w",
        "L1_ffn_gate_b", "L1_ffn_w1", "L1_ffn_b1", "L1_ffn_w2", "L1_ffn_b2"]


def kernel(**inputs):
    import concourse.bacc as bacc
    from concourse.bass_utils import run_bass_kernel_spmd

    nc = bacc.Bacc("TRN2", target_bir_lowering=False, num_devices=1)
    arrays, tensors = {}, {}
    for name in _INS:
        arrays[f"in_{name}"] = np.ascontiguousarray(inputs[name])
    for name, table in shape_constants().items():
        arrays[f"in_{name}"] = table
    for key, a in arrays.items():
        tensors[key[3:]] = nc.dram_tensor(key, a.shape, mybir.dt.from_np(a.dtype), kind="ExternalInput").ap()
    out = nc.dram_tensor("out", (B, L, D), F32, kind="ExternalOutput").ap()
    build(nc, tensors, out)
    r = run_bass_kernel_spmd(nc, [arrays], core_ids=[0])
    return r.results[0]["out"]
```

```python
from contextlib import ExitStack

import numpy as np

import concourse.bass as bass
from concourse import mybir

B, CH, IMG, P = 32, 3, 128, 16
D = 64
NG = IMG // P
NPOS = NG * NG
L = NPOS + 1
KT = CH * P * P // 128
NH = 8
G = 4
GB = B // G
PAIRS = B // 2
NE = 8
EP = NE // 2
F = 256
CAP = -(-5 * B * L // (4 * NE))
SL = 384
SC = SL // 128
DROP = 1.0e6
LN_EPS, BN_EPS = 1e-5, 1e-3
RSC = 2.0 ** -24
KW = D + L + 1
BCH = [(0, 7), (7, 7), (14, 6), (20, 6), (26, 6)]

F32 = mybir.dt.float32
BF16 = mybir.dt.bfloat16
U32 = mybir.dt.uint32
ALU = mybir.AluOpType
ACT = mybir.ActivationFunctionType
X = mybir.AxisListType.X


def shape_constants():
    l = np.arange(L)
    tau = np.tan(np.pi * l / L)
    c128 = np.zeros((128, 128 + L + 64), np.float32)
    c128[:, :128] = np.eye(128)
    c128[:, 128:128 + L] = 2.0 * RSC * tau[None]
    i, j = np.arange(128)[:, None] % 64, np.arange(64)[None]
    c128[:, 128 + L:] = np.where(j <= i, 0.0, -1.0e30)
    k = np.concatenate([np.full(D, -1), np.arange(L), [0]])
    ang = 2 * np.pi * ((l[:, None] * np.maximum(k, 0)[None]) % L) / L
    used = (k >= 0)[None] / L
    pos = np.concatenate([np.arange(1, L), [0]])
    tri = (pos[:, None] <= pos[None]).astype(np.float64)
    base = np.repeat(np.arange(NE) * SL, B)
    chained = np.tile((np.arange(B) > 0) * 1.0, NE)
    first = np.tile(NE - np.arange(NE), B)
    cl = np.concatenate([np.cos(ang) * used, np.sin(ang) * used, tau[:, None], tri], axis=1)
    cr = np.tile(np.concatenate([base, chained, first]), (L, 1))
    n = np.arange(NPOS)
    xy = np.stack([n // NG / (NG - 1), n % NG / (NG - 1), np.ones(NPOS)])
    sel = np.zeros((NE, EP, 128))
    for e in range(NE):
        sel[e, e // 2, 64 * (e % 2):64 * (e % 2) + 64] = 1.0
    return {"c128": c128, "cl": cl.astype(np.float32), "cr": cr.astype(np.float32), "cxy": xy.astype(np.float32),
            "csel": sel.reshape(NE, EP * 128).astype(np.float32)}


def build(nc, t, out):
    kd = nc.dram_tensor("kernel_rows", (D, KW), F32, kind="Internal").ap()
    slots = nc.dram_tensor("expert_slots", (NE * SL, D), F32, kind="Internal").ap()
    yslots = nc.dram_tensor("expert_out", (NE * SL, D), F32, kind="Internal").ap()

    ctx = ExitStack()
    with ctx:
        def sb(name, shape, dt=F32):
            return ctx.enter_context(nc.sbuf_tensor(name, shape, dt))

        def sem(name):
            return ctx.enter_context(nc.semaphore(name))

        ps = ctx.enter_context(nc.psum_tensor("ps", [128, 8, 512], F32))

        rx = sb("rx", [128, NX * 2048])
        rxt = sb("rxt", [128, KT * 1024])
        rz = sb("rz", [128, 8192])
        rv = sb("rv", [128, 8192])
        rs = sb("rs", [128, 3 * 32 * L])

        ximg = rx[:, :].rearrange("p (c y x) -> p c y x", c=NX, y=P)
        xt = rxt[:, :].rearrange("p (k b y x) -> p k b y x", k=KT, y=NG, x=NG)
        et = rx[0:D, 2048:3072].rearrange("p (a n) -> p a n", a=2)
        zz = [r.rearrange("p (b h j) -> p b h j", b=GB, h=NH) for r in
              (rz[0:L, 0:4096], rz[0:L, 4096:8192], rx[0:L, 0:4096], rx[0:L, 4096:8192])]
        vv = rv[:, :].rearrange("p (b h d) -> p b h d", b=B, h=NH // 2)
        xr = [rv[:, 4096 + 2048 * i:6144 + 2048 * i].rearrange("p (k g n) -> p k g n", k=2, g=NG) for i in range(2)]
        g_w = rs[:, 0:32 * L].rearrange("p (h l) -> p h l", h=32)
        g_inv = rs[:, 32 * L:64 * L].rearrange("p (h l) -> p h l", h=32)
        g_winv = rs[:, 64 * L:96 * L].rearrange("p (h l) -> p h l", h=32)
        sx = [rxt[:, 4160 + 512 * i:4672 + 512 * i] for i in range(2)]
        pp = [rx[:, 8192 + 512 * i:8704 + 512 * i] for i in range(2)]
        pt = [rx[:, 9216 + 512 * i:9728 + 512 * i] for i in range(2)]
        toep = rxt[0:L, 0:D * L].rearrange("p (h l) -> p h l", h=D)
        h1 = [rv[:, 512 * i:512 * i + 512] for i in range(2)]
        h2 = [rv[:, 1024 + 512 * i:1536 + 512 * i] for i in range(EP)]
        h2w = [rv[:, 3072 + 512 * i:3584 + 512 * i] for i in range(2)]
        y3 = [rv[0:D, 4096 + 512 * i:4608 + 512 * i] for i in range(2)]
        xb = rv[:, 5120:5120 + NE * SC * D].rearrange("p (c d) -> p c d", d=D)
        yb = rv[:, 0:NE * SC * D].rearrange("p (c d) -> p c d", d=D)
        xe = rz[0:L, 0:NE * SL].rearrange("p (e s) -> p e s", e=NE)
        hm = [rz[:, 4096 + 768 * i:4864 + 768 * i].rearrange("p (f s) -> p f s", f=2) for i in range(2)]
        up = rx[:, 0:PAIRS * D].rearrange("p (c d) -> p c d", d=D)
        yg = rx[:, 1024:1024 + PAIRS * D].rearrange("p (c d) -> p c d", d=D)
        hp = rx[:, 2048:2048 + PAIRS * D].rearrange("p (c d) -> p c d", d=D)
        uc, yc, hc = (rx[0:B, 3072 + D * i:3072 + D * i + D] for i in range(3))
        r1_, r2_ = (rx[:, 3328 + 256 * i:3584 + 256 * i] for i in range(2))
        fin = rx[:, 3840:4096].bitcast(U32)
        w1e = rx[0:L, 8192:8192 + NE * F].rearrange("p (e f) -> p e f", e=NE)
        w2e = rxt[:, 4160:4160 + NE * 2 * D].rearrange("p (e f d) -> p e f d", e=NE, f=2)
        b2e = rxt[:, 5184:5184 + NE * D].rearrange("p (e d) -> p e d", e=NE)

        c128 = sb("c128_sb", [128, 128 + L + 64])
        ident, ttab, cmask = c128[:, 0:128], c128[:, 128:128 + L], c128[:, 128 + L:]
        cl = sb("cl_sb", [L, 2 * KW + 1 + L])
        cr = rs[0:L, 2048:2048 + 3 * NE * B]
        o = 2 * KW + 1
        cosx, sinx, tau, tri = cl[:, 0:KW], cl[:, KW:2 * KW], cl[:, o - 1:o], cl[:, o:o + L]
        ebase, chained, first = (cr[:, NE * B * i:NE * B * (i + 1)] for i in range(3))
        cxy = sb("cxy_sb", [3, NPOS])
        tribf = sb("tribf", [L, L], BF16)
        onebf = sb("onebf", [L, L], BF16)
        ones = sb("ones", [1, 64])
        expo = sb("expo", [128, 2 * GB])
        hh = sb("hh", [L, B, D])
        uu = sb("uu", [L, B, D])
        bst = sb("bst", [L, 4 * G, GB, 6])
        ut = sb("ut", [L, B, L])
        lsum, ldif, lsqd, lmean, lvs, lrs = (sb(n, [L, 4 * B, k]) for n, k in (
            ("lsum", 2), ("ldif", 1), ("lsqd", 1), ("lmean", 1), ("lvs", 1), ("lrs", 1)))
        wp = sb("wp", [128, KT, D])
        w1t, w2t, bpt = sb("w1t", [3, D]), sb("w2t", [L, D]), sb("bpt", [1, D])
        rr, posb = sb("rr", [L, NPOS]), sb("posb", [NPOS, D])
        wqkv = [rz[0:L, 512 * i:512 * i + 512] for i in range(3)]
        wu = rz[0:D, 1536:2048].rearrange("p (h d) -> p h d", h=NH)
        wt = [rz[0:D, 2048 + NH * L * i:2048 + NH * L * (i + 1)].rearrange("p (h l) -> p h l", h=NH) for i in range(3)]
        mm_ = sb("mm_", [L, NH, L])
        nn_ = sb("nn_", [L, 2, NH // 2, D])
        bub = sb("bub", [L, D])
        mx, rc = sb("mx", [128, 2, NH]), sb("rc", [128, 2, NH])
        lam, pri, qri = sb("lam", [128, 2]), sb("pri", [128, 2]), sb("qri", [128, 2])
        bct = rz[0:32, 3616:4128].rearrange("p (q a n r) -> p q a n r", q=2, a=2, r=2)
        bc = sb("bc", [128, 4, 32])
        lsb, gg = sb("lsb", [128, 32]), sb("gg", [128, 32])
        dcol = sb("dcol", [D, 1])
        ws = sb("ws", [128, 8])
        wc = sb("wc", [128, 4, 2, 32])
        wtmp = sb("wtmp", [128, 2, 32])
        zeros = sb("zeros", [128, 256])
        va, vb = sb("va", [128, 32, 2, 8]), sb("vb", [128, 32, 2, 8])
        ks = rs[0:L, 4864:4864 + 8 * D].rearrange("p (c h) -> p c h", c=8)
        kt_ = rs[0:L, 5376:5376 + 10 * D].rearrange("p (c h) -> p c h", c=10)
        kx = sb("kx", [D, KW])
        bnr = sb("bnr", [40, 128])
        bn = sb("bn", [128, 10, EP])
        bna = sb("bna", [128, 4, EP])
        wra = sb("wra", [L, NE])
        w1r = rs[0:D, 3072:3584].rearrange("p (e h) -> p e h", e=NE)
        w2f = rs[:, 3584:4096].rearrange("p (a k) -> p a k", a=EP)
        wof = rs[:, 4096:4352].rearrange("p (a d) -> p a d", a=EP)
        csel = rs[0:NE, 4352:4864]
        bof = sb("bof", [NE, D])
        feat, fpart = sb("feat", [L, L]), sb("fpart", [L, L, G])
        rt = sb("rt", [L, 40])
        wtt = sb("wtt", [NE, L])
        wb = sb("wb", [128, EP, L])
        bow = sb("bow", [L, D])
        gwa = sb("gwa", [L, NE])
        ra = rs[0:L, 0:1536].rearrange("p (a n) -> p a n", a=6)
        ohb = sb("ohb", [L, 256], BF16)
        rb = sb("rb", [L, 12, B])
        ixs, ixg = sb("ixs", [128, PAIRS], U32), sb("ixg", [128, PAIRS], U32)
        crow = sb("crow", [L, 2, B], U32)
        ics, icg, cc = sb("ics", [B, 1], U32), sb("icg", [B, 1], U32), sb("cc", [B, 1])
        cp_ = sb("cp_", [128, PAIRS])

        cl_in, ft_part = sem("cl_in"), sem("ft_part")
        cst_in, tok_in, qkv_in, s4_in, cls_in = (sem(n) for n in ("cst_in", "tok_in", "qkv_in", "s4_in", "cls_in"))
        bn_in, ffn_in, moe_in = sem("bn_in"), sem("ffn_in"), sem("moe_in")
        x_in = [sem(f"x_in{i}") for i in range(2 * CH)]
        wp_in = sem("wp_in")
        w2_zero = sem("w2_zero")
        set_v, set_p = sem("set_v"), sem("set_p")
        wt_done, wt_cp, mn_done, mn_cp = sem("wt_done"), sem("wt_cp"), sem("mn_done"), sem("mn_cp")
        r_done, r_cp, pos_done, pos_cp = sem("r_done"), sem("r_cp"), sem("pos_done"), sem("pos_cp")
        bt_done, bt_cp = sem("bt_done"), sem("bt_cp")
        bn_done, bn_cp, bn_pow, bn_ok = sem("bn_done"), sem("bn_cp"), sem("bn_pow"), sem("bn_ok")
        vstep = sem("vstep")
        g_exp, g_outer, g_shift, g_sq, g_recip, g_prod = (sem(n) for n in (
            "g_exp", "g_outer", "g_shift", "g_sq", "g_recip", "g_prod"))
        g_den, vab_ok, kk_done, kk_cp, at_ok, kx_done, kx_ok = (sem(n) for n in (
            "g_den", "vab_ok", "kk_done", "kk_cp", "at_ok", "kx_done", "kx_ok"))
        kd_out, t_in, t_zero = sem("kd_out"), sem("t_in"), sem("t_zero")
        xr_ok, xt_done, xt_cv, xt_ca = sem("xr_ok"), sem("xt_done"), sem("xt_cv"), sem("xt_ca")
        emb_done, et_cp, lt_done, h0_ok = sem("emb_done"), sem("et_cp"), sem("lt_done"), sem("h0_ok")
        ln_mean, ln_vs, ln_cen, ln_pow, ln_u = (sem(n) for n in ("ln_mean", "ln_vs", "ln_cen", "ln_pow", "ln_u"))
        ut_done, ut_cp = sem("ut_done"), sem("ut_cp")
        z_done, z_cp, v_done, v_cp = sem("z_done"), sem("z_cp"), sem("v_done"), sem("v_cp")
        s_done, msk_ok, mx_ok, sub_ok, exp_ok, sum_ok, rc_ok, p_ok = (sem(n) for n in (
            "s_done", "msk_ok", "mx_ok", "sub_ok", "exp_ok", "sum_ok", "rc_ok", "p_ok"))
        pt_done, pt_cp, pv_done, bu_add, o_add = (sem(n) for n in ("pt_done", "pt_cp", "pv_done", "bu_add", "o_add"))
        ft_ok, lg_done, rt_exp, w_ok, wtt_done, wtt_cp, wb_done, wb_cp, bow_add = (sem(n) for n in (
            "ft_ok", "lg_done", "rt_exp", "w_ok", "wtt_done", "wtt_cp", "wb_done", "wb_cp", "bow_add"))
        l1_done, r1_ok, l2_done, r2_ok, wm_ok, l3_step, y3_cp, yt_done, y_add = (sem(n) for n in (
            "l1_done", "r1_ok", "l2_done", "r2_ok", "wm_ok", "l3_step", "y3_cp", "yt_done", "y_add"))
        cv_done, cv_add = sem("cv_done"), sem("cv_add")
        gt_done, gt_sub, gt_exp, oh_ok, pre_done, idx_ok, co_ok = (sem(n) for n in (
            "gt_done", "gt_sub", "gt_exp", "oh_ok", "pre_done", "idx_ok", "co_ok"))
        z_out, sc_out, xe_one = sem("z_out"), sem("sc_out"), sem("xe_one")
        xb_in = [sem(f"xb_in{i}") for i in range(2)]
        xe_done, xe_cp, f1_done, f1_ca, f1_cv, f2_done, yb_ok, y_out = (sem(n) for n in (
            "xe_done", "xe_cp", "f1_done", "f1_ca", "f1_cv", "f2_done", "yb_ok", "y_out"))
        yg_in = [sem(f"yg_in{g}") for g in range(G)]
        yc_in, uc_in, hc_in, ic_in, icc_in = sem("yc_in"), sem("uc_in"), sem("hc_in"), sem("ic_in"), sem("icc_in")
        up_ok, hp_ok, fin_ok, o_out = sem("up_ok"), sem("hp_ok"), sem("fin_ok"), sem("o_out")
        hm_zero, g_stat, gat_cp = sem("hm_zero"), sem("g_stat"), sem("gat_cp")

        def bank(i, n=512, rows=128, at=0):
            return ps[0:rows, i, at:at + n]

        def grp(x, g):
            return x[:, GB * g:GB * g + GB]

        def pairs_of(x, a, g=0, n=B):
            return x[:, GB * g + a:GB * g + n:2]

        def variances(i):
            return i + 1 if i < 2 * G else 2 * G + (i - 2 * G) // 2 + 1

        def move_patches(eng, r):
            c, k, g = r // 4, (r % 4) // 2, r % 2
            out_ = xt[:, 2 * (c % CH) + k, :, :, 4 * g:4 * g + 4].rearrange("p b y x -> p x (b y)")
            in_ = bank(r % 4).rearrange("p (x n) -> p x n", x=4)
            return eng.copy(out_, in_) if r % 2 else eng.tensor_copy(out_, in_)

        block = ctx.enter_context(nc.Block())

        @block.sync
        def _(sp):
            sp.dma_start(c128[:, :], t["c128"]).then_inc(cst_in, 16)
            for c in range(2 * CH):
                src = t["x"][16 * (c // CH):16 * (c // CH) + 16, c % CH].rearrange("b (g y) x -> b g (y x)", g=NG)
                if c >= NX:
                    sp.wait_ge(xr_ok, 2 * (c - NX + 1))
                q = 2048 * (c % NX)
                sp.dma_start(rx[:, q:q + 2048], src).then_inc(x_in[c], 16)
            sp.dma_start(cl[:, :], t["cl"]).then_inc(cl_in, 16)
            for j, name in enumerate(("v1", "g1", "b1", "m1", "be1", "v2", "g2", "b2", "m2", "be2")):
                sp.dma_start(bnr[EP * j:EP * j + EP, :],
                             t["L0_ffn_" + name].rearrange("(p e) h -> p (e h)", e=2)).then_inc(bn_in, 16)
            sp.wait_ge(set_p, N_SET_P)
            for q in range(NE * SC // 4):
                sp.dma_start(slots[512 * q:512 * q + 512, :].rearrange("(p c) d -> p (c d)", p=128),
                             zeros[:, :]).then_inc(z_out, 16)
            sp.dma_start(wra[0:D, :], t["L0_ffn_Wr"]).then_inc(ffn_in, 16)
            sp.dma_start(wra[D:L, :], t["L0_ffn_br"].unsqueeze(0)).then_inc(ffn_in, 16)
            sp.dma_start(bof[:, :], t["L0_ffn_bo"]).then_inc(ffn_in, 16)
            sp.wait_ge(kk_done, 1)
            sp.dma_start(w1r[:, :, :], t["L0_ffn_W1"].rearrange("e d h -> d e h")).then_inc(ffn_in, 16)
            sp.dma_start(wof[:, :, :], t["L0_ffn_Wo"].rearrange("(p e) h d -> (e h) p d", e=2)).then_inc(ffn_in, 16)
            sp.dma_start(csel[:, :], t["csel"]).then_inc(ffn_in, 16)
            sp.wait_ge(w2_zero, 1)
            for q in range(2):
                sp.dma_start(w2f[D * q:D * q + D, :, D * q:D * q + D],
                             t["L0_ffn_W2"].rearrange("(p e) h k -> e h p k", e=2)[q]).then_inc(ffn_in, 16)
            sp.wait_ge(kx_ok, 1)
            sp.dma_start(kd, kx[:, :]).then_inc(kd_out, 16)
            sp.wait_ge(kd_out, 16)
            for m in range(D):
                sp.dma_start(toep[m:m + 1, :, 0:D], kd[:, D - m:2 * D - m].unsqueeze(0)).then_inc(t_in, 16)
            sp.dma_start(toep[D:L, :, :], kd[:, D + 1:KW].unsqueeze(0)).then_inc(t_in, 16)
            sp.wait_ge(pv_done, 2 * PAIRS)
            sp.dma_start(cr, t["cr"]).then_inc(moe_in, 16)
            sp.dma_start(gwa[0:D, :], t["L1_ffn_gate_w"]).then_inc(moe_in, 16)
            sp.dma_start(gwa[D:L, :], t["L1_ffn_gate_b"].unsqueeze(0)).then_inc(moe_in, 16)
            sp.dma_start(w1e[0:D, :, :], t["L1_ffn_w1"].rearrange("e d f -> d e f")).then_inc(moe_in, 16)
            sp.dma_start(w1e[D:L, :, :], t["L1_ffn_b1"].unsqueeze(0)).then_inc(moe_in, 16)
            sp.dma_start(w2e[:, :, :, :], t["L1_ffn_w2"].rearrange("e (f p) d -> p e f d", p=128)).then_inc(moe_in, 16)
            sp.dma_start(b2e[:, :, :], t["L1_ffn_b2"].partition_broadcast(128)).then_inc(moe_in, 16)
            sp.wait_ge(ln_u, 4 * G)
            sp.dma_start(uc, uu[D:L, :, :]).then_inc(uc_in, 16)
            sp.dma_start(hc, hh[D:L, :, :]).then_inc(hc_in, 16)
            sp.wait_ge(idx_ok, 6)
            sp.dma_start(ics[:, :], crow[D:L, 0, :]).then_inc(ic_in, 16)
            sp.dma_start(icg[:, :], crow[D:L, 1, :]).then_inc(ic_in, 16)
            sp.wait_ge(co_ok, 1)
            sp.dma_start(cc[:, :], rb[D:L, 11, :]).then_inc(icc_in, 16)
            sp.wait_ge(sc_out, 16 * (PAIRS + 1))
            for q in range(2):
                n = NE * SC // 2
                sp.dma_start(xb[:, n * q:n * q + n, :],
                             slots[128 * n * q:128 * n * (q + 1), :].rearrange("(c p) d -> p c d", p=128)
                             ).then_inc(xb_in[q], 16)
            for e in range(NE):
                sp.wait_ge(yb_ok, e + 1)
                sp.dma_start(yslots[SL * e:SL * e + SL, :].rearrange("(c p) d -> p c d", p=128),
                             yb[:, SC * e:SC * e + SC, :]).then_inc(y_out, 16)
            sp.wait_ge(fin_ok, 1)
            sp.dma_start(out[:, 0, :], hc).then_inc(o_out, 16)
            for c in range(4):
                sp.wait_ge(fin_ok, c + 2)
                for a in range(2):
                    sp.dma_start(out[GB * c + a:GB * c + GB:2, 1:L, :].rearrange("b l d -> l b d"),
                                 hp[D * a:D * a + D, 4 * c:4 * c + 4, :]).then_inc(o_out, 16)
            sp.wait_ge(o_out, 16 * 9)

        @block.gpsimd
        def _(po):
            po.dma_start(cxy[:, :], t["cxy"]).then_inc(tok_in, 16)
            po.dma_start(w1t[0:2, :], t["L0_tok_W1"]).then_inc(tok_in, 16)
            po.dma_start(w1t[2:3, :], t["L0_tok_b1"].unsqueeze(0)).then_inc(tok_in, 16)
            po.dma_start(w2t[0:D, :], t["L0_tok_W2"]).then_inc(tok_in, 16)
            po.dma_start(w2t[D:L, :], t["L0_tok_b2"].unsqueeze(0)).then_inc(tok_in, 16)
            po.dma_start(bpt[:, :], t["L0_tok_bp"].unsqueeze(0)).then_inc(tok_in, 16)
            for n, (tile, value) in enumerate(((ones[:, :], 1.0), (rr[D:L, :], 1.0),
                                (ut[D:L, :, :], 1.0), (expo[:, :], -0.5), (zeros[:, :], 0.0),
                                (va[:, :, :, :], 0.0), (vb[:, :, :, :], 0.0))):
                po.memset(tile, value).then_inc(set_p, 1)
                po.wait_ge(set_p, n + 1)
            po.dma_start(hh[D:L, :, :], t["cls_tok"].rearrange("a b d -> (a b) d").broadcast_to([B, D]).unsqueeze(0)
                         ).then_inc(cls_in, 16)
            po.dma_start(bub[:, :], t["L0_attn_bu"].partition_broadcast(L)).then_inc(cls_in, 16)
            for r, name in ((lam, "lambda"), (pri, "p"), (qri, "q")):
                for q in range(2):
                    po.dma_start(r[D * q:D * q + D, :], t[f"L1_attn_{name}_ri"]).then_inc(s4_in, 16)
            for q in range(2):
                po.dma_start(lsb[D * q:D * q + D, :],
                             t["L1_attn_log_step"][32 * q:32 * q + 32].partition_broadcast(D)).then_inc(s4_in, 16)
            for q, name in enumerate(("B", "Ct")):
                po.dma_start(bct[:, q], t[f"L1_attn_{name}_ri"].rearrange("(a h) n r -> h a n r", a=2)).then_inc(s4_in, 16)
            po.dma_start(dcol[:, :], t["L1_attn_D"].rearrange("a b h -> (a b h)").unsqueeze(1)).then_inc(s4_in, 16)

            def centre(i):
                po.wait_ge(ln_mean, i + 1)
                g = i % G
                if i >= 3 * G:
                    po.wait_ge(cv_done, 4)
                elif i >= G:
                    po.wait_ge(ut_done, 2 * (i - G) + 2)
                po.tensor_tensor(grp(uu, g), grp(hh, g), lmean[:, GB * i:GB * i + GB, :].broadcast_to([L, GB, D]),
                                 ALU.subtract).then_inc(ln_cen, 1)

            def root(i, n):
                po.wait_ge(ln_vs, variances(i))
                v = slice(GB * i, GB * (i + n))
                po.tensor_tensor(lrs[:, v, 0], lvs[:, v, 0], expo[0:L, 0:GB * n], ALU.pow).then_inc(ln_pow, 1)

            def norm(p):
                po.wait_ge(rc_ok, p + 1)
                if p >= 2:
                    po.wait_ge(pt_done, p - 1)
                po.tensor_tensor(pp[p % 2].rearrange("p (h j) -> p h j", h=NH),
                                 sx[p % 2].rearrange("p (h j) -> p h j", h=NH),
                                 rc[:, p % 2].unsqueeze(2).broadcast_to([128, NH, 64]), ALU.mult).then_inc(p_ok, 1)

            def bias_u(g):
                po.wait_ge(ln_cen, g + 1)
                po.wait_ge(cls_in, 32)
                po.tensor_tensor(grp(hh, g), grp(hh, g), bub[:, :].unsqueeze(1).broadcast_to([L, GB, D]),
                                 ALU.add).then_inc(bu_add, 1)

            for g in range(G):
                centre(g)
                root(g, 1)
            po.wait_ge(g_exp, 1)
            po.wait_ge(cst_in, 16)
            po.tensor_tensor(g_w, gg[:, :].unsqueeze(2).broadcast_to([128, 32, L]),
                             ttab.unsqueeze(1).broadcast_to([128, 32, L]), ALU.mult).then_inc(g_outer, 1)
            for g in range(G):
                bias_u(g)
            for p in range(PAIRS + 4):
                if p < PAIRS:
                    norm(p)
                if 1 <= p <= 8:
                    po.wait_ge(g_recip, p)
                    v = slice(4 * (p - 1), 4 * p)
                    po.tensor_tensor(g_winv[:, v], g_w[:, v], g_inv[:, v], ALU.mult).then_inc(g_prod, 1)
                if p == 10:
                    po.wait_ge(bn_cp, 3)
                    for i in range(2):
                        po.tensor_tensor(bna[:, 2 * i, :], bn[:, 5 * i, :], expo[:, 0:EP], ALU.pow).then_inc(bn_pow, 1)
                if p >= 5 and (p - 5) % 4 == 0:
                    centre(G + (p - 5) // 4)
                if p >= 6 and (p - 6) % 4 == 0:
                    root(G + (p - 6) // 4, 1)
                if p == 15:
                    po.wait_ge(kk_done, 1)
                    po.memset(w2f[:, :, :], 0.0).then_inc(w2_zero, 1)
            po.wait_ge(wb_cp, 2)
            for g in range(G):
                po.wait_ge(ln_cen, G + g + 1)
                po.tensor_tensor(grp(hh, g), grp(hh, g), bow[:, :].unsqueeze(1).broadcast_to([L, GB, D]),
                                 ALU.add).then_inc(bow_add, 1)
            for n in range(2, 4):
                centre(G * n)
                centre(G * n + 1)
                root(G * n, 2)
                centre(G * n + 2)
                root(G * n + 2, 2)
                centre(G * n + 3)
            po.wait_ge(idx_ok, 6)
            po.wait_ge(z_out, 16 * NE * SC // 4)
            po.wait_ge(up_ok, 2 * G)
            for c in range(PAIRS):
                po.indirect_dma_start(out=slots, out_offset=bass.IndirectOffsetOnAxis(ap=ixs[:, c:c + 1], axis=0),
                                      in_=up[:, c, :], in_offset=None, bounds_check=NE * SL - 1,
                                      oob_is_err=False).then_inc(sc_out, 16)
            po.wait_ge(uc_in, 16)
            po.wait_ge(ic_in, 32)
            po.indirect_dma_start(out=slots, out_offset=bass.IndirectOffsetOnAxis(ap=ics[:, :], axis=0),
                                  in_=uc, in_offset=None, bounds_check=NE * SL - 1,
                                  oob_is_err=False).then_inc(sc_out, 16)
            po.wait_ge(y_out, 16 * NE)
            po.indirect_dma_start(out=yc, out_offset=None, in_=yslots,
                                  in_offset=bass.IndirectOffsetOnAxis(ap=icg[:, :], axis=0),
                                  bounds_check=NE * SL - 1, oob_is_err=False).then_inc(yc_in, 16)
            for c in range(PAIRS):
                po.indirect_dma_start(out=yg[:, c, :], out_offset=None, in_=yslots,
                                      in_offset=bass.IndirectOffsetOnAxis(ap=ixg[:, c:c + 1], axis=0),
                                      bounds_check=NE * SL - 1, oob_is_err=False).then_inc(yg_in[c // 4], 16)

        @block.scalar
        def _(sc):
            sc.dma_start(wp[:, :, :], t["L0_tok_Wp"].rearrange("(k p) d -> p k d", p=128)).then_inc(wp_in, 16)
            for w, n in zip(wqkv, "qkv"):
                sc.dma_start(w[0:D, :], t[f"L0_attn_W{n}"]).then_inc(qkv_in, 16)
                sc.dma_start(w[D:L, :], t[f"L0_attn_b{n}"].unsqueeze(0)).then_inc(qkv_in, 16)
            sc.dma_start(wu[:, :, :], t["L0_attn_Wu"].rearrange("(h e) d -> e h d", h=NH)).then_inc(qkv_in, 16)

            def patches(c):
                for r in (4 * c + 1, 4 * c + 3):
                    sc.wait_ge(xt_done, r + 1)
                    move_patches(sc, r).then_inc(xt_ca, 1)

            def embedded(g):
                sc.wait_ge(emb_done, g + 1)
                if g >= 2:
                    sc.wait_ge(lt_done, g - 1)
                sc.copy(et[:, g % 2, :], bank(4, 512, D)).then_inc(et_cp, 1)

            def turned(i, attention):
                for q in range(2):
                    sc.wait_ge(ut_done, 2 * i + q + 1)
                    if i == 0 and q == 0:
                        sc.wait_ge(set_p, N_SET_P)
                    b0 = GB * (i % G) + 4 * q
                    src = bank(q, 4 * L, D).rearrange("p (b l) -> p b l", b=4)
                    if attention:
                        sc.copy(ut[0:D, b0:b0 + 4, 1:L], src[:, :, 0:D])
                        sc.copy(ut[0:D, b0:b0 + 4, 0:1], src[:, :, D:L]).then_inc(ut_cp, 1)
                    else:
                        sc.copy(ut[0:D, b0:b0 + 4, :], src).then_inc(ut_cp, 1)

            def keys(g, h):
                sc.wait_ge(z_done, NH * g + h + 1)
                sc.copy(zz[g][:, :, h, :], bank(h % 2, 512, L).rearrange("p (b j) -> p b j", b=GB)).then_inc(z_cp, 1)

            def values(g, q):
                sc.wait_ge(v_done, 4 * g + q + 1)
                b0 = GB * g + 2 * q
                sc.copy(vv[:, b0:b0 + 2].rearrange("p b h d -> p (b h d)"), bank(2)).then_inc(v_cp, 1)

            def expo_(p):
                sc.wait_ge(sub_ok, p + 1)
                sc.activation(sx[p % 2], sx[p % 2], ACT.Exp, scale=float(D) ** -0.5).then_inc(exp_ok, 1)

            def ptcopy(p):
                sc.wait_ge(pt_done, p + 1)
                if p >= 2:
                    sc.wait_ge(pv_done, 2 * (p - 1))
                sc.copy(pt[p % 2], bank(5)).then_inc(pt_cp, 1)

            patches(0)
            patches(1)
            sc.wait_ge(r_done, 1)
            sc.activation(rr[0:D, :], bank(6, NPOS, D), ACT.Relu).then_inc(r_cp, 1)
            patches(2)
            embedded(0)
            embedded(1)
            sc.wait_ge(s4_in, 16 * N_S4)
            sc.activation(gg[:, :], lsb[:, :], ACT.Exp, scale=-1.0).then_inc(g_exp, 1)
            for c in range(3, 6):
                patches(c)
            embedded(2)
            embedded(3)
            turned(0, True)
            for q in range(4):
                keys(0, 2 * q)
                keys(0, 2 * q + 1)
                values(0, q)
            sc.wait_ge(g_shift, 1)
            sc.activation(g_inv, g_w, ACT.Square).then_inc(g_sq, 1)
            for p in range(PAIRS + 1):
                g, r = p // 4 + 1, p % 4
                prep = g < G
                if prep and r == 0:
                    turned(g, True)
                if prep:
                    keys(g, 2 * r)
                if p:
                    ptcopy(p - 1)
                if p < PAIRS:
                    expo_(p)
                if prep:
                    keys(g, 2 * r + 1)
                    values(g, r)
                if 13 <= p < PAIRS:
                    turned(G + p - 13, False)
            turned(2 * G - 1, False)

            def relu1(k):
                sc.wait_ge(l1_done, k + 1)
                if k >= 2:
                    sc.wait_ge(l2_done, k - 1)
                if k == 0:
                    sc.wait_ge(bn_ok, 2)
                    sc.wait_ge(pv_done, 2 * PAIRS)
                n = BCH[k // EP][1] * L
                sc.activation(h1[k % 2][:, 0:n], bank(k % 2, n), ACT.Relu, bias=bna[:, 1, k % EP:k % EP + 1],
                              scale=bna[:, 0, k % EP:k % EP + 1]).then_inc(r1_ok, 1)

            def relu2(k):
                sc.wait_ge(l2_done, k + 1)
                if k >= EP:
                    sc.wait_ge(wm_ok, k - EP + 1)
                n = BCH[k // EP][1] * L
                sc.activation(h2[k % EP][:, 0:n], bank(2 + k % 2, n), ACT.Relu, bias=bna[:, 3, k % EP:k % EP + 1],
                              scale=bna[:, 2, k % EP:k % EP + 1]).then_inc(r2_ok, 1)

            def mixed(c):
                sc.wait_ge(l3_step, EP * (c + 1))
                if c >= 2:
                    sc.wait_ge(yt_done, c - 1)
                n = BCH[c][1] * L
                sc.copy(y3[c % 2][:, 0:n], bank(4 + c % 2, n, D)).then_inc(y3_cp, 1)

            steps = EP * len(BCH)
            for k in range(steps + LAG3 + 1):
                if k < steps:
                    relu1(k)
                if 1 <= k <= steps:
                    relu2(k - 1)
                if k == 2:
                    sc.wait_ge(rt_exp, 1)
                    sc.activation(rt[:, 8:16], bank(6, NE, L), ACT.Exp, bias=rt[:, 0:1],
                                  accum_out=rt[:, 1:2]).then_inc(rt_exp, 1)
                if k >= LAG3 and (k - LAG3) % EP == EP - 1:
                    mixed((k - LAG3) // EP)
            for g in range(G):
                turned(2 * G + g, False)
            for g in range(G):
                for a in range(2):
                    sc.copy(up[D * a:D * a + D, 4 * g:4 * g + 4, :],
                            pairs_of(uu[0:D], a, g, GB)).then_inc(up_ok, 1)
            sc.wait_ge(gt_sub, 1)
            sc.activation(ra[:, 0, :], ra[:, 0, :], ACT.Exp).then_inc(gt_exp, 1)
            for a in range(2):
                sc.copy(hp[D * a:D * a + D, :, :], pairs_of(hh[0:D], a)).then_inc(hp_ok, 1)
            sc.wait_ge(xe_one, 1)
            for e in range(NE + 1):
                if e < NE:
                    sc.wait_ge(xe_done, e + 1)
                    sc.copy(xe[0:D, e, 0:CAP], bank(e % 2, CAP, D)).then_inc(xe_cp, 1)
                if e >= 1:
                    sc.wait_ge(f1_done, 2 * e - 1)
                    if e >= 3:
                        sc.wait_ge(f2_done, e - 2)
                    if e == 1:
                        sc.wait_ge(hm_zero, 1)
                    sc.activation(hm[(e - 1) % 2][:, 0, 0:CAP], bank(2, CAP), ACT.Relu).then_inc(f1_ca, 1)

        @block.vector
        def _(ve):
            steps = [0]

            def chain(ins):
                ins.then_inc(vstep, 1)
                steps[0] += 1
                ve.wait_ge(vstep, steps[0])

            def mean(i):
                g = i % G
                v = slice(GB * i, GB * i + GB)
                for b in range(GB):
                    m = ve.bn_stats(bst[:, i, b, :], hh[:, GB * g + b, :])
                chain(m)
                chain(ve.tensor_tensor(lsum[:, v, :], bst[:, i, :, 1:3], bst[:, i, :, 4:6], ALU.add))
                ve.tensor_scalar(lmean[:, v, 0], lsum[:, v, 0], 0.5, None, ALU.mult).then_inc(ln_mean, 1)

            def var(i, n=1):
                v = slice(GB * i, GB * (i + n))
                half_mean = bst[:, i:i + n, :, :].rearrange("p i b s -> p (i b) s")
                chain(ve.tensor_tensor(ldif[:, v, 0], half_mean[:, :, 1], half_mean[:, :, 4], ALU.subtract))
                chain(ve.scalar_tensor_tensor(lsqd[:, v, 0], ldif[:, v, 0], D / 4.0, ldif[:, v, 0], ALU.mult, ALU.mult))
                chain(ve.tensor_tensor(lsqd[:, v, 0], lsqd[:, v, 0], lsum[:, v, 1], ALU.add))
                ve.tensor_scalar(lvs[:, v, 0], lsqd[:, v, 0], 1.0 / D, LN_EPS, ALU.mult, ALU.add).then_inc(ln_vs, 1)

            def scale(i):
                ve.wait_ge(ln_pow, variances(i))
                ve.wait_ge(ln_cen, i + 1)
                ve.tensor_tensor(grp(uu, i % G), grp(uu, i % G),
                                 lrs[:, GB * i:GB * i + GB, :].broadcast_to([L, GB, D]), ALU.mult).then_inc(ln_u, 1)

            def rearranged(c):
                ve.wait_ge(x_in[c], 16)
                if c >= 2:
                    ve.wait_ge(xt_done, 4 * (c - 1))
                for k in range(2):
                    ve.tensor_copy(xr[c % 2][:, k].rearrange("p g (y x) -> p g y x", y=8),
                                   ximg[:, c % NX, 8 * k:8 * k + 8, :].rearrange("p y (g x) -> p g y x", g=NG)
                                   ).then_inc(xr_ok, 1)

            def patches(c):
                for r in (4 * c, 4 * c + 2):
                    ve.wait_ge(xt_done, r + 1)
                    move_patches(ve, r).then_inc(xt_cv, 1)

            def tokens(g):
                ve.wait_ge(lt_done, g + 1)
                if g == 0:
                    ve.wait_ge(pos_cp, 1)
                    ve.wait_ge(cls_in, 32)
                ve.tensor_tensor(grp(hh[0:NPOS], g), bank(5, 512, NPOS).rearrange("p (b d) -> p b d", b=GB),
                                 posb[:, :].unsqueeze(1).broadcast_to([NPOS, GB, D]), ALU.add).then_inc(h0_ok, 1)
                ve.wait_ge(h0_ok, g + 1)

            rearranged(0)
            for c in range(3):
                rearranged(c + 1)
                patches(c)
            ve.wait_ge(pos_done, 1)
            ve.tensor_copy(posb[:, :], bank(7, D, NPOS)).then_inc(pos_cp, 1)
            rearranged(4)
            for g in range(2):
                tokens(g)
                mean(g)
                var(g)
            for i in range(6):
                ve.wait_ge(wt_done, i + 1)
                ve.tensor_copy(wt[i // 2][:, 4 * (i % 2):4 * (i % 2) + 4, :],
                               bank(WTB[i], 4 * L, D).rearrange("p (h l) -> p h l", h=4)).then_inc(wt_cp, 1)
            for i in range(2):
                ve.wait_ge(mn_done, i + 1)
                ve.tensor_copy(mm_[:, 4 * i:4 * i + 4, :],
                               bank(6 + i, 4 * L, L).rearrange("p (h l) -> p h l", h=4)).then_inc(mn_cp, 1)
            ve.wait_ge(mn_done, 3)
            ve.tensor_copy(nn_[:, :, :, :].rearrange("p a h d -> p h a d"),
                           bank(0, 512, L).rearrange("p (h a d) -> p h a d", a=2, d=D)).then_inc(mn_cp, 1)
            ve.wait_ge(bt_done, 1)
            ve.tensor_copy(bc[:, :, :], bank(3, 128).rearrange("p (a h) -> p a h", a=4)).then_inc(bt_cp, 1)
            for c in range(3, 6):
                patches(c)
                if c == 3:
                    rearranged(5)
                if c == 4:
                    scale(0)
                    scale(1)
            for g in range(2, 4):
                tokens(g)
                mean(g)
                var(g)
            ve.memset(onebf[:, :], 1.0).then_inc(set_v, 1)
            ve.wait_ge(cl_in, 16)
            ve.tensor_copy(tribf[:, :], tri).then_inc(set_v, 1)
            scale(2)
            scale(3)

            ve.wait_ge(s4_in, 16 * N_S4)
            u_re, u_im = bc[:, 0, :], bc[:, 1, :]
            x_re, x_im = bc[:, 2, :], bc[:, 3, :]
            pc, qc = (pri[:, 0:1], pri[:, 1:2]), (qri[:, 0:1], qri[:, 1:2])
            t0, t1 = wtmp[:, 0, :], wtmp[:, 1, :]
            chain(ve.tensor_tensor(t0, x_im, u_im, ALU.mult))
            chain(ve.tensor_tensor(t1, x_re, u_re, ALU.mult))
            chain(ve.tensor_tensor(wc[:, 0, 0], t0, t1, ALU.add))
            chain(ve.tensor_tensor(t0, x_im, u_re, ALU.mult))
            chain(ve.tensor_tensor(t1, x_re, u_im, ALU.mult))
            chain(ve.tensor_tensor(wc[:, 0, 1], t1, t0, ALU.subtract))
            chain(ve.tensor_scalar(t0, x_im, pc[1], None, ALU.mult))
            chain(ve.scalar_tensor_tensor(wc[:, 1, 0], x_re, pc[0], t0, ALU.mult, ALU.add))
            chain(ve.tensor_scalar(t0, x_im, pc[0], None, ALU.mult))
            chain(ve.scalar_tensor_tensor(wc[:, 1, 1], x_re, pc[1], t0, ALU.mult, ALU.subtract))
            chain(ve.tensor_scalar(t0, u_im, qc[1], None, ALU.mult))
            chain(ve.scalar_tensor_tensor(wc[:, 2, 0], u_re, qc[0], t0, ALU.mult, ALU.add))
            chain(ve.tensor_scalar(t0, u_re, qc[1], None, ALU.mult))
            chain(ve.scalar_tensor_tensor(wc[:, 2, 1], u_im, qc[0], t0, ALU.mult, ALU.subtract))
            chain(ve.tensor_scalar(ws[:, 0:2], qri[:, :], pc[1], None, ALU.mult))
            chain(ve.tensor_scalar(ws[:, 2:4], qri[:, :], pc[0], None, ALU.mult))
            chain(ve.tensor_tensor(ws[:, 4:5], ws[:, 2:3], ws[:, 1:2], ALU.add))
            chain(ve.tensor_tensor(ws[:, 5:6], ws[:, 0:1], ws[:, 3:4], ALU.subtract))
            chain(ve.tensor_copy(wc[:, 3], ws[:, 4:6].unsqueeze(2).broadcast_to([128, 2, 32])))
            chain(ve.tensor_scalar(ws[:, 0:2], lam[:, :], RSC, None, ALU.mult))
            chain(ve.tensor_tensor(ws[:, 2:3], ws[:, 0:1], ws[:, 0:1], ALU.mult))
            chain(ve.tensor_scalar(ws[:, 3:4], ws[:, 0:1], -RSC, None, ALU.mult))
            ve.wait_ge(set_p, N_SET_P)
            for q in range(2):
                r = slice(D * q, D * q + D)
                dst_a = va[r, :, q, :].rearrange("p h c -> p c h")
                dst_b = vb[r, :, q, :].rearrange("p h (x c) -> p c x h", c=2)
                w_all = wc[r].rearrange("p x c h -> p (x c) h")
                ve.tensor_scalar(dst_a, w_all, ws[r, 3:4], None, ALU.mult).then_inc(vab_ok, 1)
                ve.tensor_scalar(dst_b[:, 0], wc[r, :, 1], -RSC, None, ALU.mult).then_inc(vab_ok, 1)
                ve.tensor_scalar(dst_b[:, 1], wc[r, :, 0], RSC, None, ALU.mult).then_inc(vab_ok, 1)
            ve.wait_ge(g_outer, 1)
            ve.tensor_scalar(g_w, g_w, ws[:, 1:2], None, ALU.add).then_inc(g_shift, 1)
            ve.wait_ge(g_sq, 1)
            ve.tensor_scalar(g_inv, g_inv, ws[:, 2:3], None, ALU.add).then_inc(g_den, 1)
            ve.wait_ge(g_den, 1)

            ve.wait_ge(emb_done, G)
            ve.memset(toep[0:D, :, D:L], 0.0).then_inc(t_zero, 1)

            def by_head(x):
                return x.rearrange("p (h j) -> p h j", h=NH)

            def rowmax(p):
                ve.wait_ge(s_done, p + 1)
                if p >= 2:
                    ve.wait_ge(p_ok, p - 1)
                ve.tensor_tensor(by_head(sx[p % 2]), by_head(bank(3 + p % 2)),
                                 cmask.unsqueeze(1).broadcast_to([128, NH, 64]), ALU.add).then_inc(msk_ok, 1)
                ve.wait_ge(msk_ok, p + 1)
                ve.tensor_reduce(mx[:, p % 2], by_head(sx[p % 2]), X, ALU.max).then_inc(mx_ok, 1)
                ve.wait_ge(mx_ok, p + 1)
                ve.tensor_tensor(by_head(sx[p % 2]), by_head(sx[p % 2]),
                                 mx[:, p % 2].unsqueeze(2).broadcast_to([128, NH, 64]), ALU.subtract).then_inc(sub_ok, 1)

            def rowsum(p):
                ve.wait_ge(exp_ok, p + 1)
                ve.tensor_reduce(mx[:, p % 2], by_head(sx[p % 2]), X, ALU.add).then_inc(sum_ok, 1)
                ve.wait_ge(sum_ok, p + 1)
                ve.reciprocal(rc[:, p % 2], mx[:, p % 2]).then_inc(rc_ok, 1)

            def attended(g):
                ve.wait_ge(pv_done, GB * (g + 1))
                ve.wait_ge(bu_add, g + 1)
                ve.tensor_tensor(grp(hh[0:NPOS], g), grp(hh[0:NPOS], g),
                                 bank(7, 512, NPOS).rearrange("p (b d) -> p b d", b=GB), ALU.add).then_inc(o_add, 1)
                ve.wait_ge(o_add, g + 1)

            def feature(g):
                ve.wait_ge(ut_cp, 2 * (G + g) + 2)
                ve.tensor_reduce(fpart[:, :, g], grp(ut, g).rearrange("p b l -> p l b"), X, ALU.add).then_inc(ft_part, 1)

            def batch_norm(part):
                if part == 0:
                    ve.wait_ge(bn_done, 1)
                    ve.tensor_copy(bn[:, :, :], bank(6, 40).rearrange("p (a e) -> p a e", a=10)).then_inc(bn_cp, 1)
                    ve.wait_ge(bn_cp, 1)
                    for i in range(2):
                        ve.tensor_scalar(bn[:, 5 * i], bn[:, 5 * i], BN_EPS, None, ALU.add).then_inc(bn_cp, 1)
                else:
                    ve.wait_ge(bn_pow, 2)
                    for i in range(2):
                        chain(ve.tensor_tensor(bna[:, 2 * i], bna[:, 2 * i], bn[:, 5 * i + 1], ALU.mult))
                        chain(ve.tensor_tensor(bna[:, 2 * i + 1], bn[:, 5 * i + 2], bn[:, 5 * i + 3], ALU.subtract))
                        chain(ve.tensor_tensor(bna[:, 2 * i + 1], bna[:, 2 * i + 1], bna[:, 2 * i], ALU.mult))
                        ve.tensor_tensor(bna[:, 2 * i + 1], bna[:, 2 * i + 1], bn[:, 5 * i + 4], ALU.add).then_inc(bn_ok, 1)

            k_ = [ks[:, i, :] for i in range(8)]
            a_ = [kt_[:, i, :] for i in range(10)]

            def tt(dst, x, y, op):
                chain(ve.tensor_tensor(dst, x, y, op))

            def at_roots(part):
                if part == 0:
                    ve.wait_ge(kk_done, 1)
                    chain(ve.tensor_copy(ks.rearrange("p c (a h) -> p c a h", a=2),
                                         bank(6, 512, L).rearrange("p (h a c) -> p c a h", a=2, c=8)))
                    ve.tensor_copy(kt_[:, 9, 0:1], ks[:, 0, 0:1]).then_inc(kk_cp, 1)
                    tt(a_[0], k_[2], k_[4], ALU.mult)
                    tt(a_[1], k_[3], k_[5], ALU.mult)
                    tt(a_[0], a_[0], a_[1], ALU.subtract)
                    tt(a_[1], k_[2], k_[5], ALU.mult)
                    tt(a_[2], k_[3], k_[4], ALU.mult)
                    tt(a_[1], a_[1], a_[2], ALU.add)
                    chain(ve.tensor_scalar(a_[2], k_[6], 1.0, None, ALU.add))
                    tt(a_[3], a_[2], a_[2], ALU.mult)
                    tt(a_[4], k_[7], k_[7], ALU.mult)
                    tt(a_[3], a_[3], a_[4], ALU.add)
                    chain(ve.reciprocal(a_[4], a_[3]))
                else:
                    tt(a_[5], a_[0], a_[2], ALU.mult)
                    tt(a_[6], a_[1], k_[7], ALU.mult)
                    tt(a_[5], a_[5], a_[6], ALU.add)
                    tt(a_[5], a_[5], a_[4], ALU.mult)
                    tt(a_[6], a_[1], a_[2], ALU.mult)
                    tt(a_[7], a_[0], k_[7], ALU.mult)
                    tt(a_[6], a_[6], a_[7], ALU.subtract)
                    tt(a_[6], a_[6], a_[4], ALU.mult)
                    tt(a_[5], k_[0], a_[5], ALU.subtract)
                    tt(a_[6], k_[1], a_[6], ALU.subtract)
                    chain(ve.scalar_tensor_tensor(a_[8], a_[6], tau, a_[5], ALU.mult, ALU.add))
                    chain(ve.tensor_scalar(a_[7], a_[5], tau, None, ALU.mult))
                    ve.tensor_tensor(a_[9], a_[6], a_[7], ALU.subtract).then_inc(at_ok, 1)

            for p in range(PAIRS + 4):
                if p < PAIRS:
                    rowmax(p)
                    if p < 8:
                        v = slice(4 * p, 4 * p + 4)
                        ve.reciprocal(g_inv[:, v], g_inv[:, v]).then_inc(g_recip, 1)
                    rowsum(p)
                if p >= 5 and (p - 5) % 4 == 0:
                    attended((p - 5) // 4)
                    mean(G + (p - 5) // 4)
                    var(G + (p - 5) // 4)
                if p == 10:
                    batch_norm(0)
                if p == 11:
                    batch_norm(1)
                if p >= 7 and (p - 7) % 4 == 0:
                    scale(G + (p - 7) // 4)
                if 14 <= p <= 16:
                    feature(p - 14)
                if 15 <= p <= 16:
                    at_roots(p - 15)

            feature(3)
            ve.wait_ge(ft_part, G)
            chain(ve.tensor_reduce(feat[:, :], fpart[:, :, :], X, ALU.add))
            ve.tensor_scalar(feat[:, :], feat[:, :], 1.0 / B, None, ALU.mult).then_inc(ft_ok, 1)
            ve.wait_ge(lg_done, 1)
            ve.tensor_reduce(rt[:, 0:1], bank(6, NE, L), X, ALU.max, negate=True).then_inc(rt_exp, 1)
            ve.wait_ge(rt_exp, 2)
            chain(ve.reciprocal(rt[:, 2:3], rt[:, 1:2]))
            ve.tensor_scalar(rt[:, 16:24], rt[:, 8:16], rt[:, 2:3], None, ALU.mult).then_inc(w_ok, 1)
            ve.wait_ge(wtt_done, 1)
            ve.tensor_copy(wtt[:, :], bank(6, L, NE)).then_inc(wtt_cp, 1)
            ve.wait_ge(wb_done, 1)
            ve.tensor_copy(wb[:, :, :], bank(7, EP * L).rearrange("p (a l) -> p a l", a=EP)).then_inc(wb_cp, 1)
            ve.tensor_copy(bow[:, :], bank(7, D, L, EP * L)).then_inc(wb_cp, 1)

            def weigh(k):
                ve.wait_ge(r2_ok, k + 1)
                if k >= 2:
                    ve.wait_ge(l3_step, k - 1)
                if k == 0:
                    ve.wait_ge(wb_cp, 2)
                nb = BCH[k // EP][1]
                ve.tensor_tensor(h2w[k % 2][:, 0:nb * L].rearrange("p (b l) -> p b l", b=nb),
                                 h2[k % EP][:, 0:nb * L].rearrange("p (b l) -> p b l", b=nb),
                                 wb[:, k % EP].unsqueeze(1).broadcast_to([128, nb, L]), ALU.mult).then_inc(wm_ok, 1)

            def fed(c):
                b0, nb = BCH[c]
                ve.wait_ge(yt_done, c + 1)
                if c == 0:
                    ve.wait_ge(bow_add, G)
                ve.tensor_tensor(hh[:, b0:b0 + nb], hh[:, b0:b0 + nb],
                                 bank(6 + c % 2, nb * D, L).rearrange("p (b d) -> p b d", b=nb),
                                 ALU.add).then_inc(y_add, 1)
                ve.wait_ge(y_add, c + 1)

            for k in range(EP * len(BCH) + 4):
                if k < EP * len(BCH):
                    weigh(k)
                if k == 1:
                    ve.wait_ge(kx_done, 1)
                    chain(ve.tensor_copy(kx[:, :], bank(7, KW, D, 330)))
                    chain(ve.tensor_scalar(kx[:, D:D + 1], kx[:, D:D + 1], dcol[:, 0:1], None, ALU.add))
                    ve.tensor_scalar(kx[:, KW - 1:KW], kx[:, KW - 1:KW], dcol[:, 0:1], None, ALU.add).then_inc(kx_ok, 1)
                if k >= 3 and (k - 3) % EP == EP - 1:
                    c = (k - 3) // EP
                    fed(c)
                    if c in (1, 2, 3):
                        mean(2 * G + c - 1)
                    if c == 2:
                        var(2 * G, 2)
            ve.memset(xe[D:L, :, :], 1.0).then_inc(xe_one, 1)
            mean(3 * G - 1)
            var(3 * G - 2, 2)
            for g in range(G):
                scale(2 * G + g)
            for m in range(2):
                q = ve.memset(hm[m][:, :, CAP:SL], 0.0)
            q.then_inc(hm_zero, 1)
            for q in range(4):
                ve.wait_ge(cv_done, q + 1)
                ve.tensor_tensor(hh[:, :, 16 * q:16 * q + 16], hh[:, :, 16 * q:16 * q + 16],
                                 bank(q, 512, L).rearrange("p (h b) -> p b h", h=16), ALU.add).then_inc(cv_add, 1)
            ve.wait_ge(cv_add, 4)
            mean(3 * G)
            mean(3 * G + 1)
            var(3 * G, 2)
            mean(3 * G + 2)
            mean(3 * G + 3)
            var(3 * G + 2, 2)
            for g in range(G):
                scale(3 * G + g)

            def be(x):
                return x.rearrange("p (b e) -> p b e", e=NE)

            def eb(x):
                return x.rearrange("p (e b) -> p b e", b=B)

            def over(x):
                return x.unsqueeze(2).broadcast_to([L, B, NE])

            gt = [ra[:, i, :] for i in range(6)]
            gb_ = [rb[:, i, :] for i in range(12)]
            ve.wait_ge(gt_done, 1)
            ve.wait_ge(moe_in, 16 * 7)
            chain(ve.tensor_reduce(gb_[0], be(bank(6, 256, L)), X, ALU.max))
            ve.tensor_tensor(be(gt[0]), be(bank(6, 256, L)), over(gb_[0]), ALU.subtract).then_inc(gt_sub, 1)
            ve.wait_ge(gt_exp, 1)
            chain(ve.tensor_reduce(gb_[1], be(gt[0]), X, ALU.add))
            chain(ve.reciprocal(gb_[2], gb_[1]))
            chain(ve.tensor_tensor(be(gt[1]), be(gt[0]), over(gb_[2]), ALU.mult))
            chain(ve.tensor_reduce(gb_[3], be(gt[1]), X, ALU.max))
            chain(ve.tensor_tensor(be(gt[2]), be(gt[1]), over(gb_[3]), ALU.is_equal))
            chain(ve.tensor_tensor(be(gt[2]), be(gt[2]), eb(first), ALU.mult))
            chain(ve.tensor_reduce(gb_[4], be(gt[2]), X, ALU.max))
            chain(ve.tensor_tensor(eb(gt[3]), be(gt[2]), over(gb_[4]), ALU.is_equal))
            ve.tensor_copy(ohb[:, :], gt[3]).then_inc(oh_ok, 1)
            chain(ve.tensor_tensor(gt[4], gt[3], ebase, ALU.mult))
            chain(ve.tensor_reduce(gb_[5], eb(gt[4]), X, ALU.add))
            ve.wait_ge(pre_done, 2)
            chain(ve.tensor_copy(gt[4], bank(1, 256, L)))
            chain(ve.tensor_tensor_scan(gt[5], chained, gt[4], 0.0, ALU.mult, ALU.add))
            chain(ve.tensor_tensor(gt[5], gt[5], gt[4], ALU.subtract))
            chain(ve.tensor_tensor(gt[5], gt[5], bank(0, 256, L), ALU.add))
            chain(ve.tensor_tensor(gt[5], gt[5], gt[3], ALU.mult))
            chain(ve.tensor_reduce(gb_[6], eb(gt[5]), X, ALU.add))
            chain(ve.tensor_scalar(gb_[7], gb_[6], float(CAP) + 0.5, DROP, ALU.is_gt, ALU.mult))
            chain(ve.tensor_tensor(gb_[8], gb_[6], gb_[7], ALU.add))
            chain(ve.tensor_tensor(gb_[8], gb_[8], gb_[5], ALU.add))
            for a in range(2):
                ve.tensor_scalar(ixs[D * a:D * a + D, :], pairs_of(gb_[8][0:D], a), -1.0, None, ALU.add).then_inc(idx_ok, 1)
            ve.tensor_scalar(crow[:, 0, :], gb_[8], -1.0, None, ALU.add).then_inc(idx_ok, 1)
            chain(ve.tensor_scalar(gb_[9], gb_[6], float(CAP), -1.0, ALU.min, ALU.add))
            for a in range(2):
                ve.tensor_tensor(ixg[D * a:D * a + D, :], pairs_of(gb_[9][0:D], a), pairs_of(gb_[5][0:D], a),
                                 ALU.add).then_inc(idx_ok, 1)
            ve.tensor_tensor(crow[:, 1, :], gb_[9], gb_[5], ALU.add).then_inc(idx_ok, 1)
            chain(ve.tensor_scalar(gb_[10], gb_[6], float(CAP) + 0.5, None, ALU.is_lt))
            ve.tensor_tensor(gb_[11], gb_[10], gb_[3], ALU.mult).then_inc(co_ok, 1)
            ve.wait_ge(co_ok, 1)
            for a in range(2):
                chain(ve.tensor_copy(cp_[D * a:D * a + D, :], pairs_of(gb_[11][0:D], a)))

            for e in range(NE + 1):
                if e < NE:
                    ve.wait_ge(f1_done, 2 * e + 2)
                    if e >= 2:
                        ve.wait_ge(f2_done, e - 1)
                    ve.tensor_scalar(hm[e % 2][:, 1, 0:CAP], bank(3, CAP), 0.0, None, ALU.max).then_inc(f1_cv, 1)
                if e >= 1:
                    ve.wait_ge(f2_done, e)
                    q = e - 1
                    ve.tensor_tensor(yb[:, SC * q:SC * q + SC, :],
                                     bank(4 + q % 2, SC * D).rearrange("p (c d) -> p c d", d=D),
                                     b2e[:, q].unsqueeze(1).broadcast_to([128, SC, D]), ALU.add).then_inc(yb_ok, 1)

            def guarded(h, y, probability, ok, r1, r2):
                chain(ve.tensor_tensor(y, y, probability, ALU.mult))
                chain(ve.tensor_scalar(ok, y, 0.0, 0.0, ALU.mult, ALU.is_equal))
                chain(ve.tensor_scalar(r1, y, 0.0, 1.0e4, ALU.is_gt, ALU.mult))
                chain(ve.tensor_scalar(r2, y, 0.0, -1.0e4, ALU.is_lt, ALU.mult))
                chain(ve.tensor_tensor(r1, r1, r2, ALU.add))
                chain(ve.copy_predicated(r1, ok, y))
                ve.tensor_tensor(h, h, r1, ALU.add).then_inc(fin_ok, 1)

            ve.wait_ge(yc_in, 16)
            ve.wait_ge(icc_in, 16)
            ve.wait_ge(hc_in, 16)
            ve.wait_ge(hp_ok, 2)
            guarded(hc, yc, cc[:, 0:1].broadcast_to([B, D]), fin[0:B, 0:D], r1_[0:B, 0:D], r2_[0:B, 0:D])
            for c in range(4):
                ve.wait_ge(yg_in[c], 16 * 4)
                v = slice(4 * c, 4 * c + 4)
                ve.wait_ge(fin_ok, c + 1)
                guarded(hp[:, v, :], yg[:, v, :], cp_[:, v].unsqueeze(2).broadcast_to([128, 4, D]),
                        *(x.rearrange("p (c d) -> p c d", c=4) for x in (fin, r1_, r2_)))

        @block.tensor
        def _(pe):
            def turn_patches(c):
                for k in range(2):
                    pe.wait_ge(xr_ok, 2 * c + k + 1)
                    for g in range(2):
                        r = 4 * c + 2 * k + g
                        if r >= 4:
                            pe.wait_ge(xt_ca if g else xt_cv, (r - 4) // 2 + 1)
                        for x in range(4):
                            m = pe.transpose(bank(r % 4, 128, 128, 128 * x), xr[c % 2][:, k, 4 * g + x, :], ident)
                        m.then_inc(xt_done, 1)

            def embed(g):
                pe.wait_ge(xt_cv, 6 * (g // 2) + 6)
                pe.wait_ge(xt_ca, 6 * (g // 2) + 6)
                if g >= 1:
                    pe.wait_ge(et_cp, g)
                b0 = GB * (g % 2)
                for k in range(KT):
                    m = pe.matmul(bank(4, 512, D), wp[:, k, :],
                                  xt[:, k, b0:b0 + GB].rearrange("p b y x -> p (b y x)"),
                                  start=(k == 0), stop=(k == KT - 1))
                m.then_inc(emb_done, 1)

            def turn_tokens(g):
                pe.wait_ge(et_cp, g + 1)
                if g >= 1:
                    pe.wait_ge(h0_ok, g)
                for b in range(GB):
                    m = pe.transpose(bank(5, D, NPOS, D * b), et[:, g % 2, NPOS * b:NPOS * b + NPOS], ident[0:D, 0:D])
                m.then_inc(lt_done, 1)

            def turn_norm(i):
                pe.wait_ge(ln_u, i + 1)
                for q in range(2):
                    for j in range(4):
                        m = pe.transpose(bank(q, L, D, L * j), uu[:, GB * (i % G) + 4 * q + j, :], ident[0:L, 0:L])
                    m.then_inc(ut_done, 1)

            def keys(g, h):
                if h >= 2:
                    pe.wait_ge(z_cp, NH * g + h - 1)
                else:
                    pe.wait_ge(ut_cp, 2 * g + 2)
                pe.matmul(bank(h % 2, 512, L), mm_[:, h, :], grp(ut, g)[:, :, 0:D],
                          start=True, stop=True).then_inc(z_done, 1)

            def values(g, q):
                if 4 * g + q >= 1:
                    pe.wait_ge(v_cp, 4 * g + q)
                for b in range(2):
                    for a in range(2):
                        m = pe.matmul(ps[D * a:D * a + D, 2, 256 * b:256 * b + 256],
                                      ut[:, GB * g + 2 * q + b, 0:D],
                                      nn_[:, a].rearrange("p h d -> p (h d)"), start=True, stop=True)
                m.then_inc(v_done, 1)

            pe.wait_ge(cst_in, 16)
            turn_patches(0)
            turn_patches(1)
            pe.wait_ge(tok_in, 16 * 6)
            pe.wait_ge(set_p, N_SET_P)
            pe.matmul(bank(6, NPOS, D), w1t[:, :], cxy[:, :], start=True, stop=True).then_inc(r_done, 1)
            turn_patches(2)
            pe.wait_ge(r_cp, 1)
            pe.matmul(bank(7, D, NPOS), rr[:, :], w2t[:, :], start=True, stop=False)
            pe.matmul(bank(7, D, NPOS), ones[:, :], bpt[:, :], start=False, stop=True).then_inc(pos_done, 1)
            pe.wait_ge(wp_in, 16)
            for g in range(2):
                embed(g)
                turn_tokens(g)
            pe.wait_ge(qkv_in, 16 * 7)
            pe.wait_ge(pos_cp, 1)
            for i in range(6):
                for j in range(4):
                    h = 4 * (i % 2) + j
                    m = pe.transpose(bank(WTB[i], L, D, L * j), wqkv[i // 2][:, D * h:D * h + D], ident[0:L, 0:L])
                m.then_inc(wt_done, 1)
            pe.wait_ge(wt_cp, 6)
            for h in range(NH):
                m = pe.matmul(bank(6 + h // 4, L, L, L * (h % 4)), wt[1][:, h, :], wt[0][:, h, :], start=True, stop=True)
                if h % 4 == 3:
                    m.then_inc(mn_done, 1)
            for h in range(NH):
                m = pe.matmul(bank(0, D, L, D * h), wt[2][:, h, :], wu[:, h, :], start=True, stop=True)
            m.then_inc(mn_done, 1)
            pe.wait_ge(s4_in, 16 * N_S4)
            for i in range(4):
                m = pe.transpose(bank(3, 32, 128, 32 * i),
                                 bct[:, i // 2, :, :, i % 2].rearrange("p a n -> p (a n)"), ident[0:32, 0:32])
            m.then_inc(bt_done, 1)
            pe.wait_ge(bt_cp, 1)
            pe.wait_ge(mn_cp, 3)
            for c in range(3, 6):
                turn_patches(c)
            for g in range(2, 4):
                embed(g)
                turn_tokens(g)
            pe.wait_ge(h0_ok, 4)

            turn_norm(0)
            for q in range(4):
                keys(0, 2 * q)
                keys(0, 2 * q + 1)
                values(0, q)

            def scores(p):
                if p >= 2:
                    pe.wait_ge(msk_ok, p - 1)
                pe.wait_ge(z_cp, NH * (p // 4) + NH)
                for a in range(2):
                    b = 2 * p + a
                    m = pe.matmul(ps[D * a:D * a + D, 3 + p % 2, :], ut[:, b, 1:L],
                                  zz[b // GB][:, b % GB].rearrange("p h j -> p (h j)"), start=True, stop=True)
                m.then_inc(s_done, 1)

            def turn_probs(p):
                pe.wait_ge(p_ok, p + 1)
                if p >= 1:
                    pe.wait_ge(pt_cp, p)
                for j in range(4):
                    m = pe.transpose(bank(5, 128, 128, 128 * j), pp[p % 2][:, 128 * j:128 * j + 128], ident)
                m.then_inc(pt_done, 1)

            def attend(p):
                pe.wait_ge(pt_cp, p + 1)
                pe.wait_ge(v_cp, p + 1)
                if p % 4 == 0 and p:
                    pe.wait_ge(o_add, p // 4)
                for a in range(2):
                    b = 2 * p + a
                    for j in range(4):
                        m = pe.matmul(bank(7, D, NPOS, D * (b % GB)), pt[p % 2][:, 128 * j + D * a:128 * j + D * a + D],
                                      vv[:, b, j, :], start=(j == 0), stop=(j == 3))
                    m.then_inc(pv_done, 1)

            for p in range(PAIRS + 1):
                g, r = p // 4 + 1, p % 4
                prep = g < G
                if prep and r == 0:
                    pe.wait_ge(z_cp, NH * g)
                    turn_norm(g)
                if p < PAIRS:
                    scores(p)
                if prep:
                    keys(g, 2 * r)
                if p:
                    turn_probs(p - 1)
                if prep:
                    keys(g, 2 * r + 1)
                    values(g, r)
                if p == 9:
                    pe.wait_ge(bn_in, 160)
                    pe.transpose(bank(6, 40), bnr[:, :], ident[0:40, 0:40]).then_inc(bn_done, 1)
                if 11 <= p < 15:
                    if p == 11:
                        pe.wait_ge(vab_ok, 6)
                        pe.wait_ge(g_prod, 8)
                        pe.wait_ge(bn_cp, 1)
                    for h in range(8 * (p - 11), 8 * (p - 10)):
                        pe.matmul(bank(6, 16, L, 16 * h), g_inv[:, h, :], va[:, h].rearrange("p a c -> p (a c)"),
                                  start=True, stop=False)
                        m = pe.matmul(bank(6, 16, L, 16 * h), g_winv[:, h, :], vb[:, h].rearrange("p a c -> p (a c)"),
                                      start=False, stop=True)
                    if p == 14:
                        m.then_inc(kk_done, 1)
                if p:
                    attend(p - 1)
                if 13 <= p < PAIRS:
                    if p == 13:
                        pe.wait_ge(z_cp, NH * G)
                    else:
                        pe.wait_ge(ut_cp, 2 * (G + p - 13))
                    turn_norm(G + p - 13)

            pe.wait_ge(ut_cp, 4 * G - 2)
            turn_norm(2 * G - 1)

            def layer1(k):
                if k >= 2:
                    pe.wait_ge(r1_ok, k - 1)
                b0, nb = BCH[k // EP]
                a = k % EP
                pe.matmul(bank(k % 2, nb * L), w1r[:, 2 * a:2 * a + 2, :].rearrange("p e h -> p (e h)"),
                          ut[0:D, b0:b0 + nb].rearrange("p b l -> p (b l)"), start=True, stop=True).then_inc(l1_done, 1)

            def layer2(k):
                pe.wait_ge(r1_ok, k + 1)
                if k >= 2:
                    pe.wait_ge(r2_ok, k - 1)
                n = BCH[k // EP][1] * L
                pe.matmul(bank(2 + k % 2, n), w2f[:, k % EP, :], h1[k % 2][:, 0:n],
                          start=True, stop=True).then_inc(l2_done, 1)

            def layer3(k):
                pe.wait_ge(wm_ok, k + 1)
                c, a = k // EP, k % EP
                if a == 0 and c >= 2:
                    pe.wait_ge(y3_cp, c - 1)
                n = BCH[c][1] * L
                pe.matmul(bank(4 + c % 2, n, D), wof[:, a, :], h2w[k % 2][:, 0:n],
                          start=(a == 0), stop=(a == EP - 1)).then_inc(l3_step, 1)

            def turn_mixed(c):
                pe.wait_ge(y3_cp, c + 1)
                if c >= 2:
                    pe.wait_ge(y_add, c - 1)
                if c == 1:
                    pe.wait_ge(kx_ok, 1)
                for b in range(BCH[c][1]):
                    m = pe.transpose(bank(6 + c % 2, D, L, D * b), y3[c % 2][:, L * b:L * b + L], ident[0:D, 0:D])
                m.then_inc(yt_done, 1)

            pe.wait_ge(bn_ok, 2)
            pe.wait_ge(ffn_in, 16 * N_FFN)
            pe.wait_ge(ut_cp, 4 * G)
            pe.wait_ge(msk_ok, PAIRS)
            pe.wait_ge(pt_cp, PAIRS)
            for k in range(EP * len(BCH) + LAG3 + 1):
                if k < EP * len(BCH):
                    layer1(k)
                if 1 <= k <= EP * len(BCH):
                    layer2(k - 1)
                if k == 2:
                    pe.wait_ge(ft_ok, 1)
                    pe.wait_ge(kk_cp, 1)
                    pe.matmul(bank(6, NE, L), feat[:, :], wra[:, :], start=True, stop=True).then_inc(lg_done, 1)
                if k == 3:
                    pe.wait_ge(w_ok, 1)
                    pe.transpose(bank(6, L, NE), rt[:, 16:24], ident[0:L, 0:L]).then_inc(wtt_done, 1)
                    pe.wait_ge(wtt_cp, 1)
                    pe.wait_ge(o_add, G)
                    for a in range(EP):
                        pe.matmul(bank(7, L, 128, L * a), csel[:, 128 * a:128 * a + 128], wtt[:, :], start=True, stop=True)
                    pe.matmul(bank(7, D, L, EP * L), wtt[:, :], bof[:, :], start=True, stop=True).then_inc(wb_done, 1)
                if k == 4:
                    pe.wait_ge(wb_cp, 2)
                    pe.wait_ge(at_ok, 1)
                    pe.matmul(bank(7, KW, D, 330), kt_[:, 8, :], cosx, start=True, stop=False)
                    pe.matmul(bank(7, KW, D, 330), kt_[:, 9, :], sinx, start=False, stop=True).then_inc(kx_done, 1)
                if LAG3 <= k < EP * len(BCH) + LAG3:
                    layer3(k - LAG3)
                if k >= LAG3 + 1 and (k - LAG3 - 1) % EP == EP - 1:
                    turn_mixed((k - LAG3 - 1) // EP)

            pe.wait_ge(ln_u, 3 * G)
            pe.wait_ge(t_in, 16 * L)
            pe.wait_ge(t_zero, 1)
            pe.wait_ge(r2_ok, EP * len(BCH))
            for h in range(D):
                m = pe.matmul(bank(h // 16, B, L, B * (h % 16)), toep[:, h, :], uu[:, :, h], start=True, stop=True)
                if h % 16 == 15:
                    m.then_inc(cv_done, 1)
            pe.wait_ge(cv_add, 4)
            pe.wait_ge(y_add, len(BCH))
            pe.wait_ge(moe_in, 16 * 7)

            def gate(g):
                pe.wait_ge(ut_cp, 2 * (2 * G + g) + 2)
                for b in range(GB * g, GB * g + GB):
                    m = pe.matmul(bank(6, NE, L, NE * b), ut[:, b, :], gwa[:, :], start=True, stop=True)
                if g == G - 1:
                    m.then_inc(gt_done, 1)

            for g in range(G + 1):
                if g < G:
                    if g:
                        pe.wait_ge(ut_cp, 2 * (2 * G + g))
                    pe.wait_ge(ln_u, 3 * G + g + 1)
                    for q in range(2):
                        for j in range(4):
                            m = pe.transpose(bank(q, L, D, L * j), uu[:, GB * g + 4 * q + j, :], ident[0:L, 0:L])
                        m.then_inc(ut_done, 1)
                if g >= 1:
                    gate(g - 1)
            pe.wait_ge(set_v, 2)
            pe.wait_ge(oh_ok, 1)
            pe.matmul(bank(0, 256, L), tribf[:, :], ohb[:, :], start=True, stop=True).then_inc(pre_done, 1)
            pe.matmul(bank(1, 256, L), onebf[:, :], ohb[:, :], start=True, stop=True).then_inc(pre_done, 1)
            pe.wait_ge(idx_ok, 6)

            def turn_slots(e):
                pe.wait_ge(xb_in[e // (NE // 2)], 16)
                if e >= 2:
                    pe.wait_ge(xe_cp, e - 1)
                for c in range(SC):
                    n = min(128, CAP - 128 * c)
                    m = pe.transpose(bank(e % 2, n, D, 128 * c), xb[0:n, SC * e + c, :], ident[0:n, 0:n])
                m.then_inc(xe_done, 1)

            def up_(e):
                pe.wait_ge(xe_cp, e + 1)
                for f in range(2):
                    if e:
                        pe.wait_ge(f1_cv if f else f1_ca, e)
                    pe.matmul(bank(2 + f, CAP), w1e[:, e, 128 * f:128 * f + 128], xe[:, e, 0:CAP],
                              start=True, stop=True).then_inc(f1_done, 1)

            def down(e):
                pe.wait_ge(f1_ca, e + 1)
                pe.wait_ge(f1_cv, e + 1)
                if e >= 2:
                    pe.wait_ge(yb_ok, e - 1)
                for c in range(SC):
                    for f in range(2):
                        m = pe.matmul(bank(4 + e % 2, D, 128, D * c), hm[e % 2][:, f, 128 * c:128 * c + 128],
                                      w2e[:, e, f, :], start=(f == 0), stop=(f == 1))
                m.then_inc(f2_done, 1)

            for e in range(NE + 2):
                if e < NE:
                    turn_slots(e)
                if 1 <= e <= NE:
                    up_(e - 1)
                if e >= 2:
                    down(e - 2)


WTB = (0, 1, 2, 3, 6, 7)
LAG3 = 4
NX = 5
N_S4, N_FFN, N_SET_P = 11, 8, 7

_INS = ["x", "cls_tok", "L0_tok_Wp", "L0_tok_bp", "L0_tok_W1", "L0_tok_b1", "L0_tok_W2", "L0_tok_b2",
        "L0_attn_Wq", "L0_attn_bq", "L0_attn_Wk", "L0_attn_bk", "L0_attn_Wv", "L0_attn_bv", "L0_attn_Wu",
        "L0_attn_bu", "L0_ffn_Wr", "L0_ffn_br", "L0_ffn_W1", "L0_ffn_b1", "L0_ffn_g1", "L0_ffn_be1",
        "L0_ffn_m1", "L0_ffn_v1", "L0_ffn_W2", "L0_ffn_b2", "L0_ffn_g2", "L0_ffn_be2", "L0_ffn_m2",
        "L0_ffn_v2", "L0_ffn_Wo", "L0_ffn_bo", "L1_attn_p_ri", "L1_attn_q_ri", "L1_attn_lambda_ri",
        "L1_attn_B_ri", "L1_attn_Ct_ri", "L1_attn_D", "L1_attn_log_step", "L1_ffn_gate_w",
        "L1_ffn_gate_b", "L1_ffn_w1", "L1_ffn_b1", "L1_ffn_w2", "L1_ffn_b2"]


def kernel(**inputs):
    import concourse.bacc as bacc
    from concourse.bass_utils import run_bass_kernel_spmd

    nc = bacc.Bacc("TRN2", target_bir_lowering=False, num_devices=1)
    arrays, tensors = {}, {}
    for name in _INS:
        arrays[f"in_{name}"] = np.ascontiguousarray(inputs[name])
    for name, table in shape_constants().items():
        arrays[f"in_{name}"] = table
    for key, a in arrays.items():
        tensors[key[3:]] = nc.dram_tensor(key, a.shape, mybir.dt.from_np(a.dtype), kind="ExternalInput").ap()
    out = nc.dram_tensor("out", (B, L, D), F32, kind="ExternalOutput").ap()
    build(nc, tensors, out)
    r = run_bass_kernel_spmd(nc, [arrays], core_ids=[0])
    return r.results[0]["out"]
```

```python
from contextlib import ExitStack

import numpy as np

import concourse.bass as bass
from concourse import mybir

B, CH, IMG, P = 32, 3, 128, 16
D = 64
NG = IMG // P
NPOS = NG * NG
L = NPOS + 1
KT = CH * P * P // 128
NH = 8
G = 4
GB = B // G
PAIRS = B // 2
NE = 8
EP = NE // 2
F = 256
CAP = -(-5 * B * L // (4 * NE))
SC = -(-CAP // 128)
SP = -(-CAP // SC)
SL = SC * SP
DROP = 1.0e6
LN_EPS, BN_EPS = 1e-5, 1e-3
RSC = 2.0 ** -24
KW = D + L + 1
BCH = [(0, 7), (7, 7), (14, 6), (20, 6), (26, 6)]

F32 = mybir.dt.float32
BF16 = mybir.dt.bfloat16
U32 = mybir.dt.uint32
ALU = mybir.AluOpType
ACT = mybir.ActivationFunctionType
X = mybir.AxisListType.X


def shape_constants():
    l = np.arange(L)
    tau = np.tan(np.pi * l / L)
    c128 = np.zeros((128, 128 + L + 128), np.float32)
    c128[:, :128] = np.eye(128)
    c128[:, 128:128 + L] = 2.0 * RSC * tau[None]
    i, j = np.arange(128)[:, None] % 64, np.arange(64)[None]
    c128[:, 128 + L:192 + L] = np.where(j <= i, 0.0, -1.0e30)
    c128[:, 192 + L:] = i == j
    k = np.concatenate([np.full(D, -1), np.arange(L), [0]])
    ang = 2 * np.pi * ((l[:, None] * np.maximum(k, 0)[None]) % L) / L
    used = (k >= 0)[None] / L
    pos = np.concatenate([np.arange(1, L), [0]])
    tri = (pos[:, None] <= pos[None]).astype(np.float64)
    chained = np.tile((np.arange(B // 2) > 0) * 1.0, NE)
    first = np.tile(NE - np.arange(NE), B // 2)
    cl = np.concatenate([np.cos(ang) * used, np.sin(ang) * used, tau[:, None], tri], axis=1)
    cr = np.tile(np.concatenate([chained, first]), (L, 1))
    n = np.arange(NPOS)
    xy = np.stack([n // NG / (NG - 1), n % NG / (NG - 1), np.ones(NPOS)])
    sel = np.zeros((NE, EP, 128))
    for e in range(NE):
        sel[e, e // 2, 64 * (e % 2):64 * (e % 2) + 64] = 1.0
    return {"c128": c128, "cl": cl.astype(np.float32), "cr": cr.astype(np.float32), "cxy": xy.astype(np.float32),
            "csel": sel.reshape(NE, EP * 128).astype(np.float32)}


def build(nc, t, out):
    kd = nc.dram_tensor("kernel_windows", (L, D, L), F32, kind="Internal").ap()
    slots = nc.dram_tensor("expert_slots", (NE * SL, D), F32, kind="Internal").ap()
    yslots = nc.dram_tensor("expert_out", (NE * SL, D), F32, kind="Internal").ap()

    ctx = ExitStack()
    with ctx:
        def sb(name, shape, dt=F32):
            return ctx.enter_context(nc.sbuf_tensor(name, shape, dt))

        def sem(name):
            return ctx.enter_context(nc.semaphore(name))

        ps = ctx.enter_context(nc.psum_tensor("ps", [128, 8, 512], F32))

        rx = sb("rx", [128, NX * 2048])
        rxt = sb("rxt", [128, KT * 1024])
        rz = sb("rz", [128, 8192])
        rv = sb("rv", [128, 8192])
        rs = sb("rs", [128, 3 * 32 * L])

        ximg = rx[:, :].rearrange("p (c y x) -> p c y x", c=NX, y=P)
        xt = rxt[:, :].rearrange("p (k b y x) -> p k b y x", k=KT, y=NG, x=NG)
        et = rx[:, 2048:3072].rearrange("p (a n) -> p a n", a=2)
        zz = [r.rearrange("p (b h j) -> p b h j", b=GB, h=NH) for r in
              (rz[:, 0:4096], rz[:, 4096:8192], rx[:, 0:4096], rx[:, 4096:8192])]
        vv = rv[:, :].rearrange("p (b h d) -> p b h d", b=B, h=NH // 2)
        xr = [rv[:, 4096 + 2048 * i:6144 + 2048 * i].rearrange("p (k g n) -> p k g n", k=2, g=NG) for i in range(2)]
        g_w = rs[:, 0:32 * L].rearrange("p (h l) -> p h l", h=32)
        g_inv = rs[:, 32 * L:64 * L].rearrange("p (h l) -> p h l", h=32)
        g_winv = rs[:, 64 * L:96 * L].rearrange("p (h l) -> p h l", h=32)
        sx = [rxt[:, 4160 + 512 * i:4672 + 512 * i] for i in range(3)]
        pp = [rx[:, 8192 + 512 * i:8704 + 512 * i] for i in range(2)]
        pt = [rx[:, 9216 + 512 * i:9728 + 512 * i] for i in range(2)]
        toep = rxt[0:L, 0:D * L].rearrange("p (h l) -> p h l", h=D)
        h1 = [rv[:, 512 * i:512 * i + 512] for i in range(2)]
        h2 = [rv[:, q + 512 * i:q + 512 + 512 * i] for q in (1024, 6144) for i in range(4)]
        h2w = [rv[:, 3072 + 512 * i:3584 + 512 * i] for i in range(4)]
        y3 = [rv[:, 5120 + 512 * i:5632 + 512 * i] for i in range(2)]
        cls_conv = rv[D:L, 6144:6144 + B * D].rearrange("p (b d) -> p b d", b=B)
        xb = rv[:, 5120:5120 + NE * SC * D].rearrange("p (c d) -> p c d", d=D)
        yb = rv[:, 0:NE * SC * D].rearrange("p (c d) -> p c d", d=D)
        xe = rz[:, 0:NE * SL].rearrange("p (e s) -> p e s", e=NE)
        hm = [rz[:, 4096 + 768 * i:4864 + 768 * i].rearrange("p (f s) -> p f s", f=2) for i in range(2)]
        up = rx[:, 0:PAIRS * D].rearrange("p (c d) -> p c d", d=D)
        yg = rx[:, 1024:1024 + PAIRS * D].rearrange("p (c d) -> p c d", d=D)
        hp = rx[:, 2048:2048 + PAIRS * D].rearrange("p (c d) -> p c d", d=D)
        uc, yc, hc = (rx[0:B, 3072 + D * i:3072 + D * i + D] for i in range(3))
        fin_, r1_, r2_ = (rx[:, 3328 + 384 * i:3712 + 384 * i] for i in range(3))
        fin = fin_.bitcast(U32)
        w1e = rx[:, 8192:8192 + NE * F].rearrange("p (e f) -> p e f", e=NE)
        w2e = rxt[:, 4160:4160 + NE * 2 * D].rearrange("p (e f d) -> p e f d", e=NE, f=2)
        b2e = rxt[:, 5184:5184 + NE * D].rearrange("p (e d) -> p e d", e=NE)

        c128 = sb("c128_sb", [128, 128 + L + 128])
        ident, ttab, cmask = c128[:, 0:128], c128[:, 128:128 + L], c128[:, 128 + L:192 + L]
        ident2 = c128[:, 192 + L:]
        cl = sb("cl_sb", [L, 2 * KW + 1 + L])
        cr = rs[0:L, 2048:2048 + NE * B]
        o = 2 * KW + 1
        cosx, sinx, tau, tri = cl[:, 0:KW], cl[:, KW:2 * KW], cl[:, o - 1:o], cl[:, o:o + L]
        chained, first = cr[:, 0:NE * B // 2], cr[:, NE * B // 2:]
        cxy = sb("cxy_sb", [3, NPOS])
        tribf = sb("tribf", [L, L], BF16)
        onebf = sb("onebf", [L, L], BF16)
        ones = sb("ones", [1, 64])
        expo = sb("expo", [128, 2 * GB])
        hh = sb("hh", [L, B, D])
        uu = sb("uu", [L, B, D])
        bst = sb("bst", [L, 4 * G, GB, 6])
        ut = sb("ut", [128, B, L])
        lsum, ldif, lsqd, lmean, lvs, lrs = (sb(n, [L, 4 * B, k]) for n, k in (
            ("lsum", 2), ("ldif", 1), ("lsqd", 1), ("lmean", 1), ("lvs", 1), ("lrs", 1)))
        wp = sb("wp", [128, KT, D])
        w1t, w2t, bpt = sb("w1t", [3, D]), sb("w2t", [L, D]), sb("bpt", [1, D])
        rr, posb = sb("rr", [L, NPOS]), sb("posb", [NPOS, D])
        wqkv = [rz[0:L, 512 * i:512 * i + 512] for i in range(3)]
        wu = rz[0:D, 1536:2048].rearrange("p (h d) -> p h d", h=NH)
        wt = [rz[0:D, 2048 + NH * L * i:2048 + NH * L * (i + 1)].rearrange("p (h l) -> p h l", h=NH) for i in range(3)]
        mm_ = sb("mm_", [128, NH, 128])
        nn_ = sb("nn_", [128, 2, NH // 2, D])
        bub = sb("bub", [L, D])
        mx, rc = sb("mx", [128, 3, NH]), sb("rc", [128, 3, NH])
        lam, pri, qri = sb("lam", [128, 2]), sb("pri", [128, 2]), sb("qri", [128, 2])
        bct = rz[0:32, 3616:4128].rearrange("p (q a n r) -> p q a n r", q=2, a=2, r=2)
        bc = sb("bc", [128, 4, 32])
        lsb, gg = sb("lsb", [128, 32]), sb("gg", [128, 32])
        dcol = sb("dcol", [D, 1])
        ws = sb("ws", [128, 8])
        wc = sb("wc", [128, 4, 2, 32])
        wtmp = sb("wtmp", [128, 2, 32])
        zeros = sb("zeros", [128, 256])
        va, vb = sb("va", [128, 32, 2, 8]), sb("vb", [128, 32, 2, 8])
        ks = rs[0:L, 4864:4864 + 8 * D].rearrange("p (c h) -> p c h", c=8)
        kt_ = rs[0:L, 5376:5376 + 10 * D].rearrange("p (c h) -> p c h", c=10)
        kx = sb("kx", [D, KW])
        bnr = sb("bnr", [40, 128])
        bn = sb("bn", [128, 10, EP])
        bna = sb("bna", [128, 4, EP])
        wra = sb("wra", [L, NE])
        w1r = rs[:, 3072:3584].rearrange("p (e h) -> p e h", e=NE)
        w2f = rs[:, 3584:4096].rearrange("p (a k) -> p a k", a=EP)
        wof = rs[:, 4096:4352].rearrange("p (a d) -> p a d", a=EP)
        csel = rs[0:NE, 4352:4864]
        bof = sb("bof", [NE, D])
        feat = sb("feat", [L, L])
        fpart = rs[0:L, 0:L * G].rearrange("p (l g) -> p l g", g=G)
        rt = sb("rt", [L, 40])
        wtt = sb("wtt", [NE, L])
        wb = sb("wb", [128, EP, L])
        bow = sb("bow", [L, D])
        gwa = sb("gwa", [L, NE])
        ra = rs[0:L, 0:1536].rearrange("p (a n) -> p a n", a=6)
        ohb = sb("ohb", [L, 256], BF16)
        rb = rs[0:L, 1536:1536 + 12 * B].rearrange("p (a b) -> p a b", a=12)
        ixs, ixg = sb("ixs", [128, PAIRS], U32), sb("ixg", [128, PAIRS], U32)
        crow = sb("crow", [L, 2, B], U32)
        ics, icg, cc = sb("ics", [B, 1], U32), sb("icg", [B, 1], U32), sb("cc", [B, 1])
        cp_ = sb("cp_", [128, PAIRS])

        cl_in, ft_part = sem("cl_in"), sem("ft_part")
        cst_in, tok_in, qkv_in, s4_in, cls_in = (sem(n) for n in ("cst_in", "tok_in", "qkv_in", "s4_in", "cls_in"))
        bn_in, ffn_in, moe_in = sem("bn_in"), sem("ffn_in"), sem("moe_in")
        x_in = [sem(f"x_in{i}") for i in range(2 * CH)]
        wp_in = sem("wp_in")
        w2_zero = sem("w2_zero")
        set_v, set_p = sem("set_v"), sem("set_p")
        wt_done, wt_cp, mn_done, mn_cp = sem("wt_done"), sem("wt_cp"), sem("mn_done"), sem("mn_cp")
        r_done, r_cp, pos_done, pos_cp = sem("r_done"), sem("r_cp"), sem("pos_done"), sem("pos_cp")
        bt_done, bt_cp = sem("bt_done"), sem("bt_cp")
        bn_done, bn_cp, bn_pow, bn_ok = sem("bn_done"), sem("bn_cp"), sem("bn_pow"), sem("bn_ok")
        vstep = sem("vstep")
        g_exp, g_outer, g_shift, g_sq, g_recip, g_prod = (sem(n) for n in (
            "g_exp", "g_outer", "g_shift", "g_sq", "g_recip", "g_prod"))
        g_den, vab_ok, kk_done, kk_cp, at_ok, kx_done, kx_ok = (sem(n) for n in (
            "g_den", "vab_ok", "kk_done", "kk_cp", "at_ok", "kx_done", "kx_ok"))
        kd_out, t_in, t_zero = sem("kd_out"), sem("t_in"), sem("t_zero")
        xr_ok, xt_done, xt_cv, xt_ca = sem("xr_ok"), sem("xt_done"), sem("xt_cv"), sem("xt_ca")
        emb_done, et_cp, lt_done, h0_ok = sem("emb_done"), sem("et_cp"), sem("lt_done"), sem("h0_ok")
        ln_mean, ln_vs, ln_cen, ln_pow, ln_u = (sem(n) for n in ("ln_mean", "ln_vs", "ln_cen", "ln_pow", "ln_u"))
        ut_done, ut_cp = sem("ut_done"), sem("ut_cp")
        z_done, z_cp, v_done, v_cp = sem("z_done"), sem("z_cp"), sem("v_done"), sem("v_cp")
        s_done, msk_ok, mx_ok, sub_ok, exp_ok, sum_ok, rc_ok, p_ok = (sem(n) for n in (
            "s_done", "msk_ok", "mx_ok", "sub_ok", "exp_ok", "sum_ok", "rc_ok", "p_ok"))
        pt_done, pt_cp, pv_done, bu_add, o_add = (sem(n) for n in ("pt_done", "pt_cp", "pv_done", "bu_add", "o_add"))
        ft_ok, lg_done, rt_exp, w_ok, wtt_done, wtt_cp, wb_done, wb_cp, bow_add = (sem(n) for n in (
            "ft_ok", "lg_done", "rt_exp", "w_ok", "wtt_done", "wtt_cp", "wb_done", "wb_cp", "bow_add"))
        l1_done, r1_ok, l2_done, r2_ok, wm_ok, l3_step, y3_cp, yt_done, y_add = (sem(n) for n in (
            "l1_done", "r1_ok", "l2_done", "r2_ok", "wm_ok", "l3_step", "y3_cp", "yt_done", "y_add"))
        cv_done, cv_add, cls_add = sem("cv_done"), sem("cv_add"), sem("cls_add")
        gt_done, gt_sub, gt_exp, oh_ok, pre_done, idx_ok, co_ok = (sem(n) for n in (
            "gt_done", "gt_sub", "gt_exp", "oh_ok", "pre_done", "idx_ok", "co_ok"))
        ixg_ok = sem("ixg_ok")
        z_out, sc_near, sc_out, xe_one, w1_zero = sem("z_out"), sem("sc_near"), sem("sc_out"), sem("xe_one"), sem("w1_zero")
        xb_in = [sem(f"xb_in{i}") for i in range(4)]
        xe_done, xe_cp, f1_done, f1_ca, f1_cv, f2_done, yb_ok, y_out = (sem(n) for n in (
            "xe_done", "xe_cp", "f1_done", "f1_ca", "f1_cv", "f2_done", "yb_ok", "y_out"))
        yg_in = [sem(f"yg_in{g}") for g in range(G)]
        yc_in, uc_in, hc_in, ic_in, icc_in = sem("yc_in"), sem("uc_in"), sem("hc_in"), sem("ic_in"), sem("icc_in")
        up_ok, hp_ok, fin_ok, o_out = sem("up_ok"), sem("hp_ok"), sem("fin_ok"), sem("o_out")

        def bank(i, n=512, rows=128, at=0):
            return ps[0:rows, i, at:at + n]

        def grp(x, g):
            return x[:, GB * g:GB * g + GB]

        def pairs_of(x, a, g=0, n=B):
            return x[:, GB * g + a:GB * g + n:2]

        def variances(i):
            return i + 1 if i <= 2 * G else i

        def turn_bank(i, q):
            return {2 * G - 2: 4 + q, 2 * G - 1: 5 + 2 * q}.get(i, q)

        def by_scalar(r):
            return r % 2 == 1 or (r >= 4 * CH and r % 4 == 2)

        def patches_moved(r, scalar):
            return sum(by_scalar(i) == scalar for i in range(r + 1))

        def move_patches(eng, r):
            c, k, g = r // 4, (r % 4) // 2, r % 2
            out_ = xt[:, 2 * (c % CH) + k, :, :, 4 * g:4 * g + 4].rearrange("p b y x -> p x (b y)")
            in_ = bank(r % 4).rearrange("p (x n) -> p x n", x=4)
            return eng.copy(out_, in_) if by_scalar(r) else eng.tensor_copy(out_, in_)

        block = ctx.enter_context(nc.Block())

        @block.sync
        def _(sp):
            for c in range(2 * CH):
                src = t["x"][16 * (c // CH):16 * (c // CH) + 16, c % CH].rearrange("b (g y) x -> b g (y x)", g=NG)
                if c >= NX:
                    sp.wait_ge(xr_ok, 2 * (c - NX + 1))
                q = 2048 * (c % NX)
                sp.dma_start(rx[:, q:q + 2048], src).then_inc(x_in[c], 16)
            sp.dma_start(cl[:, :], t["cl"]).then_inc(cl_in, 16)
            for j, name in enumerate(("v1", "g1", "b1", "m1", "be1", "v2", "g2", "b2", "m2", "be2")):
                sp.dma_start(bnr[EP * j:EP * j + EP, :],
                             t["L0_ffn_" + name].rearrange("(p e) h -> p (e h)", e=2)).then_inc(bn_in, 16)
            sp.wait_ge(set_p, N_SET_P)
            for q in range(NE * SC // 4):
                sp.dma_start(slots.rearrange("(p q c) d -> q p (c d)", p=SP, c=4)[q], zeros[0:SP, :]).then_inc(z_out, 16)
            sp.dma_start(wra[0:D, :], t["L0_ffn_Wr"]).then_inc(ffn_in, 16)
            sp.dma_start(wra[D:L, :], t["L0_ffn_br"].unsqueeze(0)).then_inc(ffn_in, 16)
            sp.dma_start(bof[:, :], t["L0_ffn_bo"]).then_inc(ffn_in, 16)
            sp.wait_ge(kk_done, 1)
            sp.dma_start(w1r[0:D, :, :], t["L0_ffn_W1"].rearrange("e d h -> d e h")).then_inc(ffn_in, 16)
            sp.dma_start(wof[:, :, :], t["L0_ffn_Wo"].rearrange("(p e) h d -> (e h) p d", e=2)).then_inc(ffn_in, 16)
            sp.dma_start(csel[:, :], t["csel"]).then_inc(ffn_in, 16)
            sp.wait_ge(w2_zero, 1)
            for q in range(2):
                sp.dma_start(w2f[D * q:D * q + D, :, D * q:D * q + D],
                             t["L0_ffn_W2"].rearrange("(p e) h k -> e h p k", e=2)[q]).then_inc(ffn_in, 16)
            sp.wait_ge(kx_ok, 1)
            windows = bass.AP(kx[:, :].tensor, kx[:, D:D + 1].offset, [kx[:, :].ap[0], [-1, D], [1, D]])
            sp.dma_start(kd[0:D, :, 0:D].rearrange("m h l -> h m l"), windows).then_inc(kd_out, 16)
            sp.dma_start(kd[D:L].rearrange("a h l -> h (a l)"), kx[:, D + 1:KW]).then_inc(kd_out, 16)
            sp.wait_ge(kd_out, 32)
            sp.dma_start(toep[0:D, :, 0:D], kd[0:D, :, 0:D]).then_inc(t_in, 16)
            sp.dma_start(toep[D:L, :, :], kd[D:L]).then_inc(t_in, 16)
            sp.wait_ge(pv_done, PAIRS)
            sp.dma_start(cr, t["cr"]).then_inc(moe_in, 16)
            sp.dma_start(gwa[0:D, :], t["L1_ffn_gate_w"]).then_inc(moe_in, 16)
            sp.dma_start(gwa[D:L, :], t["L1_ffn_gate_b"].unsqueeze(0)).then_inc(moe_in, 16)
            sp.wait_ge(w1_zero, 1)
            sp.dma_start(w1e[0:D, :, :], t["L1_ffn_w1"].rearrange("e d f -> d e f")).then_inc(moe_in, 16)
            sp.dma_start(w1e[D:L, :, :], t["L1_ffn_b1"].unsqueeze(0)).then_inc(moe_in, 16)
            sp.dma_start(w2e[:, :, :, :], t["L1_ffn_w2"].rearrange("e (f p) d -> p e f d", p=128)).then_inc(moe_in, 16)
            sp.dma_start(b2e[:, :, :], t["L1_ffn_b2"].partition_broadcast(128)).then_inc(moe_in, 16)
            sp.wait_ge(ln_u, 4 * G)
            sp.dma_start(uc, uu[D:L, :, :]).then_inc(uc_in, 16)
            sp.dma_start(hc, hh[D:L, :, :]).then_inc(hc_in, 16)
            sp.wait_ge(idx_ok, 5)
            sp.dma_start(ics[:, :], crow[D:L, 0, :]).then_inc(ic_in, 16)
            sp.wait_ge(ixg_ok, 3)
            sp.dma_start(icg[:, :], crow[D:L, 1, :]).then_inc(ic_in, 16)
            sp.wait_ge(co_ok, 1)
            sp.dma_start(cc[:, :], rb[D:L, 10, :]).then_inc(icc_in, 16)
            sp.wait_ge(sc_near, 16)
            sp.wait_ge(sc_out, 16 * PAIRS)
            for q in range(4):
                n = NE // 4
                sp.dma_start(xb[0:SP, SC * n * q:SC * n * (q + 1), :].rearrange("p (e c) d -> p e (c d)", e=n),
                             slots[SL * n * q:SL * n * (q + 1), :].rearrange("(e p c) d -> p e (c d)", e=n, c=SC)[0:SP]
                             ).then_inc(xb_in[q], 16)
            for e in range(NE):
                sp.wait_ge(yb_ok, e + 1)
                sp.dma_start(yslots[SL * e:SL * e + SL, :].rearrange("(p c) d -> p (c d)", c=SC)[0:SP],
                             yb[0:SP, SC * e:SC * e + SC, :].rearrange("p c d -> p (c d)")).then_inc(y_out, 16)
            sp.wait_ge(fin_ok, 1)
            sp.dma_start(out[:, 0, :], hc).then_inc(o_out, 16)
            for c, (p0, n) in enumerate(OCH):
                sp.wait_ge(fin_ok, c + 2)
                for a in range(2):
                    sp.dma_start(out[2 * p0 + a:2 * (p0 + n):2, 1:L, :].rearrange("b l d -> l b d"),
                                 hp[D * a:D * a + D, p0:p0 + n, :]).then_inc(o_out, 16)
            sp.wait_ge(o_out, 16 * 9)

        @block.gpsimd
        def _(po):
            po.dma_start(cxy[:, :], t["cxy"]).then_inc(tok_in, 16)
            po.dma_start(w1t[0:2, :], t["L0_tok_W1"]).then_inc(tok_in, 16)
            po.dma_start(w1t[2:3, :], t["L0_tok_b1"].unsqueeze(0)).then_inc(tok_in, 16)
            po.dma_start(w2t[0:D, :], t["L0_tok_W2"]).then_inc(tok_in, 16)
            po.dma_start(w2t[D:L, :], t["L0_tok_b2"].unsqueeze(0)).then_inc(tok_in, 16)
            po.dma_start(bpt[:, :], t["L0_tok_bp"].unsqueeze(0)).then_inc(tok_in, 16)
            for n, (tile, value) in enumerate(((ones[:, :], 1.0), (rr[D:L, :], 1.0), (expo[:, :], -0.5),
                                (mm_[:, :, :], 0.0), (nn_[:, :, :, :], 0.0), (ut[D:128, :, :], 0.0),
                                (ut[D:L, :, :], 1.0), (zeros[:, :], 0.0),
                                (va[:, :, :, :], 0.0), (vb[:, :, :, :], 0.0))):
                po.memset(tile, value).then_inc(set_p, 1)
                po.wait_ge(set_p, n + 1)
            po.dma_start(hh[D:L, :, :], t["cls_tok"].rearrange("a b d -> (a b) d").broadcast_to([B, D]).unsqueeze(0)
                         ).then_inc(cls_in, 16)
            po.dma_start(bub[:, :], t["L0_attn_bu"].partition_broadcast(L)).then_inc(cls_in, 16)
            for r, name in ((lam, "lambda"), (pri, "p"), (qri, "q")):
                for q in range(2):
                    po.dma_start(r[D * q:D * q + D, :], t[f"L1_attn_{name}_ri"]).then_inc(s4_in, 16)
            for q in range(2):
                po.dma_start(lsb[D * q:D * q + D, :],
                             t["L1_attn_log_step"][32 * q:32 * q + 32].partition_broadcast(D)).then_inc(s4_in, 16)
            for q, name in enumerate(("B", "Ct")):
                po.dma_start(bct[:, q], t[f"L1_attn_{name}_ri"].rearrange("(a h) n r -> h a n r", a=2)).then_inc(s4_in, 16)
            po.dma_start(dcol[:, :], t["L1_attn_D"].rearrange("a b h -> (a b h)").unsqueeze(1)).then_inc(s4_in, 16)

            def centre(i):
                po.wait_ge(ln_mean, i + 1)
                g = i % G
                if i >= 3 * G:
                    po.wait_ge(cv_done, 4)
                elif i >= G:
                    po.wait_ge(ut_done, 2 * (i - G) + 2)
                po.tensor_tensor(grp(uu, g), grp(hh, g), lmean[:, GB * i:GB * i + GB, :].broadcast_to([L, GB, D]),
                                 ALU.subtract).then_inc(ln_cen, 1)

            def root(i, n):
                po.wait_ge(ln_vs, variances(i))
                v = slice(GB * i, GB * (i + n))
                po.tensor_tensor(lrs[:, v, 0], lvs[:, v, 0], expo[0:L, 0:GB * n], ALU.pow).then_inc(ln_pow, 1)

            def norm(p):
                po.wait_ge(rc_ok, p + 1)
                if p >= 2:
                    po.wait_ge(pt_done, p - 1)
                po.tensor_tensor(pp[p % 2].rearrange("p (h j) -> p h j", h=NH),
                                 sx[p % 3].rearrange("p (h j) -> p h j", h=NH),
                                 rc[:, p % 3].unsqueeze(2).broadcast_to([128, NH, 64]), ALU.mult).then_inc(p_ok, 1)

            def bias_u(g):
                po.wait_ge(ln_cen, g + 1)
                po.wait_ge(cls_in, 32)
                po.tensor_tensor(grp(hh, g), grp(hh, g), bub[:, :].unsqueeze(1).broadcast_to([L, GB, D]),
                                 ALU.add).then_inc(bu_add, 1)

            for g in range(G):
                centre(g)
                root(g, 1)
                if g == 1:
                    po.wait_ge(g_exp, 1)
                    po.wait_ge(cst_in, 16)
                    po.tensor_tensor(g_w, gg[:, :].unsqueeze(2).broadcast_to([128, 32, L]),
                                     ttab.unsqueeze(1).broadcast_to([128, 32, L]), ALU.mult).then_inc(g_outer, 1)
            for g in range(G):
                bias_u(g)
            for p in range(PAIRS + 4):
                if p == 13:
                    po.wait_ge(kk_done, 1)
                    po.memset(w2f[:, :, :], 0.0).then_inc(w2_zero, 1)
                    po.wait_ge(w2_zero, 1)
                    po.memset(w1r[D:128, :, :], 0.0).then_inc(w2_zero, 1)
                    po.wait_ge(w2_zero, 2)
                if p < PAIRS:
                    norm(p)
                if 1 <= p <= 8:
                    po.wait_ge(g_recip, p)
                    v = slice(4 * (p - 1), 4 * p)
                    po.tensor_tensor(g_winv[:, v], g_w[:, v], g_inv[:, v], ALU.mult).then_inc(g_prod, 1)
                if p == 8:
                    po.wait_ge(bn_cp, 3)
                    for i in range(2):
                        po.tensor_tensor(bna[:, 2 * i, :], bn[:, 5 * i, :], expo[:, 0:EP], ALU.pow).then_inc(bn_pow, 1)
                if p in CENTRE2:
                    centre(G + CENTRE2.index(p))
                    root(G + CENTRE2.index(p), 1)
            po.wait_ge(wb_cp, 2)
            for g in range(G):
                po.wait_ge(ln_cen, G + g + 1)
                po.tensor_tensor(grp(hh, g), grp(hh, g), bow[:, :].unsqueeze(1).broadcast_to([L, GB, D]),
                                 ALU.add).then_inc(bow_add, 1)
            po.wait_ge(bow_add, G)
            po.memset(xe[D:128, :, :], 0.0).then_inc(xe_one, 1)
            po.wait_ge(xe_one, 1)
            po.memset(xe[D:L, :, :], 1.0).then_inc(xe_one, 1)
            po.wait_ge(xe_one, 2)
            po.memset(w1e[D:128, :, :], 0.0).then_inc(w1_zero, 1)
            po.wait_ge(w1_zero, 1)
            for i, n in ((2 * G, 2), *((j, 1) for j in range(2 * G + 2, 4 * G))):
                if i not in (3 * G - 1, 3 * G + 1):
                    centre(i)
                if n == 2:
                    centre(i + 1)
                root(i, n)
            po.wait_ge(z_out, 16 * NE * SC // 4)
            for c in range(PAIRS):
                if c % (PAIRS // 2) == 0:
                    po.wait_ge(up_ok, G * (2 * c // PAIRS + 1))
                    po.wait_ge(idx_ok, 4 * c // PAIRS + 2)
                po.indirect_dma_start(out=slots, out_offset=bass.IndirectOffsetOnAxis(ap=ixs[:, c:c + 1], axis=0),
                                      in_=up[:, c, :], in_offset=None, bounds_check=NE * SL - 1,
                                      oob_is_err=False).then_inc(sc_near if c == PAIRS - 3 else sc_out, 16)
            po.wait_ge(uc_in, 16)
            po.wait_ge(ic_in, 32)
            po.indirect_dma_start(out=slots, out_offset=bass.IndirectOffsetOnAxis(ap=ics[:, :], axis=0),
                                  in_=uc, in_offset=None, bounds_check=NE * SL - 1,
                                  oob_is_err=False).then_inc(sc_out, 16)

            def chunk_of(c):
                return sum(p0 <= c for p0, _ in OCH) - 1

            po.wait_ge(y_out, 16 * NE)
            po.indirect_dma_start(out=yc, out_offset=None, in_=yslots,
                                  in_offset=bass.IndirectOffsetOnAxis(ap=icg[:, :], axis=0),
                                  bounds_check=NE * SL - 1, oob_is_err=False).then_inc(yc_in, 16)
            for c in range(PAIRS):
                po.indirect_dma_start(out=yg[:, c, :], out_offset=None, in_=yslots,
                                      in_offset=bass.IndirectOffsetOnAxis(ap=ixg[:, c:c + 1], axis=0),
                                      bounds_check=NE * SL - 1, oob_is_err=False).then_inc(yg_in[chunk_of(c)], 16)

        @block.scalar
        def _(sc):
            sc.dma_start(c128[:, :], t["c128"]).then_inc(cst_in, 16)
            sc.dma_start(wp[:, :, :], t["L0_tok_Wp"].rearrange("(k p) d -> p k d", p=128)).then_inc(wp_in, 16)
            for w, n in zip(wqkv, "qkv"):
                sc.dma_start(w[0:D, :], t[f"L0_attn_W{n}"]).then_inc(qkv_in, 16)
                sc.dma_start(w[D:L, :], t[f"L0_attn_b{n}"].unsqueeze(0)).then_inc(qkv_in, 16)
            sc.dma_start(wu[:, :, :], t["L0_attn_Wu"].rearrange("(h e) d -> e h d", h=NH)).then_inc(qkv_in, 16)

            def patches(c):
                for r in range(4 * c, 4 * c + 4):
                    if by_scalar(r):
                        sc.wait_ge(xt_done, r + 1)
                        move_patches(sc, r).then_inc(xt_ca, 1)

            def embedded(a):
                sc.wait_ge(emb_done, a + 1)
                sc.copy(et[:, a, :], bank(4)).then_inc(et_cp, 1)

            def turned(i, attention):
                for q in range(2):
                    sc.wait_ge(ut_done, 2 * i + q + 1)
                    if i == 0 and q == 0:
                        sc.wait_ge(set_p, N_SET_P)
                    b0 = GB * (i % G) + 4 * q
                    src = bank(turn_bank(i, q), 4 * L, D).rearrange("p (b l) -> p b l", b=4)
                    if attention:
                        sc.copy(ut[0:D, b0:b0 + 4, 1:L], src[:, :, 0:D])
                        sc.copy(ut[0:D, b0:b0 + 4, 0:1], src[:, :, D:L]).then_inc(ut_cp, 1)
                    else:
                        sc.copy(ut[0:D, b0:b0 + 4, :], src).then_inc(ut_cp, 1)

            def keys(g, h):
                sc.wait_ge(z_done, NH * g + h + 1)
                sc.copy(zz[g][:, :, h, :], bank(h % 2).rearrange("p (b j) -> p b j", b=GB)).then_inc(z_cp, 1)

            def values(g, q):
                sc.wait_ge(v_done, 4 * g + q + 1)
                b0 = GB * g + 2 * q
                sc.copy(vv[:, b0:b0 + 2].rearrange("p b h d -> p (b h d)"), bank(2)).then_inc(v_cp, 1)

            def expo_(p):
                sc.wait_ge(sub_ok, p + 1)
                sc.activation(sx[p % 3], sx[p % 3], ACT.Exp, scale=float(D) ** -0.5).then_inc(exp_ok, 1)

            def ptcopy(p):
                sc.wait_ge(pt_done, p + 1)
                if p >= 2:
                    sc.wait_ge(pv_done, p - 1)
                sc.copy(pt[p % 2], bank(5)).then_inc(pt_cp, 1)

            def relu1(k):
                sc.wait_ge(l1_done, k + 1)
                if k >= 2:
                    sc.wait_ge(l2_done, k - 1)
                if k == 0:
                    sc.wait_ge(bn_ok, 2)
                    sc.wait_ge(pv_done, 12)
                n = BCH[k // EP][1] * L
                sc.activation(h1[k % 2][:, 0:n], bank(k % 2, n), ACT.Relu, bias=bna[:, 1, k % EP:k % EP + 1],
                              scale=bna[:, 0, k % EP:k % EP + 1]).then_inc(r1_ok, 1)

            def relu2(k):
                sc.wait_ge(l2_done, k + 1)
                if k == 4:
                    sc.wait_ge(pv_done, PAIRS)
                if k >= 8:
                    sc.wait_ge(wm_ok, k - 7)
                n = BCH[k // EP][1] * L
                sc.activation(h2[k % 8][:, 0:n], bank(2 + k % 2, n), ACT.Relu, bias=bna[:, 3, k % EP:k % EP + 1],
                              scale=bna[:, 2, k % EP:k % EP + 1]).then_inc(r2_ok, 1)

            def mixed(c):
                sc.wait_ge(l3_step, 2 * (c + 1))
                if c >= 2:
                    sc.wait_ge(yt_done, c - 1)
                n = BCH[c][1] * L
                sc.copy(y3[c % 2][:, 0:n], bank(4 + c % 2, n)).then_inc(y3_cp, 1)

            steps = EP * len(BCH)

            def experts(k):
                if k < steps:
                    relu1(k)
                if 1 <= k <= steps:
                    relu2(k - 1)
                if k in (2, 5):
                    turned(2 * G - (2 if k == 2 else 1), False)
                if k == 7:
                    sc.wait_ge(rt_exp, 1)
                    sc.activation(rt[:, 8:16], bank(6, NE, L), ACT.Exp, bias=rt[:, 0:1],
                                  accum_out=rt[:, 1:2]).then_inc(rt_exp, 1)
                if k in STEP3[1::2]:
                    mixed(STEP3[1::2].index(k))

            patches(0)
            patches(1)
            patches(2)
            sc.wait_ge(r_done, 1)
            sc.activation(rr[0:D, :], bank(6, NPOS, D), ACT.Relu).then_inc(r_cp, 1)
            embedded(0)
            patches(3)
            patches(4)
            sc.wait_ge(s4_in, 16 * N_S4)
            sc.activation(gg[:, :], lsb[:, :], ACT.Exp, scale=-1.0).then_inc(g_exp, 1)
            patches(5)
            embedded(1)
            turned(0, True)
            for q in range(4):
                keys(0, 2 * q)
                keys(0, 2 * q + 1)
                values(0, q)
                if q == 1:
                    sc.wait_ge(g_shift, 1)
                    sc.activation(g_inv, g_w, ACT.Square).then_inc(g_sq, 1)
            for p in range(PAIRS + 2):
                g, r = p // 4 + 1, p % 4
                prep = g < G
                if prep and r == 0:
                    turned(g, True)
                if prep:
                    keys(g, 2 * r)
                if p >= 2:
                    ptcopy(p - 2)
                if p >= PAIRS:
                    experts(p - PAIRS)
                if prep:
                    keys(g, 2 * r + 1)
                    values(g, r)
                if p < PAIRS:
                    expo_(p)
                if p in TURN2:
                    turned(G + TURN2.index(p), False)

            for k in range(2, STEP3[-1] + 1):
                experts(k)

            for i in (2 * G, 2 * G + 1):
                sc.wait_ge(ln_pow, variances(i))
                sc.wait_ge(ln_cen, i + 1)
                for b in range(GB * (i % G), GB * (i % G) + GB):
                    m = sc.activation(uu[:, b, :], uu[:, b, :], ACT.Copy, scale=lrs[:, 2 * B + b, :])
                m.then_inc(ln_u, 1)

            def gate_exp(s):
                sc.wait_ge(gt_sub, s + 1)
                e_ = ra[:, 0, 128 * s:128 * s + 128]
                sc.activation(e_, e_, ACT.Exp).then_inc(gt_exp, 1)

            def rows(g):
                for a in range(2):
                    sc.copy(up[D * a:D * a + D, 4 * g:4 * g + 4, :],
                            pairs_of(uu[0:D], a, g, GB)).then_inc(up_ok, 1)

            turned(2 * G, False)
            rows(0)
            turned(2 * G + 1, False)
            rows(1)
            gate_exp(0)
            for g in (2, 3):
                turned(2 * G + g, False)
            for g in (2, 3):
                rows(g)
            gate_exp(1)
            for a in range(2):
                sc.copy(hp[D * a:D * a + D, :, :], pairs_of(hh[0:D], a)).then_inc(hp_ok, 1)
            sc.wait_ge(xe_one, 2)
            for e in range(NE + 1):
                if e < NE:
                    sc.wait_ge(xe_done, e + 1)
                    sc.copy(xe[0:D, e, :], bank(e % 2, SL, D)).then_inc(xe_cp, 1)
                if e >= 1:
                    sc.wait_ge(f1_done, 2 * e - 1)
                    if e >= 3:
                        sc.wait_ge(f2_done, e - 2)
                    sc.activation(hm[(e - 1) % 2][:, 0, 0:SL], bank(2, SL), ACT.Relu).then_inc(f1_ca, 1)

        @block.vector
        def _(ve):
            steps = [0]

            def chain(ins):
                ins.then_inc(vstep, 1)
                steps[0] += 1
                ve.wait_ge(vstep, steps[0])

            def mean(i):
                g = i % G
                v = slice(GB * i, GB * i + GB)
                for b in range(GB):
                    m = ve.bn_stats(bst[:, i, b, :], hh[:, GB * g + b, :])
                chain(m)
                chain(ve.tensor_tensor(lsum[:, v, :], bst[:, i, :, 1:3], bst[:, i, :, 4:6], ALU.add))
                ve.tensor_scalar(lmean[:, v, 0], lsum[:, v, 0], 0.5, None, ALU.mult).then_inc(ln_mean, 1)

            def var(i, n=1):
                v = slice(GB * i, GB * (i + n))
                half_mean = bst[:, i:i + n, :, :].rearrange("p i b s -> p (i b) s")
                chain(ve.tensor_tensor(ldif[:, v, 0], half_mean[:, :, 1], half_mean[:, :, 4], ALU.subtract))
                chain(ve.scalar_tensor_tensor(lsqd[:, v, 0], ldif[:, v, 0], D / 4.0, ldif[:, v, 0], ALU.mult, ALU.mult))
                chain(ve.tensor_tensor(lsqd[:, v, 0], lsqd[:, v, 0], lsum[:, v, 1], ALU.add))
                ve.tensor_scalar(lvs[:, v, 0], lsqd[:, v, 0], 1.0 / D, LN_EPS, ALU.mult, ALU.add).then_inc(ln_vs, 1)

            def own_centre(i):
                ve.tensor_tensor(grp(uu, i % G), grp(hh, i % G),
                                 lmean[:, GB * i:GB * i + GB, :].broadcast_to([L, GB, D]),
                                 ALU.subtract).then_inc(ln_cen, 1)

            def scale(i):
                ve.wait_ge(ln_pow, variances(i))
                ve.wait_ge(ln_cen, i + 1)
                ve.tensor_tensor(grp(uu, i % G), grp(uu, i % G),
                                 lrs[:, GB * i:GB * i + GB, :].broadcast_to([L, GB, D]), ALU.mult).then_inc(ln_u, 1)

            def rearranged(c):
                ve.wait_ge(x_in[c], 16)
                if c >= 2:
                    ve.wait_ge(xt_done, 4 * (c - 1))
                for k in range(2):
                    ve.tensor_copy(xr[c % 2][:, k].rearrange("p g (y x) -> p g y x", y=8),
                                   ximg[:, c % NX, 8 * k:8 * k + 8, :].rearrange("p y (g x) -> p g y x", g=NG)
                                   ).then_inc(xr_ok, 1)

            def patches(c):
                for r in range(4 * c, 4 * c + 4):
                    if not by_scalar(r):
                        ve.wait_ge(xt_done, r + 1)
                        move_patches(ve, r).then_inc(xt_cv, 1)

            def tokens(g):
                ve.wait_ge(lt_done, g + 1)
                if g == 0:
                    ve.wait_ge(pos_cp, 1)
                    ve.wait_ge(cls_in, 32)
                ve.tensor_tensor(grp(hh[0:NPOS], g), bank(5 - g % 2, 512, NPOS).rearrange("p (b d) -> p b d", b=GB),
                                 posb[:, :].unsqueeze(1).broadcast_to([NPOS, GB, D]), ALU.add).then_inc(h0_ok, 1)
                ve.wait_ge(h0_ok, g + 1)

            rearranged(0)
            for c in range(3):
                rearranged(c + 1)
                patches(c)
            rearranged(4)
            patches(3)
            ve.wait_ge(pos_done, 1)
            ve.tensor_copy(posb[:, :], bank(7, D, NPOS)).then_inc(pos_cp, 1)
            tokens(0)
            tokens(1)
            rearranged(5)
            patches(4)
            mean(0)
            var(0)
            patches(5)
            mean(1)
            var(1)
            scale(0)
            ve.wait_ge(bt_done, 1)
            ve.tensor_copy(bc[:, :, :], bank(5, 128).rearrange("p (a h) -> p a h", a=4)).then_inc(bt_cp, 1)
            ve.wait_ge(bt_cp, 1)
            ve.wait_ge(s4_in, 16 * N_S4)
            u_re, u_im = bc[:, 0, :], bc[:, 1, :]
            x_re, x_im = bc[:, 2, :], bc[:, 3, :]
            pc, qc = (pri[:, 0:1], pri[:, 1:2]), (qri[:, 0:1], qri[:, 1:2])
            t0, t1 = wtmp[:, 0, :], wtmp[:, 1, :]
            chain(ve.tensor_tensor(t0, x_im, u_im, ALU.mult))
            chain(ve.tensor_tensor(t1, x_re, u_re, ALU.mult))
            chain(ve.tensor_tensor(wc[:, 0, 0], t0, t1, ALU.add))
            chain(ve.tensor_tensor(t0, x_im, u_re, ALU.mult))
            chain(ve.tensor_tensor(t1, x_re, u_im, ALU.mult))
            chain(ve.tensor_tensor(wc[:, 0, 1], t1, t0, ALU.subtract))
            for i in range(6):
                ve.wait_ge(wt_done, i + 1)
                ve.tensor_copy(wt[i // 2][:, 4 * (i % 2):4 * (i % 2) + 4, :],
                               bank(WTB[i], 4 * L, D).rearrange("p (h l) -> p h l", h=4)).then_inc(wt_cp, 1)
            chain(ve.tensor_scalar(t0, x_im, pc[1], None, ALU.mult))
            chain(ve.scalar_tensor_tensor(wc[:, 1, 0], x_re, pc[0], t0, ALU.mult, ALU.add))
            chain(ve.tensor_scalar(t0, x_im, pc[0], None, ALU.mult))
            chain(ve.scalar_tensor_tensor(wc[:, 1, 1], x_re, pc[1], t0, ALU.mult, ALU.subtract))
            chain(ve.tensor_scalar(t0, u_im, qc[1], None, ALU.mult))
            chain(ve.scalar_tensor_tensor(wc[:, 2, 0], u_re, qc[0], t0, ALU.mult, ALU.add))
            chain(ve.tensor_scalar(t0, u_re, qc[1], None, ALU.mult))
            chain(ve.scalar_tensor_tensor(wc[:, 2, 1], u_im, qc[0], t0, ALU.mult, ALU.subtract))
            for i in range(2):
                ve.wait_ge(mn_done, i + 1)
                ve.tensor_copy(mm_[0:L, 4 * i:4 * i + 4, 0:L],
                               bank(6 + i, 4 * L, L).rearrange("p (h l) -> p h l", h=4)).then_inc(mn_cp, 1)
            ve.wait_ge(mn_done, 3)
            ve.tensor_copy(nn_[0:L, :, :, :].rearrange("p a h d -> p h a d"),
                           bank(2, 512, L).rearrange("p (h a d) -> p h a d", a=2, d=D)).then_inc(mn_cp, 1)
            chain(ve.tensor_scalar(ws[:, 0:2], qri[:, :], pc[1], None, ALU.mult))
            chain(ve.tensor_scalar(ws[:, 2:4], qri[:, :], pc[0], None, ALU.mult))
            chain(ve.tensor_tensor(ws[:, 4:5], ws[:, 2:3], ws[:, 1:2], ALU.add))
            chain(ve.tensor_tensor(ws[:, 5:6], ws[:, 0:1], ws[:, 3:4], ALU.subtract))
            chain(ve.tensor_copy(wc[:, 3], ws[:, 4:6].unsqueeze(2).broadcast_to([128, 2, 32])))
            chain(ve.tensor_scalar(ws[:, 0:2], lam[:, :], RSC, None, ALU.mult))
            chain(ve.tensor_tensor(ws[:, 2:3], ws[:, 0:1], ws[:, 0:1], ALU.mult))
            chain(ve.tensor_scalar(ws[:, 3:4], ws[:, 0:1], -RSC, None, ALU.mult))
            ve.wait_ge(g_outer, 1)
            ve.tensor_scalar(g_w, g_w, ws[:, 1:2], None, ALU.add).then_inc(g_shift, 1)
            tokens(2)
            tokens(3)
            for g in range(2, 4):
                mean(g)
                var(g)
            ve.wait_ge(g_sq, 1)
            ve.tensor_scalar(g_inv, g_inv, ws[:, 2:3], None, ALU.add).then_inc(g_den, 1)
            ve.wait_ge(set_p, N_SET_P)
            for q in range(2):
                r = slice(D * q, D * q + D)
                dst_a = va[r, :, q, :].rearrange("p h c -> p c h")
                dst_b = vb[r, :, q, :].rearrange("p h (x c) -> p c x h", c=2)
                w_all = wc[r].rearrange("p x c h -> p (x c) h")
                ve.tensor_scalar(dst_a, w_all, ws[r, 3:4], None, ALU.mult).then_inc(vab_ok, 1)
                ve.tensor_scalar(dst_b[:, 0], wc[r, :, 1], -RSC, None, ALU.mult).then_inc(vab_ok, 1)
                ve.tensor_scalar(dst_b[:, 1], wc[r, :, 0], RSC, None, ALU.mult).then_inc(vab_ok, 1)
            scale(1)
            ve.memset(onebf[:, :], 1.0).then_inc(set_v, 1)
            ve.wait_ge(cl_in, 16)
            ve.tensor_scalar(tribf[:, :], tri, -1.0, None, ALU.add).then_inc(set_v, 1)
            scale(2)
            scale(3)

            ve.wait_ge(g_den, 1)

            ve.wait_ge(emb_done, 2)
            ve.memset(toep[0:D, :, D:L], 0.0).then_inc(t_zero, 1)

            def by_head(x):
                return x.rearrange("p (h j) -> p h j", h=NH)

            def rowmax(p):
                ve.wait_ge(s_done, p + 1)
                if p >= 3:
                    ve.wait_ge(p_ok, p - 2)
                ve.tensor_tensor(by_head(sx[p % 3]), by_head(bank(3 + p % 2)),
                                 cmask.unsqueeze(1).broadcast_to([128, NH, 64]), ALU.add).then_inc(msk_ok, 1)
                ve.wait_ge(msk_ok, p + 1)
                ve.tensor_reduce(mx[:, p % 3], by_head(sx[p % 3]), X, ALU.max).then_inc(mx_ok, 1)
                ve.wait_ge(mx_ok, p + 1)
                ve.tensor_tensor(by_head(sx[p % 3]), by_head(sx[p % 3]),
                                 mx[:, p % 3].unsqueeze(2).broadcast_to([128, NH, 64]), ALU.subtract).then_inc(sub_ok, 1)

            def rowsum(p):
                ve.wait_ge(exp_ok, p + 1)
                ve.tensor_reduce(mx[:, p % 3], by_head(sx[p % 3]), X, ALU.add).then_inc(sum_ok, 1)
                ve.wait_ge(sum_ok, p + 1)
                ve.reciprocal(rc[:, p % 3], mx[:, p % 3]).then_inc(rc_ok, 1)

            def attended(g):
                ve.wait_ge(pv_done, 4 * (g + 1))
                ve.wait_ge(bu_add, g + 1)
                for a in range(2):
                    h = pairs_of(hh[0:NPOS], a, g, GB)
                    ve.tensor_tensor(h, h, ps[D * a:D * a + D, 7, 0:256].rearrange("p (b d) -> p b d", d=D),
                                     ALU.add).then_inc(o_add, 1)
                ve.wait_ge(o_add, 2 * g + 2)

            def feature(g):
                ve.wait_ge(ut_cp, 2 * (G + g) + 2)
                ve.tensor_reduce(fpart[:, :, g], grp(ut[0:L], g).rearrange("p b l -> p l b"), X,
                                 ALU.add).then_inc(ft_part, 1)

            def batch_norm(part):
                if part == 0:
                    ve.wait_ge(bn_done, 1)
                    ve.tensor_copy(bn[:, :, :], bank(6, 40).rearrange("p (a e) -> p a e", a=10)).then_inc(bn_cp, 1)
                    ve.wait_ge(bn_cp, 1)
                    for i in range(2):
                        ve.tensor_scalar(bn[:, 5 * i], bn[:, 5 * i], BN_EPS, None, ALU.add).then_inc(bn_cp, 1)
                else:
                    ve.wait_ge(bn_pow, 2)
                    for i in range(2):
                        chain(ve.tensor_tensor(bna[:, 2 * i], bna[:, 2 * i], bn[:, 5 * i + 1], ALU.mult))
                        chain(ve.tensor_tensor(bna[:, 2 * i + 1], bn[:, 5 * i + 2], bn[:, 5 * i + 3], ALU.subtract))
                        chain(ve.tensor_tensor(bna[:, 2 * i + 1], bna[:, 2 * i + 1], bna[:, 2 * i], ALU.mult))
                        ve.tensor_tensor(bna[:, 2 * i + 1], bna[:, 2 * i + 1], bn[:, 5 * i + 4], ALU.add).then_inc(bn_ok, 1)

            k_ = [ks[:, i, :] for i in range(8)]
            a_ = [kt_[:, i, :] for i in range(10)]

            def tt(dst, x, y, op):
                chain(ve.tensor_tensor(dst, x, y, op))

            def at_roots(part):
                if part == 0:
                    ve.wait_ge(kk_done, 1)
                    chain(ve.tensor_copy(ks.rearrange("p c (a h) -> p c a h", a=2),
                                         bank(6, 512, L).rearrange("p (h a c) -> p c a h", a=2, c=8)))
                    ve.tensor_copy(kt_[:, 9, 0:1], ks[:, 0, 0:1]).then_inc(kk_cp, 1)
                    tt(a_[0], k_[2], k_[4], ALU.mult)
                    tt(a_[1], k_[3], k_[5], ALU.mult)
                    tt(a_[0], a_[0], a_[1], ALU.subtract)
                    tt(a_[1], k_[2], k_[5], ALU.mult)
                    tt(a_[2], k_[3], k_[4], ALU.mult)
                    tt(a_[1], a_[1], a_[2], ALU.add)
                    chain(ve.tensor_scalar(a_[2], k_[6], 1.0, None, ALU.add))
                    tt(a_[3], a_[2], a_[2], ALU.mult)
                    tt(a_[4], k_[7], k_[7], ALU.mult)
                    tt(a_[3], a_[3], a_[4], ALU.add)
                    chain(ve.reciprocal(a_[4], a_[3]))
                elif part == 1:
                    tt(a_[5], a_[0], a_[2], ALU.mult)
                    tt(a_[6], a_[1], k_[7], ALU.mult)
                    tt(a_[5], a_[5], a_[6], ALU.add)
                    tt(a_[5], a_[5], a_[4], ALU.mult)
                    tt(a_[6], a_[1], a_[2], ALU.mult)
                    tt(a_[7], a_[0], k_[7], ALU.mult)
                    tt(a_[6], a_[6], a_[7], ALU.subtract)
                    tt(a_[6], a_[6], a_[4], ALU.mult)
                else:
                    tt(a_[5], k_[0], a_[5], ALU.subtract)
                    tt(a_[6], k_[1], a_[6], ALU.subtract)
                    chain(ve.scalar_tensor_tensor(a_[8], a_[6], tau, a_[5], ALU.mult, ALU.add))
                    chain(ve.tensor_scalar(a_[7], a_[5], tau, None, ALU.mult))
                    ve.tensor_tensor(a_[9], a_[6], a_[7], ALU.subtract).then_inc(at_ok, 1)

            for p in range(PAIRS + 5):
                if p >= 6 and (p - 6) % 4 == 0:
                    attended((p - 6) // 4)
                if p < PAIRS:
                    rowmax(p)
                if 1 <= p <= PAIRS:
                    rowsum(p - 1)
                if p < 8:
                    v = slice(4 * p, 4 * p + 4)
                    ve.reciprocal(g_inv[:, v], g_inv[:, v]).then_inc(g_recip, 1)
                if p >= 6 and (p - 6) % 4 == 0:
                    mean(G + (p - 6) // 4)
                    var(G + (p - 6) // 4)
                if p == 2:
                    batch_norm(0)
                if p == 11:
                    batch_norm(1)
                if p == PAIRS:
                    at_roots(0)
                if p >= 8 and (p - 8) % 4 == 0:
                    scale(G + (p - 8) // 4)
                if p == PAIRS + 1:
                    feature(0)
                    feature(1)
                if p == PAIRS + 3:
                    at_roots(1)

            feature(2)
            at_roots(2)
            feature(3)
            ve.wait_ge(ft_part, G)
            chain(ve.tensor_reduce(feat[:, :], fpart[:, :, :], X, ALU.add))
            ve.tensor_scalar(feat[:, :], feat[:, :], 1.0 / B, None, ALU.mult).then_inc(ft_ok, 1)
            ve.wait_ge(lg_done, 1)
            ve.tensor_reduce(rt[:, 0:1], bank(6, NE, L), X, ALU.max, negate=True).then_inc(rt_exp, 1)
            ve.wait_ge(rt_exp, 2)
            chain(ve.reciprocal(rt[:, 2:3], rt[:, 1:2]))
            ve.tensor_scalar(rt[:, 16:24], rt[:, 8:16], rt[:, 2:3], None, ALU.mult).then_inc(w_ok, 1)
            ve.wait_ge(wtt_done, 1)
            ve.tensor_copy(wtt[:, :], bank(6, L, NE)).then_inc(wtt_cp, 1)
            ve.wait_ge(wb_done, 1)
            ve.tensor_copy(wb[:, :, :], bank(7, EP * L).rearrange("p (a l) -> p a l", a=EP)).then_inc(wb_cp, 1)
            ve.tensor_copy(bow[:, :], bank(7, D, L, EP * L)).then_inc(wb_cp, 1)

            def weigh(k):
                ve.wait_ge(r2_ok, k + 1)
                if k >= 4:
                    ve.wait_ge(l3_step, (k - 4) // 2 + 1)
                if k == 0:
                    ve.wait_ge(wb_cp, 2)
                nb = BCH[k // EP][1]
                ve.tensor_tensor(h2w[k % 4][:, 0:nb * L].rearrange("p (b l) -> p b l", b=nb),
                                 h2[k % 8][:, 0:nb * L].rearrange("p (b l) -> p b l", b=nb),
                                 wb[:, k % EP].unsqueeze(1).broadcast_to([128, nb, L]), ALU.mult).then_inc(wm_ok, 1)

            def fed(c):
                b0, nb = BCH[c]
                ve.wait_ge(yt_done, c + 1)
                if c == 0:
                    ve.wait_ge(bow_add, G)
                ve.tensor_tensor(hh[:, b0:b0 + nb], hh[:, b0:b0 + nb],
                                 bank(6 + c % 2, nb * D, L).rearrange("p (b d) -> p b d", b=nb),
                                 ALU.add).then_inc(y_add, 1)
                ve.wait_ge(y_add, c + 1)

            for k in range(EP * len(BCH) + 4):
                if k < EP * len(BCH):
                    weigh(k)
                if k == 2:
                    ve.wait_ge(kx_done, 1)
                    chain(ve.tensor_copy(kx[:, :], bank(6, KW, D)))
                    chain(ve.tensor_scalar(kx[:, D:D + 1], kx[:, D:D + 1], dcol[:, 0:1], None, ALU.add))
                    ve.tensor_scalar(kx[:, KW - 1:KW], kx[:, KW - 1:KW], dcol[:, 0:1], None, ALU.add).then_inc(kx_ok, 1)
                if k >= 7 and (k - 7) % EP == 0:
                    c = (k - 7) // EP
                    fed(c)
                    if c in (1, 3):
                        mean(2 * G + c - 1)
                    if c == 3:
                        var(2 * G + 2)
                if k == 17:
                    mean(2 * G + 1)
                    var(2 * G, 2)
            mean(3 * G - 1)
            var(3 * G - 1)
            scale(3 * G - 2)
            own_centre(3 * G - 1)
            scale(3 * G - 1)
            ve.wait_ge(ln_u, 3 * G)
            ve.wait_ge(t_in, 32)
            chain(ve.tensor_tensor(cls_conv, uu[D:L, :, :], toep[D:L, :, D].unsqueeze(1).broadcast_to([1, B, D]), ALU.mult))
            ve.tensor_tensor(hh[D:L, :, :], hh[D:L, :, :], cls_conv, ALU.add).then_inc(cls_add, 1)
            for q in range(4):
                ve.wait_ge(cv_done, q + 1)
                for a in range(2):
                    h = hh[0:NPOS, :, 16 * q + 8 * a:16 * q + 8 * a + 8]
                    ve.tensor_tensor(h, h, ps[D * a:D * a + D, q, 0:8 * B].rearrange("p (h b) -> p b h", h=8),
                                     ALU.add).then_inc(cv_add, 1)
            ve.wait_ge(cls_add, 1)
            ve.wait_ge(cv_add, 8)
            for g in range(2):
                mean(3 * G + g)
                var(3 * G + g)
            scale(3 * G)
            own_centre(3 * G + 1)
            mean(3 * G + 2)
            var(3 * G + 2)
            scale(3 * G + 1)
            mean(3 * G + 3)
            var(3 * G + 3)
            scale(3 * G + 2)

            HB = B // 2

            def be(x):
                return x.rearrange("p (b e) -> p b e", e=NE)

            def eb(x):
                return x.rearrange("p (e b) -> p b e", b=HB)

            def over(x):
                return x.unsqueeze(2).broadcast_to([L, HB, NE])

            best, total, share, prob, rank, place, base, row, last, kept, coef, dropped = (
                rb[:, i, :] for i in range(12))

            def choice(s):
                v = slice(HB * s, HB * s + HB)
                e_, p_, hot = (ra[:, i, 128 * s:128 * s + 128] for i in range(3))
                logit = bank(6 + s, 128, L)
                ve.wait_ge(gt_done, s + 1)
                chain(ve.tensor_reduce(best[:, v], be(logit), X, ALU.max))
                ve.tensor_tensor(be(e_), be(logit), over(best[:, v]), ALU.subtract).then_inc(gt_sub, 1)
                if s == 0:
                    scale(4 * G - 1)
                ve.wait_ge(gt_exp, s + 1)
                chain(ve.tensor_reduce(total[:, v], be(e_), X, ALU.add))
                chain(ve.reciprocal(share[:, v], total[:, v]))
                chain(ve.tensor_tensor(be(p_), be(e_), over(share[:, v]), ALU.mult))
                chain(ve.tensor_reduce(prob[:, v], be(p_), X, ALU.max))
                chain(ve.tensor_tensor(be(p_), be(p_), over(prob[:, v]), ALU.is_equal))
                chain(ve.tensor_tensor(be(p_), be(p_), be(first), ALU.mult))
                chain(ve.tensor_reduce(rank[:, v], be(p_), X, ALU.max))
                ve.tensor_tensor(eb(ohb[:, 128 * s:128 * s + 128]), be(p_), over(rank[:, v]),
                                 ALU.is_equal).then_inc(oh_ok, 1)
                ve.tensor_tensor(eb(hot), be(p_), over(rank[:, v]), ALU.is_equal)
                chain(ve.tensor_scalar(base[:, v], rank[:, v], -float(SL), float(NE * SL - 1), ALU.mult, ALU.add))

            def places(s):
                v = slice(HB * s, HB * s + HB)
                hot, run, q = (ra[:, i, 128 * s:128 * s + 128] for i in range(2, 5))
                ve.wait_ge(pre_done, 2 * s + 2)
                chain(ve.tensor_tensor_scan(run, chained, bank(3 + 2 * s, 128, L), 0.0, ALU.mult, ALU.add))
                if s:
                    before = ra[:, 3, 0:128].rearrange("p (e b) -> p e b", b=HB)[:, :, HB - 1:HB]
                    by_expert = run.rearrange("p (e b) -> p e b", b=HB)
                    chain(ve.tensor_tensor(by_expert, by_expert, before.broadcast_to([L, NE, HB]), ALU.add))
                chain(ve.tensor_tensor(q, run, bank(2 + 2 * s, 128, L), ALU.add))
                chain(ve.tensor_tensor(q, q, hot, ALU.mult))
                chain(ve.tensor_reduce(place[:, v], eb(q), X, ALU.add))
                ve.tensor_scalar(dropped[:, v], place[:, v], float(CAP) + 0.5, DROP, ALU.is_gt, ALU.mult)
                chain(ve.tensor_tensor(row[:, v], place[:, v], base[:, v], ALU.add))
                for a in range(2):
                    w = slice(HB * s + a, HB * s + HB, 2)
                    ve.tensor_tensor(ixs[D * a:D * a + D, HB // 2 * s:HB // 2 * (s + 1)],
                                     row[0:D, w], dropped[0:D, w], ALU.add).then_inc(idx_ok, 1)

            ve.wait_ge(moe_in, 16 * 7)
            for s in range(2):
                choice(s)
                places(s)
            ve.tensor_tensor(crow[:, 0, :], row, dropped, ALU.add).then_inc(idx_ok, 1)
            chain(ve.tensor_scalar(last, place, float(CAP), None, ALU.min))
            for a in range(2):
                ve.tensor_tensor(ixg[D * a:D * a + D, :], pairs_of(last[0:D], a), pairs_of(base[0:D], a),
                                 ALU.add).then_inc(ixg_ok, 1)
            ve.tensor_tensor(crow[:, 1, :], last, base, ALU.add).then_inc(ixg_ok, 1)
            chain(ve.tensor_scalar(kept, place, float(CAP) + 0.5, None, ALU.is_lt))
            ve.tensor_tensor(coef, kept, prob, ALU.mult).then_inc(co_ok, 1)
            ve.wait_ge(co_ok, 1)
            for a in range(2):
                chain(ve.tensor_copy(cp_[D * a:D * a + D, :], pairs_of(coef[0:D], a)))

            for e in range(NE + 1):
                if e < NE:
                    ve.wait_ge(f1_done, 2 * e + 2)
                    if e >= 2:
                        ve.wait_ge(f2_done, e - 1)
                    ve.tensor_scalar(hm[e % 2][:, 1, 0:SL], bank(3, SL), 0.0, None, ALU.max).then_inc(f1_cv, 1)
                if e >= 1:
                    ve.wait_ge(f2_done, e)
                    q = e - 1
                    ve.tensor_tensor(yb[0:SP, SC * q:SC * q + SC, :],
                                     bank(4 + q % 2, SC * D, SP).rearrange("p (c d) -> p c d", d=D),
                                     b2e[0:SP, q].unsqueeze(1).broadcast_to([SP, SC, D]), ALU.add).then_inc(yb_ok, 1)

            def guarded(h, y, probability, ok, r1, r2):
                chain(ve.tensor_tensor(y, y, probability, ALU.mult))
                chain(ve.tensor_scalar(ok, y, 0.0, 0.0, ALU.mult, ALU.is_equal))
                chain(ve.tensor_scalar(r1, y, 0.0, 1.0e4, ALU.is_gt, ALU.mult))
                chain(ve.tensor_scalar(r2, y, 0.0, -1.0e4, ALU.is_lt, ALU.mult))
                chain(ve.tensor_tensor(r1, r1, r2, ALU.add))
                chain(ve.copy_predicated(r1, ok, y))
                ve.tensor_tensor(h, h, r1, ALU.add).then_inc(fin_ok, 1)

            ve.wait_ge(yc_in, 16)
            ve.wait_ge(icc_in, 16)
            ve.wait_ge(hc_in, 16)
            ve.wait_ge(hp_ok, 2)
            guarded(hc, yc, cc[:, 0:1].broadcast_to([B, D]), fin[0:B, 0:D], r1_[0:B, 0:D], r2_[0:B, 0:D])
            for c, (p0, n) in enumerate(OCH):
                ve.wait_ge(yg_in[c], 16 * n)
                v = slice(p0, p0 + n)
                ve.wait_ge(fin_ok, c + 1)
                guarded(hp[:, v, :], yg[:, v, :], cp_[:, v].unsqueeze(2).broadcast_to([128, n, D]),
                        *(x[:, 0:n * D].rearrange("p (c d) -> p c d", c=n) for x in (fin, r1_, r2_)))

        @block.tensor
        def _(pe):
            def turn_patches(c):
                for k in range(2):
                    pe.wait_ge(xr_ok, 2 * c + k + 1)
                    for g in range(2):
                        r = 4 * c + 2 * k + g
                        if r >= 4:
                            pe.wait_ge(xt_ca if by_scalar(r - 4) else xt_cv, patches_moved(r - 4, by_scalar(r - 4)))
                        for x in range(4):
                            m = pe.transpose(bank(r % 4, 128, 128, 128 * x), xr[c % 2][:, k, 4 * g + x, :], ident)
                        m.then_inc(xt_done, 1)

            def embed(a, c):
                pe.wait_ge(xt_cv, patches_moved(12 * a + 4 * c + 3, False))
                pe.wait_ge(xt_ca, patches_moved(12 * a + 4 * c + 3, True))
                if a and c == 0:
                    pe.wait_ge(h0_ok, 2)
                for k in (2 * c, 2 * c + 1):
                    for q in range(2):
                        m = pe.matmul(ps[D * q:D * q + D, 4, :], wp[:, k, :],
                                      xt[:, k, GB * q:GB * q + GB].rearrange("p b y x -> p (b y x)"),
                                      start=(k == 0), stop=(k == KT - 1))
                if c == CH - 1:
                    m.then_inc(emb_done, 1)

            def turn_tokens(g):
                pe.wait_ge(et_cp, g // 2 + 1)
                if g >= 2:
                    pe.wait_ge(h0_ok, g - 1)
                q = D * (g % 2)
                for b in range(GB):
                    m = pe.transpose(bank(5 - g % 2, D, NPOS, D * b), et[q:q + D, g // 2, NPOS * b:NPOS * b + NPOS],
                                     ident[q:q + D, q:q + D])
                m.then_inc(lt_done, 1)

            def turn_norm(i):
                pe.wait_ge(ln_u, i + 1)
                for q in range(2):
                    for j in range(4):
                        m = pe.transpose(bank(turn_bank(i, q), L, D, L * j), uu[:, GB * (i % G) + 4 * q + j, :],
                                         ident[0:L, 0:L])
                    m.then_inc(ut_done, 1)

            def keys(g, h):
                if h >= 2:
                    pe.wait_ge(z_cp, NH * g + h - 1)
                else:
                    pe.wait_ge(ut_cp, 2 * g + 2)
                pe.matmul(bank(h % 2), mm_[:, h, :], grp(ut, g)[:, :, 0:D],
                          start=True, stop=True).then_inc(z_done, 1)

            def values(g, q):
                if 4 * g + q >= 1:
                    pe.wait_ge(v_cp, 4 * g + q)
                for b in range(2):
                    for a in range(2):
                        m = pe.matmul(ps[D * a:D * a + D, 2, 256 * b:256 * b + 256],
                                      ut[:, GB * g + 2 * q + b, 0:D],
                                      nn_[:, a].rearrange("p h d -> p (h d)"), start=True, stop=True)
                m.then_inc(v_done, 1)

            pe.wait_ge(cst_in, 16)
            turn_patches(0)
            turn_patches(1)
            pe.wait_ge(wp_in, 16)
            embed(0, 0)
            turn_patches(2)
            embed(0, 1)
            embed(0, 2)
            turn_patches(3)
            pe.wait_ge(tok_in, 16 * 6)
            pe.wait_ge(set_p, 2)
            pe.matmul(bank(6, NPOS, D), w1t[:, :], cxy[:, :], start=True, stop=True).then_inc(r_done, 1)
            pe.wait_ge(r_cp, 1)
            pe.matmul(bank(7, D, NPOS), rr[:, :], w2t[:, :], start=True, stop=False)
            pe.matmul(bank(7, D, NPOS), ones[:, :], bpt[:, :], start=False, stop=True).then_inc(pos_done, 1)
            for g in range(2):
                turn_tokens(g)
            turn_patches(4)
            embed(1, 0)
            pe.wait_ge(s4_in, 16 * N_S4)
            pe.wait_ge(h0_ok, 1)
            for i in range(4):
                m = pe.transpose(bank(5, 32, 128, 32 * i),
                                 bct[:, i // 2, :, :, i % 2].rearrange("p a n -> p (a n)"), ident[0:32, 0:32])
            m.then_inc(bt_done, 1)
            turn_patches(5)
            embed(1, 1)
            pe.wait_ge(qkv_in, 16 * 7)
            pe.wait_ge(pos_cp, 1)
            pe.wait_ge(xt_cv, patches_moved(23, False))
            pe.wait_ge(xt_ca, patches_moved(23, True))
            for i in range(6):
                for j in range(4):
                    h = 4 * (i % 2) + j
                    m = pe.transpose(bank(WTB[i], L, D, L * j), wqkv[i // 2][:, D * h:D * h + D], ident[0:L, 0:L])
                m.then_inc(wt_done, 1)
            embed(1, 2)
            pe.wait_ge(wt_cp, 6)
            for h in range(NH):
                m = pe.matmul(bank(6 + h // 4, L, L, L * (h % 4)), wt[1][:, h, :], wt[0][:, h, :], start=True, stop=True)
                if h % 4 == 3:
                    m.then_inc(mn_done, 1)
            for h in range(NH):
                m = pe.matmul(bank(2, D, L, D * h), wt[2][:, h, :], wu[:, h, :], start=True, stop=True)
            m.then_inc(mn_done, 1)
            turn_norm(0)
            pe.wait_ge(bt_cp, 1)
            for g in range(2, 4):
                turn_tokens(g)
            pe.wait_ge(mn_cp, 3)

            for q in range(4):
                keys(0, 2 * q)
                keys(0, 2 * q + 1)
                values(0, q)

            def scores(p):
                if p == 0:
                    pe.wait_ge(h0_ok, G)
                if p >= 2:
                    pe.wait_ge(msk_ok, p - 1)
                pe.wait_ge(z_cp, NH * (p // 4) + NH)
                for a in range(2):
                    b = 2 * p + a
                    m = pe.matmul(ps[D * a:D * a + D, 3 + p % 2, :], ut[:, b, 1:L],
                                  zz[b // GB][:, b % GB].rearrange("p h j -> p (h j)"), start=True, stop=True)
                m.then_inc(s_done, 1)

            def turn_probs(p):
                pe.wait_ge(p_ok, p + 1)
                if p >= 1:
                    pe.wait_ge(pt_cp, p)
                for j in range(4):
                    m = pe.transpose(bank(5, 128, 128, 128 * j), pp[p % 2][:, 128 * j:128 * j + 128], ident)
                m.then_inc(pt_done, 1)

            def attend(p):
                pe.wait_ge(pt_cp, p + 1)
                pe.wait_ge(v_cp, p + 1)
                if p % 4 == 0 and p:
                    pe.wait_ge(o_add, p // 2)
                for j in range(4):
                    for a in range(2):
                        m = pe.matmul(ps[D * a:D * a + D, 7, D * (p % 4):D * (p % 4) + D],
                                      pt[p % 2][:, 128 * j + D * a:128 * j + D * a + D],
                                      vv[:, 2 * p + a, j, :], start=(j == 0), stop=(j == 3))
                m.then_inc(pv_done, 1)

            def layer1(k):
                if k >= 2:
                    pe.wait_ge(r1_ok, k - 1)
                b0, nb = BCH[k // EP]
                a = k % EP
                pe.wait_ge(ut_cp, 2 * G + (b0 + nb - 1) // 4 + 1)
                pe.matmul(bank(k % 2, nb * L), w1r[:, 2 * a:2 * a + 2, :].rearrange("p e h -> p (e h)"),
                          ut[:, b0:b0 + nb].rearrange("p b l -> p (b l)"), start=True, stop=True).then_inc(l1_done, 1)

            def layer2(k):
                pe.wait_ge(r1_ok, k + 1)
                if k == 0:
                    pe.wait_ge(v_cp, 4 * G)
                    pe.wait_ge(msk_ok, PAIRS - 1)
                if k >= 2:
                    pe.wait_ge(r2_ok, k - 1)
                n = BCH[k // EP][1] * L
                pe.matmul(bank(2 + k % 2, n), w2f[:, k % EP, :], h1[k % 2][:, 0:n],
                          start=True, stop=True).then_inc(l2_done, 1)

            def layer3(k):
                pe.wait_ge(wm_ok, k + 1)
                c, a = k // EP, k % EP
                if a == 1 and c >= 2:
                    pe.wait_ge(y3_cp, c - 1)
                n = BCH[c][1] * L
                for q in range(2):
                    m = pe.matmul(ps[D * q:D * q + D, 4 + c % 2, 0:n], wof[:, a - 1 + q, :],
                                  h2w[(k - 1 + q) % 4][:, 0:n], start=(a == 1), stop=(a == EP - 1))
                m.then_inc(l3_step, 1)

            def turn_mixed(c):
                pe.wait_ge(y3_cp, c + 1)
                if c >= 2:
                    pe.wait_ge(y_add, c - 1)
                if c < 2:
                    pe.wait_ge((kx_ok, wb_cp)[c], c + 1)
                for b in range(BCH[c][1]):
                    m = pe.matmul(bank(6 + c % 2, D, L, D * b), y3[c % 2][:, L * b:L * b + L], ident2,
                                  start=True, stop=True)
                m.then_inc(yt_done, 1)

            def experts(k):
                if k < EP * len(BCH):
                    layer1(k)
                if 1 <= k <= EP * len(BCH):
                    layer2(k - 1)
                if k == 2:
                    turn_norm(2 * G - 2)
                if k == 5:
                    pe.wait_ge(o_add, 2 * G)
                    pe.wait_ge(ut_cp, 4 * G - 2)
                    turn_norm(2 * G - 1)
                if k == 7:
                    pe.wait_ge(ft_ok, 1)
                    pe.wait_ge(kk_cp, 1)
                    pe.matmul(bank(6, NE, L), feat[:, :], wra[:, :], start=True, stop=True).then_inc(lg_done, 1)
                if k == 8:
                    pe.wait_ge(w_ok, 1)
                    pe.transpose(bank(6, L, NE), rt[:, 16:24], ident[0:L, 0:L]).then_inc(wtt_done, 1)
                    pe.wait_ge(wtt_cp, 1)
                    for a in range(EP):
                        pe.matmul(bank(7, L, 128, L * a), csel[:, 128 * a:128 * a + 128], wtt[:, :], start=True, stop=True)
                    pe.matmul(bank(7, D, L, EP * L), wtt[:, :], bof[:, :], start=True, stop=True).then_inc(wb_done, 1)
                if k == 9:
                    pe.wait_ge(at_ok, 1)
                    pe.wait_ge(wtt_cp, 1)
                    pe.matmul(bank(6, KW, D), kt_[:, 8, :], cosx, start=True, stop=False)
                    pe.matmul(bank(6, KW, D), kt_[:, 9, :], sinx, start=False, stop=True).then_inc(kx_done, 1)
                if k in STEP3:
                    layer3(2 * STEP3.index(k) + 1)
                if k - 1 in STEP3[1::2]:
                    turn_mixed(STEP3[1::2].index(k - 1))

            for p in range(PAIRS + 2):
                g, r = p // 4 + 1, p % 4
                prep = g < G
                if prep and r == 0:
                    pe.wait_ge(z_cp, NH * g)
                    turn_norm(g)
                if p < PAIRS:
                    scores(p)
                if prep:
                    keys(g, 2 * r)
                if p == PAIRS:
                    pe.wait_ge(bn_ok, 2)
                    pe.wait_ge(ffn_in, 16 * N_FFN)
                    pe.wait_ge(w2_zero, 2)
                    pe.wait_ge(ut_cp, 2 * (G + 2))
                if p >= 2:
                    turn_probs(p - 2)
                if p >= PAIRS:
                    experts(p - PAIRS)
                if prep:
                    keys(g, 2 * r + 1)
                    values(g, r)
                if p == 1:
                    pe.wait_ge(bn_in, 160)
                    pe.transpose(bank(6, 40), bnr[:, :], ident[0:40, 0:40]).then_inc(bn_done, 1)
                if 11 <= p < 14:
                    if p == 11:
                        pe.wait_ge(vab_ok, 6)
                        pe.wait_ge(g_prod, 8)
                        pe.wait_ge(bn_cp, 1)
                    for h in range(11 * (p - 11), min(32, 11 * (p - 10))):
                        pe.matmul(bank(6, 16, L, 16 * h), g_inv[:, h, :], va[:, h].rearrange("p a c -> p (a c)"),
                                  start=True, stop=False)
                        m = pe.matmul(bank(6, 16, L, 16 * h), g_winv[:, h, :], vb[:, h].rearrange("p a c -> p (a c)"),
                                      start=False, stop=True)
                    if p == 13:
                        m.then_inc(kk_done, 1)
                if p >= 2:
                    attend(p - 2)
                if p in TURN2:
                    i = TURN2.index(p)
                    if i == 0:
                        pe.wait_ge(z_cp, NH * G)
                    else:
                        pe.wait_ge(ut_cp, 2 * (G + i))
                    turn_norm(G + i)

            pe.wait_ge(msk_ok, PAIRS)
            pe.wait_ge(pt_cp, PAIRS)
            for k in range(2, STEP3[-1] + 2):
                experts(k)

            def keep_warm(b, n):
                for _ in range(n):
                    pe.matmul(bank(b, 256), ident, zeros[:, :], start=True, stop=True)

            pe.wait_ge(r2_ok, EP * len(BCH))
            keep_warm(2, 12)
            pe.wait_ge(ln_u, 3 * G)
            pe.wait_ge(t_in, 32)
            pe.wait_ge(t_zero, 1)
            for q in range(4):
                for j in range(8):
                    for a in range(2):
                        h = 16 * q + 8 * a + j
                        m = pe.matmul(ps[D * a:D * a + D, q, B * j:B * j + B], toep[:, h, 0:NPOS], uu[:, :, h],
                                      start=True, stop=True)
                m.then_inc(cv_done, 1)
            pe.wait_ge(cv_add, 8)
            pe.wait_ge(y_add, len(BCH))
            pe.wait_ge(moe_in, 16 * 7)

            def turn_last(g):
                if g:
                    pe.wait_ge(ut_cp, 2 * (2 * G + g))
                pe.wait_ge(ln_u, 3 * G + g + 1)
                for q in range(2):
                    for j in range(4):
                        m = pe.transpose(bank(q, L, D, L * j), uu[:, GB * g + 4 * q + j, :], ident[0:L, 0:L])
                    m.then_inc(ut_done, 1)

            def gate(g):
                pe.wait_ge(ut_cp, 2 * (2 * G + g) + 2)
                for b in range(GB):
                    m = pe.matmul(bank(6 + g // 2, NE, L, NE * (GB * (g % 2) + b)), ut[0:L, GB * g + b, :], gwa[:, :],
                                  start=True, stop=True)
                if g % 2:
                    m.then_inc(gt_done, 1)

            def queue(s):
                pe.wait_ge(oh_ok, s + 1)
                hot = ohb[:, 128 * s:128 * s + 128]
                pe.matmul(bank(2 + 2 * s, 128, L), tribf[:, :], hot, start=True, stop=True).then_inc(pre_done, 1)
                pe.matmul(bank(3 + 2 * s, 128, L), onebf[:, :], hot, start=True, stop=True).then_inc(pre_done, 1)

            pe.wait_ge(set_v, 2)
            for g in range(G):
                turn_last(g)
                if g == G - 1:
                    queue(0)
                gate(g)
            queue(1)
            pe.wait_ge(idx_ok, 5)
            pe.wait_ge(co_ok, 1)
            pe.wait_ge(sc_near, 16)
            keep_warm(0, 6)

            def turn_slots(e):
                pe.wait_ge(xb_in[e // (NE // 4)], 16)
                if e >= 2:
                    pe.wait_ge(xe_cp, e - 1)
                for c in range(SC):
                    m = pe.transpose(bank(e % 2, SP, D, SP * c), xb[0:SP, SC * e + c, :], ident[0:SP, 0:SP])
                m.then_inc(xe_done, 1)

            def up_(e):
                pe.wait_ge(xe_cp, e + 1)
                for f in range(2):
                    if e:
                        pe.wait_ge(f1_cv if f else f1_ca, e)
                    pe.matmul(bank(2 + f, SL), w1e[:, e, 128 * f:128 * f + 128], xe[:, e, :],
                              start=True, stop=True).then_inc(f1_done, 1)

            def down(e):
                pe.wait_ge(f1_ca, e + 1)
                pe.wait_ge(f1_cv, e + 1)
                if e >= 2:
                    pe.wait_ge(yb_ok, e - 1)
                for c in range(SC):
                    for f in range(2):
                        m = pe.matmul(bank(4 + e % 2, D, SP, D * c), hm[e % 2][:, f, SP * c:SP * c + SP],
                                      w2e[:, e, f, :], start=(f == 0), stop=(f == 1))
                m.then_inc(f2_done, 1)

            for e in range(NE + 2):
                if e < NE:
                    turn_slots(e)
                if 1 <= e <= NE:
                    up_(e - 1)
                if e >= 2:
                    down(e - 2)


WTB = (0, 1, 2, 3, 6, 7)
STEP3 = (10, 11, 13, 14, 15, 17, 18, 20, 21, 22)
OCH = ((0, 5), (5, 5), (10, 4), (14, 2))
CENTRE2 = (5, 9, 15, 17)
TURN2 = (13, 14)
NX = 5
N_S4, N_FFN, N_SET_P = 11, 8, 10

_INS = ["x", "cls_tok", "L0_tok_Wp", "L0_tok_bp", "L0_tok_W1", "L0_tok_b1", "L0_tok_W2", "L0_tok_b2",
        "L0_attn_Wq", "L0_attn_bq", "L0_attn_Wk", "L0_attn_bk", "L0_attn_Wv", "L0_attn_bv", "L0_attn_Wu",
        "L0_attn_bu", "L0_ffn_Wr", "L0_ffn_br", "L0_ffn_W1", "L0_ffn_b1", "L0_ffn_g1", "L0_ffn_be1",
        "L0_ffn_m1", "L0_ffn_v1", "L0_ffn_W2", "L0_ffn_b2", "L0_ffn_g2", "L0_ffn_be2", "L0_ffn_m2",
        "L0_ffn_v2", "L0_ffn_Wo", "L0_ffn_bo", "L1_attn_p_ri", "L1_attn_q_ri", "L1_attn_lambda_ri",
        "L1_attn_B_ri", "L1_attn_Ct_ri", "L1_attn_D", "L1_attn_log_step", "L1_ffn_gate_w",
        "L1_ffn_gate_b", "L1_ffn_w1", "L1_ffn_b1", "L1_ffn_w2", "L1_ffn_b2"]


def kernel(**inputs):
    import concourse.bacc as bacc
    from concourse.bass_utils import run_bass_kernel_spmd

    nc = bacc.Bacc("TRN2", target_bir_lowering=False, num_devices=1)
    arrays, tensors = {}, {}
    for name in _INS:
        arrays[f"in_{name}"] = np.ascontiguousarray(inputs[name])
    for name, table in shape_constants().items():
        arrays[f"in_{name}"] = table
    for key, a in arrays.items():
        tensors[key[3:]] = nc.dram_tensor(key, a.shape, mybir.dt.from_np(a.dtype), kind="ExternalInput").ap()
    out = nc.dram_tensor("out", (B, L, D), F32, kind="ExternalOutput").ap()
    build(nc, tensors, out)
    r = run_bass_kernel_spmd(nc, [arrays], core_ids=[0])
    return r.results[0]["out"]
```
